# Optimizing a Trainium2 kernel written in Bass

```python
import numpy as np
import jax
import jax.numpy as jnp

def _softmax(x, axis=-1):
    return jax.nn.softmax(x, axis=axis)

def _gelu(x):
    return jax.nn.gelu(x, approximate=True)

def _silu(x):
    return jax.nn.silu(x)

def _sigmoid(x):
    return jax.nn.sigmoid(x)

def _layernorm(x, axis=-1, eps=1e-05):
    m = jnp.mean(x, axis=axis, keepdims=True)
    v = jnp.var(x, axis=axis, keepdims=True)
    return (x - m) / jnp.sqrt(v + eps)

def _scatter_add(tgt, idx, src, axis=0):
    return tgt.at[idx].add(src)

def _segment_sum(src, seg, n):
    return jax.ops.segment_sum(src, seg, n)
kernel_name = 'mk_cond_seq_d4_seqx_r4_3f8c28'

def setup_inputs(seed: int=0):
    np.random.seed(seed)
    _w = jnp.asarray

    def _rec_inputs():
        import jax
        import jax.numpy as jnp
        _rk = jax.random.key(seed)
        x = 7.22e-05 + 1 * jax.random.normal(jax.random.fold_in(_rk, 1), (64, 64, 256), jnp.float32)
        _lenS = 64 - jax.random.randint(jax.random.fold_in(_rk, 7), (64,), 0, max(1, 64 // 4) + 1, jnp.int32)
        _lenS2 = 64 - jax.random.randint(jax.random.fold_in(_rk, 8), (64,), 0, max(1, 64 // 4) + 1, jnp.int32)
        cond_1024 = 0.0061147 + 1.02565 * jax.random.normal(jax.random.fold_in(_rk, 11), (64, 256), jnp.float32)
        _validS = jnp.arange(64)[None, :] < _lenS[:, None]
        _validS2 = jnp.arange(64)[None, :] < _lenS2[:, None]
        _causal = jnp.tril(jnp.ones((64, 64), dtype=bool))
        mask_BxS_bk1 = jnp.broadcast_to(_validS[:, :], (64, 64))
        return (x, cond_1024, mask_BxS_bk1)
    x, cond_1024, mask_BxS_bk1 = _rec_inputs()

    def _L0_cond_setup():
        import jax, jax.numpy as jnp
        import numpy as np
        DIM = 256
        MLP_RATIO = 4
        EPS = 1e-06

        def rmsnorm(x, w):
            return x * jax.lax.rsqrt(jnp.mean(x * x, axis=-1, keepdims=True) + EPS) * w

        def film(x, cond, w, b):
            ss = cond @ w + b
            scale, shift = jnp.split(ss, 2, axis=-1)
            return x * (1.0 + scale[:, None, :]) + shift[:, None, :]
        key = jax.random.key(seed)
        ks = jax.random.split(key, 16)
        B, N, D = (4, 512, DIM)
        H = D * MLP_RATIO
        s = lambda fan_in: 1.0 / np.sqrt(fan_in)
        return {'x': jax.random.normal(ks[0], (B, N, D), jnp.float32), 'cond': jax.random.normal(ks[1], (B, D), jnp.float32), 'norm1_w': jnp.ones((D,), jnp.float32), 'film1_w': jax.random.normal(ks[2], (D, 2 * D), jnp.float32) * s(D), 'film1_b': jnp.zeros((2 * D,), jnp.float32), 'q_w': jax.random.normal(ks[3], (D, D), jnp.float32) * s(D), 'q_b': jnp.zeros((D,), jnp.float32), 'k_w': jax.random.normal(ks[4], (D, D), jnp.float32) * s(D), 'k_b': jnp.zeros((D,), jnp.float32), 'v_w': jax.random.normal(ks[5], (D, D), jnp.float32) * s(D), 'v_b': jnp.zeros((D,), jnp.float32), 'proj_w': jax.random.normal(ks[6], (D, D), jnp.float32) * s(D), 'proj_b': jnp.zeros((D,), jnp.float32), 'norm2_w': jnp.ones((D,), jnp.float32), 'film2_w': jax.random.normal(ks[7], (D, 2 * D), jnp.float32) * s(D), 'film2_b': jnp.zeros((2 * D,), jnp.float32), 'mlp_w1': jax.random.normal(ks[8], (D, H), jnp.float32) * s(D), 'mlp_b1': jnp.zeros((H,), jnp.float32), 'mlp_w2': jax.random.normal(ks[9], (H, D), jnp.float32) * s(H), 'mlp_b2': jnp.zeros((D,), jnp.float32)}
    _L0_cond_all = _L0_cond_setup()
    _L0_cond_in = {k: v for k, v in _L0_cond_all.items() if k in ('norm1_w', 'film1_w', 'film1_b', 'q_w', 'q_b', 'k_w', 'k_b', 'v_w', 'v_b', 'proj_w', 'proj_b', 'norm2_w', 'film2_w', 'film2_b', 'mlp_w1', 'mlp_b1', 'mlp_w2', 'mlp_b2')}
    del _L0_cond_all

    def _L1_cond_setup():
        import jax, jax.numpy as jnp
        import numpy as np
        EPS = float(np.finfo(np.float32).eps)

        def _rmsnorm(x, g):
            return x * jax.lax.rsqrt(jnp.mean(x * x, axis=-1, keepdims=True) + EPS) * g

        def _silu(x):
            return x * jax.nn.sigmoid(x)

        def _swiglu(x):
            a, gate = jnp.split(x, 2, axis=-1)
            return a * _silu(gate)

        def _rope(x):
            T, hd = (x.shape[1], x.shape[-1])
            inv_freq = 1.0 / 10000.0 ** (jnp.arange(0, hd, 2, dtype=jnp.float32) / hd)
            ang = jnp.arange(T, dtype=jnp.float32)[:, None] * inv_freq[None, :]
            cos = jnp.cos(ang)[None, :, None, :]
            sin = jnp.sin(ang)[None, :, None, :]
            x0, x1 = (x[..., 0::2], x[..., 1::2])
            o0 = x0 * cos - x1 * sin
            o1 = x1 * cos + x0 * sin
            return jnp.stack([o0, o1], axis=-1).reshape(x.shape)

        def _mha(x, w_qkv, b_qkv, w_ao, b_ao, n_head):
            B, T, C = x.shape
            hd = C // n_head
            qkv = x @ w_qkv + b_qkv
            q, k, v = jnp.split(qkv, 3, axis=-1)
            q = _rope(q.reshape(B, T, n_head, hd)).transpose(0, 2, 1, 3)
            k = _rope(k.reshape(B, T, n_head, hd)).transpose(0, 2, 1, 3)
            v = v.reshape(B, T, n_head, hd).transpose(0, 2, 1, 3)
            attn = jnp.einsum('bhqd,bhkd->bhqk', q, k) * (1.0 / np.sqrt(hd))
            attn = jax.nn.softmax(attn, axis=-1)
            out = jnp.einsum('bhqk,bhkd->bhqd', attn, v)
            out = out.transpose(0, 2, 1, 3).reshape(B, T, C)
            return out @ w_ao + b_ao

        def _ffn(x, w_fc, b_fc, w_fo, b_fo):
            return _swiglu(x @ w_fc + b_fc) @ w_fo + b_fo
        key = jax.random.key(seed)
        ks = jax.random.split(key, 10)
        B, T, D, H = (2, 512, 256, 16)
        s = 0.02
        return {'x': jax.random.normal(ks[0], (B, T, D), jnp.float32), 'time_emb': jax.random.normal(ks[1], (B, D), jnp.float32), 'g1': jnp.ones((D,), jnp.float32), 'g2': jnp.ones((D,), jnp.float32), 'w_qkv': jax.random.normal(ks[2], (D, 3 * D), jnp.float32) * s, 'b_qkv': jnp.zeros((3 * D,), jnp.float32), 'w_ao': jax.random.normal(ks[3], (D, D), jnp.float32) * s, 'b_ao': jnp.zeros((D,), jnp.float32), 'w_fc': jax.random.normal(ks[4], (D, 8 * D), jnp.float32) * s, 'b_fc': jnp.zeros((8 * D,), jnp.float32), 'w_fo': jax.random.normal(ks[5], (4 * D, D), jnp.float32) * s, 'b_fo': jnp.zeros((D,), jnp.float32), 'w_t1': jax.random.normal(ks[6], (D, 2 * D), jnp.float32) * s, 'b_t1': jnp.zeros((2 * D,), jnp.float32), 'w_t2': jax.random.normal(ks[7], (D, 4 * D), jnp.float32) * s, 'b_t2': jnp.zeros((4 * D,), jnp.float32)}
    _L1_cond_all = _L1_cond_setup()
    _L1_cond_in = {k: v for k, v in _L1_cond_all.items() if k in ('g1', 'g2', 'w_qkv', 'b_qkv', 'w_ao', 'b_ao', 'w_fc', 'b_fc', 'w_fo', 'b_fo', 'w_t1', 'b_t1', 'w_t2', 'b_t2')}
    del _L1_cond_all

    def _L2_cond_setup():
        import jax, jax.numpy as jnp
        import numpy as np
        B, T, DIM = (4, 256, 256)
        COND = 256
        HEADS, DH = (16, 64)
        INNER = HEADS * DH
        MLP = 1024
        EPS = 1e-05

        def _layernorm(x):
            mu = jnp.mean(x, axis=-1, keepdims=True)
            var = jnp.mean(jnp.square(x - mu), axis=-1, keepdims=True)
            return (x - mu) * jax.lax.rsqrt(var + EPS)

        def _modulate(x, shift, scale):
            return x * (1.0 + scale) + shift

        def _attention(x, W_qkv, W_out, b_out):
            Bq, Tq, _ = x.shape
            qkv = x @ W_qkv
            q, k, v = jnp.split(qkv, 3, axis=-1)
            q = q.reshape(Bq, Tq, HEADS, DH)
            k = k.reshape(Bq, Tq, HEADS, DH)
            v = v.reshape(Bq, Tq, HEADS, DH)
            scale = DH ** (-0.5)
            attn = jnp.einsum('bqhd,bkhd->bhqk', q, k) * scale
            attn = jax.nn.softmax(attn, axis=-1)
            out = jnp.einsum('bhqk,bkhd->bqhd', attn, v).reshape(Bq, Tq, INNER)
            return out @ W_out + b_out

        def _ff(x, W1, b1, W2, b2):
            return jax.nn.gelu(x @ W1 + b1, approximate=False) @ W2 + b2
        key = jax.random.key(seed)
        ks = jax.random.split(key, 12)
        s = 0.02
        return {'x': jax.random.normal(ks[0], (B, T, DIM), jnp.float32), 'c': jax.random.normal(ks[1], (B, 1, COND), jnp.float32), 'W_mod': jax.random.normal(ks[2], (COND, 6 * DIM), jnp.float32) * s, 'b_mod': jax.random.normal(ks[3], (6 * DIM,), jnp.float32) * s, 'W_qkv': jax.random.normal(ks[4], (DIM, 3 * INNER), jnp.float32) * s, 'W_out': jax.random.normal(ks[5], (INNER, DIM), jnp.float32) * s, 'b_out': jax.random.normal(ks[6], (DIM,), jnp.float32) * s, 'W1': jax.random.normal(ks[7], (DIM, MLP), jnp.float32) * s, 'b1': jax.random.normal(ks[8], (MLP,), jnp.float32) * s, 'W2': jax.random.normal(ks[9], (MLP, DIM), jnp.float32) * s, 'b2': jax.random.normal(ks[10], (DIM,), jnp.float32) * s}
    _L2_cond_all = _L2_cond_setup()
    _L2_cond_in = {k: v for k, v in _L2_cond_all.items() if k in ('W_mod', 'b_mod', 'W_qkv', 'W_out', 'b_out', 'W1', 'b1', 'W2', 'b2')}
    del _L2_cond_all

    def _L3_cond_setup():
        import jax, jax.numpy as jnp
        import numpy as np
        B, N, C = (8, 256, 256)
        H = 16
        HD = C // H
        MLP = 4 * C
        EPS = 1e-06

        def _layernorm(x):
            mu = jnp.mean(x, axis=-1, keepdims=True)
            var = jnp.mean((x - mu) ** 2, axis=-1, keepdims=True)
            return (x - mu) * jax.lax.rsqrt(var + EPS)

        def _modulate(x, shift, scale):
            return x * (1.0 + scale[:, None, :]) + shift[:, None, :]

        def _attention(x, padding_mask, qkv_w, qkv_b, proj_w, proj_b):
            b, n, cdim = x.shape
            qkv = x @ qkv_w.T + qkv_b
            qkv = qkv.reshape(b, n, 3, H, HD).transpose(2, 0, 3, 1, 4)
            q, k, v = (qkv[0], qkv[1], qkv[2])
            scale = HD ** (-0.5)
            attn = jnp.einsum('bhnd,bhmd->bhnm', q, k) * scale
            mask = padding_mask[:, None, :] & padding_mask[:, :, None]
            attn = jnp.where(mask[:, None, :, :], attn, -1000000000.0)
            attn = jax.nn.softmax(attn, axis=-1)
            out = jnp.einsum('bhnm,bhmd->bhnd', attn, v)
            out = out.transpose(0, 2, 1, 3).reshape(b, n, cdim)
            return out @ proj_w.T + proj_b
        key = jax.random.key(seed)
        ks = jax.random.split(key, 12)
        x = jax.random.normal(ks[0], (B, N, C), dtype=jnp.float32)
        c = jax.random.normal(ks[1], (B, C), dtype=jnp.float32)
        lengths = jax.random.randint(ks[2], (B,), N // 2, N + 1)
        padding_mask = jnp.arange(N)[None, :] < lengths[:, None]
        s = 0.02
        qkv_w = jax.random.normal(ks[3], (3 * C, C), dtype=jnp.float32) * s
        qkv_b = jnp.zeros((3 * C,), dtype=jnp.float32)
        proj_w = jax.random.normal(ks[4], (C, C), dtype=jnp.float32) * s
        proj_b = jnp.zeros((C,), dtype=jnp.float32)
        fc1_w = jax.random.normal(ks[5], (MLP, C), dtype=jnp.float32) * s
        fc1_b = jnp.zeros((MLP,), dtype=jnp.float32)
        fc2_w = jax.random.normal(ks[6], (C, MLP), dtype=jnp.float32) * s
        fc2_b = jnp.zeros((C,), dtype=jnp.float32)
        ada_w = jax.random.normal(ks[7], (6 * C, C), dtype=jnp.float32) * s
        ada_b = jnp.zeros((6 * C,), dtype=jnp.float32)
        return {'x': x, 'c': c, 'padding_mask': padding_mask, 'qkv_w': qkv_w, 'qkv_b': qkv_b, 'proj_w': proj_w, 'proj_b': proj_b, 'fc1_w': fc1_w, 'fc1_b': fc1_b, 'fc2_w': fc2_w, 'fc2_b': fc2_b, 'ada_w': ada_w, 'ada_b': ada_b}
    _L3_cond_all = _L3_cond_setup()
    _L3_cond_in = {k: v for k, v in _L3_cond_all.items() if k in ('qkv_w', 'qkv_b', 'proj_w', 'proj_b', 'fc1_w', 'fc1_b', 'fc2_w', 'fc2_b', 'ada_w', 'ada_b')}
    del _L3_cond_all
    return {'x': x, 'cond_1024': cond_1024, 'mask_BxS_bk1': mask_BxS_bk1, 'L0_cond_norm1_w': _L0_cond_in['norm1_w'], 'L0_cond_film1_w': _L0_cond_in['film1_w'], 'L0_cond_film1_b': _L0_cond_in['film1_b'], 'L0_cond_q_w': _L0_cond_in['q_w'], 'L0_cond_q_b': _L0_cond_in['q_b'], 'L0_cond_k_w': _L0_cond_in['k_w'], 'L0_cond_k_b': _L0_cond_in['k_b'], 'L0_cond_v_w': _L0_cond_in['v_w'], 'L0_cond_v_b': _L0_cond_in['v_b'], 'L0_cond_proj_w': _L0_cond_in['proj_w'], 'L0_cond_proj_b': _L0_cond_in['proj_b'], 'L0_cond_norm2_w': _L0_cond_in['norm2_w'], 'L0_cond_film2_w': _L0_cond_in['film2_w'], 'L0_cond_film2_b': _L0_cond_in['film2_b'], 'L0_cond_mlp_w1': _L0_cond_in['mlp_w1'], 'L0_cond_mlp_b1': _L0_cond_in['mlp_b1'], 'L0_cond_mlp_w2': _L0_cond_in['mlp_w2'], 'L0_cond_mlp_b2': _L0_cond_in['mlp_b2'], 'L1_cond_g1': _L1_cond_in['g1'], 'L1_cond_g2': _L1_cond_in['g2'], 'L1_cond_w_qkv': _L1_cond_in['w_qkv'], 'L1_cond_b_qkv': _L1_cond_in['b_qkv'], 'L1_cond_w_ao': _L1_cond_in['w_ao'], 'L1_cond_b_ao': _L1_cond_in['b_ao'], 'L1_cond_w_fc': _L1_cond_in['w_fc'], 'L1_cond_b_fc': _L1_cond_in['b_fc'], 'L1_cond_w_fo': _L1_cond_in['w_fo'], 'L1_cond_b_fo': _L1_cond_in['b_fo'], 'L1_cond_w_t1': _L1_cond_in['w_t1'], 'L1_cond_b_t1': _L1_cond_in['b_t1'], 'L1_cond_w_t2': _L1_cond_in['w_t2'], 'L1_cond_b_t2': _L1_cond_in['b_t2'], 'L2_cond_W_mod': _L2_cond_in['W_mod'], 'L2_cond_b_mod': _L2_cond_in['b_mod'], 'L2_cond_W_qkv': _L2_cond_in['W_qkv'], 'L2_cond_W_out': _L2_cond_in['W_out'], 'L2_cond_b_out': _L2_cond_in['b_out'], 'L2_cond_W1': _L2_cond_in['W1'], 'L2_cond_b1': _L2_cond_in['b1'], 'L2_cond_W2': _L2_cond_in['W2'], 'L2_cond_b2': _L2_cond_in['b2'], 'L3_cond_qkv_w': _L3_cond_in['qkv_w'], 'L3_cond_qkv_b': _L3_cond_in['qkv_b'], 'L3_cond_proj_w': _L3_cond_in['proj_w'], 'L3_cond_proj_b': _L3_cond_in['proj_b'], 'L3_cond_fc1_w': _L3_cond_in['fc1_w'], 'L3_cond_fc1_b': _L3_cond_in['fc1_b'], 'L3_cond_fc2_w': _L3_cond_in['fc2_w'], 'L3_cond_fc2_b': _L3_cond_in['fc2_b'], 'L3_cond_ada_w': _L3_cond_in['ada_w'], 'L3_cond_ada_b': _L3_cond_in['ada_b']}

def reference(x, cond_1024, mask_BxS_bk1, L0_cond_norm1_w, L0_cond_film1_w, L0_cond_film1_b, L0_cond_q_w, L0_cond_q_b, L0_cond_k_w, L0_cond_k_b, L0_cond_v_w, L0_cond_v_b, L0_cond_proj_w, L0_cond_proj_b, L0_cond_norm2_w, L0_cond_film2_w, L0_cond_film2_b, L0_cond_mlp_w1, L0_cond_mlp_b1, L0_cond_mlp_w2, L0_cond_mlp_b2, L1_cond_g1, L1_cond_g2, L1_cond_w_qkv, L1_cond_b_qkv, L1_cond_w_ao, L1_cond_b_ao, L1_cond_w_fc, L1_cond_b_fc, L1_cond_w_fo, L1_cond_b_fo, L1_cond_w_t1, L1_cond_b_t1, L1_cond_w_t2, L1_cond_b_t2, L2_cond_W_mod, L2_cond_b_mod, L2_cond_W_qkv, L2_cond_W_out, L2_cond_b_out, L2_cond_W1, L2_cond_b1, L2_cond_W2, L2_cond_b2, L3_cond_qkv_w, L3_cond_qkv_b, L3_cond_proj_w, L3_cond_proj_b, L3_cond_fc1_w, L3_cond_fc1_b, L3_cond_fc2_w, L3_cond_fc2_b, L3_cond_ada_w, L3_cond_ada_b):
    import jax
    import jax.numpy as jnp

    def _L0_cond_ref(x, cond, norm1_w, film1_w, film1_b, q_w, q_b, k_w, k_b, v_w, v_b, proj_w, proj_b, norm2_w, film2_w, film2_b, mlp_w1, mlp_b1, mlp_w2, mlp_b2):
        import jax, jax.numpy as jnp
        import numpy as np
        DIM = 256
        MLP_RATIO = 4
        EPS = 1e-06

        def rmsnorm(x, w):
            return x * jax.lax.rsqrt(jnp.mean(x * x, axis=-1, keepdims=True) + EPS) * w

        def film(x, cond, w, b):
            ss = cond @ w + b
            scale, shift = jnp.split(ss, 2, axis=-1)
            return x * (1.0 + scale[:, None, :]) + shift[:, None, :]
        B, N, D = x.shape
        x_in = x
        h = film(rmsnorm(x, norm1_w), cond, film1_w, film1_b)
        Q = h @ q_w + q_b
        K = h @ k_w + k_b
        V = h @ v_w + v_b
        scores = jnp.einsum('bnd,bmd->bnm', Q, K) * D ** (-0.5)
        attn = jax.nn.softmax(scores, axis=-1)
        out = jnp.einsum('bnm,bmd->bnd', attn, V)
        x = x_in + (out @ proj_w + proj_b)
        x_in = x
        h = film(rmsnorm(x, norm2_w), cond, film2_w, film2_b)
        h = jax.nn.gelu(h @ mlp_w1 + mlp_b1, approximate=False) @ mlp_w2 + mlp_b2
        return x_in + h

    def _L1_cond_ref(x, time_emb, g1, g2, w_qkv, b_qkv, w_ao, b_ao, w_fc, b_fc, w_fo, b_fo, w_t1, b_t1, w_t2, b_t2):
        import jax, jax.numpy as jnp
        import numpy as np
        EPS = float(np.finfo(np.float32).eps)

        def _rmsnorm(x, g):
            return x * jax.lax.rsqrt(jnp.mean(x * x, axis=-1, keepdims=True) + EPS) * g

        def _silu(x):
            return x * jax.nn.sigmoid(x)

        def _swiglu(x):
            a, gate = jnp.split(x, 2, axis=-1)
            return a * _silu(gate)

        def _rope(x):
            T, hd = (x.shape[1], x.shape[-1])
            inv_freq = 1.0 / 10000.0 ** (jnp.arange(0, hd, 2, dtype=jnp.float32) / hd)
            ang = jnp.arange(T, dtype=jnp.float32)[:, None] * inv_freq[None, :]
            cos = jnp.cos(ang)[None, :, None, :]
            sin = jnp.sin(ang)[None, :, None, :]
            x0, x1 = (x[..., 0::2], x[..., 1::2])
            o0 = x0 * cos - x1 * sin
            o1 = x1 * cos + x0 * sin
            return jnp.stack([o0, o1], axis=-1).reshape(x.shape)

        def _mha(x, w_qkv, b_qkv, w_ao, b_ao, n_head):
            B, T, C = x.shape
            hd = C // n_head
            qkv = x @ w_qkv + b_qkv
            q, k, v = jnp.split(qkv, 3, axis=-1)
            q = _rope(q.reshape(B, T, n_head, hd)).transpose(0, 2, 1, 3)
            k = _rope(k.reshape(B, T, n_head, hd)).transpose(0, 2, 1, 3)
            v = v.reshape(B, T, n_head, hd).transpose(0, 2, 1, 3)
            attn = jnp.einsum('bhqd,bhkd->bhqk', q, k) * (1.0 / np.sqrt(hd))
            attn = jax.nn.softmax(attn, axis=-1)
            out = jnp.einsum('bhqk,bhkd->bhqd', attn, v)
            out = out.transpose(0, 2, 1, 3).reshape(B, T, C)
            return out @ w_ao + b_ao

        def _ffn(x, w_fc, b_fc, w_fo, b_fo):
            return _swiglu(x @ w_fc + b_fc) @ w_fo + b_fo
        n_head = 16
        tp = _swiglu(time_emb @ w_t1 + b_t1) @ w_t2 + b_t2
        shift1, scale1, shift2, scale2 = jnp.split(tp, 4, axis=-1)
        h = _rmsnorm(x, g1) * (1.0 + scale1[:, None, :]) + shift1[:, None, :]
        x = x + _mha(h, w_qkv, b_qkv, w_ao, b_ao, n_head)
        h = _rmsnorm(x, g2) * (1.0 + scale2[:, None, :]) + shift2[:, None, :]
        x = x + _ffn(h, w_fc, b_fc, w_fo, b_fo)
        return x

    def _L2_cond_ref(x, c, W_mod, b_mod, W_qkv, W_out, b_out, W1, b1, W2, b2):
        import jax, jax.numpy as jnp
        import numpy as np
        B, T, DIM = (4, 256, 256)
        COND = 256
        HEADS, DH = (16, 64)
        INNER = HEADS * DH
        MLP = 1024
        EPS = 1e-05

        def _layernorm(x):
            mu = jnp.mean(x, axis=-1, keepdims=True)
            var = jnp.mean(jnp.square(x - mu), axis=-1, keepdims=True)
            return (x - mu) * jax.lax.rsqrt(var + EPS)

        def _modulate(x, shift, scale):
            return x * (1.0 + scale) + shift

        def _attention(x, W_qkv, W_out, b_out):
            Bq, Tq, _ = x.shape
            qkv = x @ W_qkv
            q, k, v = jnp.split(qkv, 3, axis=-1)
            q = q.reshape(Bq, Tq, HEADS, DH)
            k = k.reshape(Bq, Tq, HEADS, DH)
            v = v.reshape(Bq, Tq, HEADS, DH)
            scale = DH ** (-0.5)
            attn = jnp.einsum('bqhd,bkhd->bhqk', q, k) * scale
            attn = jax.nn.softmax(attn, axis=-1)
            out = jnp.einsum('bhqk,bkhd->bqhd', attn, v).reshape(Bq, Tq, INNER)
            return out @ W_out + b_out

        def _ff(x, W1, b1, W2, b2):
            return jax.nn.gelu(x @ W1 + b1, approximate=False) @ W2 + b2
        mod = jax.nn.silu(c) @ W_mod + b_mod
        sh_msa, sc_msa, g_msa, sh_mlp, sc_mlp, g_mlp = jnp.split(mod, 6, axis=-1)
        x = x + g_msa * _attention(_modulate(_layernorm(x), sh_msa, sc_msa), W_qkv, W_out, b_out)
        x = x + g_mlp * _ff(_modulate(_layernorm(x), sh_mlp, sc_mlp), W1, b1, W2, b2)
        return x

    def _L3_cond_ref(x, c, padding_mask, qkv_w, qkv_b, proj_w, proj_b, fc1_w, fc1_b, fc2_w, fc2_b, ada_w, ada_b):
        import jax, jax.numpy as jnp
        import numpy as np
        B, N, C = (8, 256, 256)
        H = 16
        HD = C // H
        MLP = 4 * C
        EPS = 1e-06

        def _layernorm(x):
            mu = jnp.mean(x, axis=-1, keepdims=True)
            var = jnp.mean((x - mu) ** 2, axis=-1, keepdims=True)
            return (x - mu) * jax.lax.rsqrt(var + EPS)

        def _modulate(x, shift, scale):
            return x * (1.0 + scale[:, None, :]) + shift[:, None, :]

        def _attention(x, padding_mask, qkv_w, qkv_b, proj_w, proj_b):
            b, n, cdim = x.shape
            qkv = x @ qkv_w.T + qkv_b
            qkv = qkv.reshape(b, n, 3, H, HD).transpose(2, 0, 3, 1, 4)
            q, k, v = (qkv[0], qkv[1], qkv[2])
            scale = HD ** (-0.5)
            attn = jnp.einsum('bhnd,bhmd->bhnm', q, k) * scale
            mask = padding_mask[:, None, :] & padding_mask[:, :, None]
            attn = jnp.where(mask[:, None, :, :], attn, -1000000000.0)
            attn = jax.nn.softmax(attn, axis=-1)
            out = jnp.einsum('bhnm,bhmd->bhnd', attn, v)
            out = out.transpose(0, 2, 1, 3).reshape(b, n, cdim)
            return out @ proj_w.T + proj_b
        mod = jax.nn.silu(c) @ ada_w.T + ada_b
        shift_msa, scale_msa, gate_msa, shift_mlp, scale_mlp, gate_mlp = jnp.split(mod, 6, axis=1)
        h = _modulate(_layernorm(x), shift_msa, scale_msa)
        x = x + gate_msa[:, None, :] * _attention(h, padding_mask, qkv_w, qkv_b, proj_w, proj_b)
        h = _modulate(_layernorm(x), shift_mlp, scale_mlp)
        h = jax.nn.gelu(h @ fc1_w.T + fc1_b, approximate=True) @ fc2_w.T + fc2_b
        x = x + gate_mlp[:, None, :] * h
        return x
    x = _L0_cond_ref(x, cond_1024, L0_cond_norm1_w, L0_cond_film1_w, L0_cond_film1_b, L0_cond_q_w, L0_cond_q_b, L0_cond_k_w, L0_cond_k_b, L0_cond_v_w, L0_cond_v_b, L0_cond_proj_w, L0_cond_proj_b, L0_cond_norm2_w, L0_cond_film2_w, L0_cond_film2_b, L0_cond_mlp_w1, L0_cond_mlp_b1, L0_cond_mlp_w2, L0_cond_mlp_b2)
    x = _L1_cond_ref(x, cond_1024, L1_cond_g1, L1_cond_g2, L1_cond_w_qkv, L1_cond_b_qkv, L1_cond_w_ao, L1_cond_b_ao, L1_cond_w_fc, L1_cond_b_fc, L1_cond_w_fo, L1_cond_b_fo, L1_cond_w_t1, L1_cond_b_t1, L1_cond_w_t2, L1_cond_b_t2)
    x = _L2_cond_ref(x, cond_1024[:, None, :], L2_cond_W_mod, L2_cond_b_mod, L2_cond_W_qkv, L2_cond_W_out, L2_cond_b_out, L2_cond_W1, L2_cond_b1, L2_cond_W2, L2_cond_b2)
    x = _L3_cond_ref(x, cond_1024, mask_BxS_bk1, L3_cond_qkv_w, L3_cond_qkv_b, L3_cond_proj_w, L3_cond_proj_b, L3_cond_fc1_w, L3_cond_fc1_b, L3_cond_fc2_w, L3_cond_fc2_b, L3_cond_ada_w, L3_cond_ada_b)
    return x

_drawn_inputs = setup_inputs


def setup_inputs(seed=0):
    import zlib

    import numpy as np

    out = dict(_drawn_inputs(seed))
    spreads = {'L0_cond_norm1_w': (1.0, 0.2),
     'L0_cond_film1_b': (0.0, 0.1),
     'L0_cond_q_b': (0.0, 0.1),
     'L0_cond_k_b': (0.0, 0.8),
     'L0_cond_v_b': (0.0, 0.1),
     'L0_cond_proj_b': (0.0, 0.1),
     'L0_cond_norm2_w': (1.0, 0.2),
     'L0_cond_film2_b': (0.0, 0.1),
     'L0_cond_mlp_b1': (0.0, 0.1),
     'L0_cond_mlp_b2': (0.0, 0.1),
     'L1_cond_g1': (1.0, 0.6),
     'L1_cond_g2': (1.0, 0.6),
     'L1_cond_b_qkv': (0.0, 0.491),
     'L1_cond_b_ao': (0.0, 0.1),
     'L1_cond_b_fc': (0.0, 0.8),
     'L1_cond_b_fo': (0.0, 0.1),
     'L1_cond_b_t1': (0.0, 0.8),
     'L1_cond_b_t2': (0.0, 0.8),
     'L3_cond_qkv_b': (0.0, 0.8),
     'L3_cond_proj_b': (0.0, 0.74),
     'L3_cond_fc1_b': (0.0, 0.8),
     'L3_cond_fc2_b': (0.0, 0.735),
     'L3_cond_ada_b': (0.0, 0.75)}
    factors = {'L1_cond_w_fc': 2.846,
     'L1_cond_w_fo': 2.812,
     'L1_cond_w_t1': 8.0,
     'L1_cond_w_t2': 8.0,
     'L2_cond_W_mod': 3.047,
     'L2_cond_b_mod': 8.0,
     'L2_cond_W_qkv': 3.617,
     'L2_cond_W_out': 3.655,
     'L2_cond_b_out': 8.0,
     'L2_cond_W1': 5.348,
     'L2_cond_b1': 8.0,
     'L2_cond_W2': 5.286,
     'L2_cond_b2': 8.0,
     'L3_cond_qkv_w': 6.822,
     'L3_cond_proj_w': 6.205,
     'L3_cond_fc1_w': 4.676,
     'L3_cond_fc2_w': 4.38,
     'L3_cond_ada_w': 2.85}
    for name, (base, spread) in spreads.items():
        noise = np.random.default_rng([zlib.crc32(name.encode()), seed]).standard_normal(out[name].shape)
        drawn = base * np.exp(spread * noise) if base else spread * noise
        out[name] = jnp.asarray(drawn.astype(out[name].dtype))
    for name, factor in factors.items():
        out[name] = (out[name] * factor).astype(out[name].dtype)
    return out
```

```python
from contextlib import ExitStack

import numpy as np

import concourse.bass as bass
from concourse import mybir

ALU = mybir.AluOpType
ACT = mybir.ActivationFunctionType
AX = mybir.AxisListType
F32 = mybir.dt.float32
F32R = mybir.dt.float32r
U8 = mybir.dt.uint8

P = 128
S = 64
D = 256
DC = D // P
BLK = 512
SEQ = BLK // S
TILES = BLK // P
PAIRS = 8
HID = 8
VW = 33
MASKED = 4e9
CREDIT = 2

PHASES = [(kind, layer) for layer in range(4) for kind in ("attn", "mlp")]
UP = {("attn", 0): DC * 768, ("mlp", 0): DC * 1024, ("attn", 1): DC * 1280, ("mlp", 1): DC * 2048,
      ("attn", 2): DC * 3072, ("mlp", 2): DC * 1024, ("attn", 3): DC * 768, ("mlp", 3): DC * 1024}
DOWN = {(kind, layer): (8 if kind == "mlp" or layer == 2 else 2) * D for kind, layer in PHASES}
EPS = (1e-6, float(np.finfo(np.float32).eps), 1e-5, 1e-6)
SCORE_SCALE = (1 / 16, 1 / 4, 1 / 8, 1 / 4)

MOD = {("attn", 0): (0, 2, None), ("mlp", 0): (4, 6, None), ("attn", 1): (10, 8, None), ("mlp", 1): (14, 12, None),
       ("attn", 2): (18, 16, 20), ("mlp", 2): (24, 22, 26), ("attn", 3): (30, 28, 32), ("mlp", 3): (36, 34, 38)}
MODS = 40
MOD_COLS = {"film": DC * 1024, "t1": DC * 512, "mod2": DC * 1536, "mod3": DC * 1536, "t2": DC * 1024}

VEC = {}
for _name, _n in (("mod_b", MODS), ("t1_b", 4), ("norm", 8),
                  ("q0", 2), ("k0", 2), ("v0", 2), ("o0", 2), ("u0", 8), ("d0", 2),
                  ("q1", 2), ("k1", 2), ("qs1", 2), ("ks1", 2), ("v1", 2), ("o1", 2), ("u1", 16), ("d1", 2),
                  ("o2", 2), ("u2", 8), ("d2", 2),
                  ("q3", 2), ("k3", 2), ("v3", 2), ("o3", 2), ("u3", 8), ("d3", 2),
                  ("even", 1), ("odd", 1), ("cos", S), ("sin", S), ("ident", P)):
    VEC[_name] = (sum(n for _, n in VEC.values()), _n)
VECS = sum(n for _, n in VEC.values())


def order_of(kind, layer):
    own = lambda s, k=0: (s, k, False)
    nxt = lambda s, k=0: (s, k, True)
    norm = [nxt("stats"), nxt("norm"), nxt("turn")]
    if kind == "mlp":
        ahead = norm + [nxt("up", 0), nxt("up", 1)]
        body = []
        for k in range(2, HID):
            body += [own("up", k), own("down", k - 2)]
            if k == 3:
                body += [nxt("stats"), nxt("norm")]
        body += [nxt("turn"), own("down", 6), nxt("up", 0), own("down", 7), nxt("up", 1), own("back")]
        return ahead, body
    if layer == 0:
        ahead = norm + [nxt("q", 0), nxt("q", 1), nxt("k", 0), nxt("k", 1), nxt("v", 0), nxt("v", 1)]
        body = [own("scores"), nxt("stats"), nxt("norm"), own("even_out"), nxt("turn"), own("probs_t"), nxt("q", 0),
                own("pv"), nxt("q", 1), nxt("k", 0), own("proj"), nxt("k", 1), nxt("v", 0), nxt("v", 1), own("back")]
        return ahead, body
    if layer in (1, 3):
        ahead = norm + [nxt("q", 0), nxt("k", 0), nxt("q", 1), nxt("k", 1), nxt("v", 0), nxt("v", 1)]
        body = []
        for p in range(PAIRS):
            body += [own("scores", p)]
            body += [own("probs_t", p - 1)] if p >= 1 else []
            body += [own("pv", p - 2)] if p >= 2 else []
            body += {1: [nxt("stats")], 2: [nxt("norm")], 3: [nxt("turn")], 5: [nxt("q", 0)], 6: [nxt("k", 0)],
                     7: [nxt("q", 1)]}.get(p, [])
        body += [own("probs_t", 7), own("pv", 6), nxt("k", 1), own("pv", 7), nxt("v", 0), own("merge"), nxt("v", 1),
                 own("proj"), own("back")]
        return ahead, body
    ahead = norm + [nxt("v", j) for j in range(8)] + [nxt("q", 0), nxt("k", 0)]
    body = []
    for p in range(PAIRS):
        body += [own("scores", p)]
        body += [own("even_out", p - 1)] if p >= 1 else []
        body += [own("pv", p - 2), own("pv2", p - 2)] if p >= 2 else []
        body += [own("q", p + 1), own("k", p + 1)] if p < 7 else []
        body += [own("probs_t", p - 1)] if p >= 1 else []
        body += [own("proj", p - 3)] if p >= 3 else []
        body += {2: [nxt("stats")], 4: [nxt("norm")], 6: [nxt("turn")]}.get(p, [])
    body += [own("even_out", 7), own("pv", 6), own("proj", 5), own("pv2", 6), own("probs_t", 7), own("proj", 6),
             own("pv", 7), nxt("v", 0), own("pv2", 7)]
    body += [nxt("v", j) for j in range(1, 8)] + [own("proj", 7), nxt("q", 0), nxt("k", 0), own("back")]
    return ahead, body


def counts_of(kind, layer):
    c = dict(stats_raw=1, stats=1, mean_sq=1 if layer < 2 else 0, rstd_in=1, rstd=1, normed=1, eps_added=1, modded=2,
             h_hi=2, h=2, out_rows=2, x_done=1)
    if kind == "mlp":
        n = HID * (2 if layer == 1 else 1)
        c.update({"a_full0": 1, "a_full1": 1, "a_free0": 1, "a_free1": 1,
                  "s_full0": n // 2, "s_full1": n // 2, "s_free0": n // 2, "s_free1": n // 2,
                  "hid32": HID, "hid_hi": HID, "hid": HID, "down": HID, "gate_in": HID if layer == 1 else 0,
                  "back": 1})
        return c
    fills = {0: 8, 1: 12, 2: 26, 3: 8}[layer] // 2
    c.update({"a_full0": fills, "a_full1": fills, "a_free0": fills, "a_free1": fills})
    n = 1 if layer == 0 else PAIRS
    c.update({"s_full0": n - n // 2, "s_full1": n // 2, "s_free0": n - n // 2, "s_free1": n // 2,
              "row_max": n, "shifted": n * (2 if layer == 0 else 1), "probs": n, "t_full": n, "probs_t": n})
    if layer in (0, 2):
        c.update(row_sum=n, row_inv=n, even=n)
    if layer == 0:
        c.update(q=2, k=2, v=2, w_full=3, w_free=1, att_hi=2, att=2)
    if layer in (1, 3):
        c.update(o_full=n, o_inv=n, o_free=n, q=2 * 2, k=2, v=2 * 2, q32=2, w_full=3, w_free=1, att_hi=2, att=2)
    if layer == 1:
        c.update(rot_a=4, rot_b=4)
    if layer == 3:
        c.update(masked=n, mask_k=1, mask_raw=1, mask=1)
    if layer == 2:
        c.update(q=2 * n, k=n, v=8, pv1=n, o_full=n, o_free=n, att_hi=n, att=n, proj=n, w_full=1)
    return c


NAMES = sorted({name for ph in PHASES for name in counts_of(*ph)})


def build(nc, x_in, cond_in, mask_k_in, mask_q_in, vec_in, modw_in, weights_in, out, phases=len(PHASES)):
    batch = cond_in.shape[2]
    blocks = batch // SEQ
    tiles = blocks * TILES

    before = {name: [0] for name in NAMES}
    for ph in range(len(PHASES)):
        for name in NAMES:
            before[name].append(before[name][-1] + blocks * counts_of(*PHASES[ph]).get(name, 0))

    def n_at(name, ph, b, k):
        return b * counts_of(*PHASES[ph]).get(name, 0) + (CREDIT + before[name][ph] + k)

    with ExitStack() as ctx:
        sem = {name: ctx.enter_context(nc.semaphore(name)) for name in NAMES}
        x_loaded = ctx.enter_context(nc.semaphore("x_loaded"))
        vec_loaded = ctx.enter_context(nc.semaphore("vec_loaded"))
        modw_loaded = [ctx.enter_context(nc.semaphore(f"modw_loaded{i}")) for i in range(5)]
        mask_loaded = ctx.enter_context(nc.semaphore("mask_loaded"))
        w_staged = ctx.enter_context(nc.semaphore("w_staged"))
        w_hi_done = ctx.enter_context(nc.semaphore("w_hi_done"))
        w_ready = ctx.enter_context(nc.semaphore("w_ready"))
        consts_ready = ctx.enter_context(nc.semaphore("consts_ready"))
        zeroed = ctx.enter_context(nc.semaphore("zeroed"))
        mod_mm = ctx.enter_context(nc.semaphore("mod_mm"))
        mod_act = ctx.enter_context(nc.semaphore("mod_act"))
        mod_dve = ctx.enter_context(nc.semaphore("mod_dve"))
        waits_passed = ctx.enter_context(nc.semaphore("waits_passed"))
        stored = ctx.enter_context(nc.semaphore("stored"))

        at = [nc.sbuf_base + (-nc.sbuf_base) % 32]

        def place(name, shape, dt, where=None):
            size = int(np.prod(shape[1:])) * (1 if dt == U8 else 4)
            size += -size % 32
            offset = at[0] if where is None else where
            if where is None:
                at[0] += size
            assert offset + size <= nc.sbuf_usable_end, (name, offset, size)
            return nc.alloc_sbuf_tensor_at(name, shape, dt, offset=offset)

        xres = place("xres", [P, tiles, D], F32)
        mod = place("mod", [P, MODS, batch], F32)
        vec = place("vec", [P, VECS], F32)
        xn = place("xn", [P, TILES, D], F32)
        hm = place("hm", [P, DC, BLK], F32)
        h_hi = place("h_hi", [P, DC, BLK], F32R)
        h_lo = place("h_lo", [P, DC, BLK], F32R)
        y = place("y", [P, DC, BLK], F32)
        stage = place("stage", [P, 1024], F32)
        st = place("st", [P, TILES, 6], F32)
        mv = place("mv", [P, TILES, 2], F32)
        ms = place("ms", [P, TILES], F32)
        rstd = place("rstd", [P, TILES], F32)
        eps_t = place("eps_t", [P, 4, TILES], F32)
        half_t = place("half_t", [P, TILES], F32)
        mx = place("mx", [P, 2, SEQ], F32)
        sm = place("sm", [P, 2, SEQ], F32)
        ri = place("ri", [P, 2, SEQ], F32)
        mask_q = place("mask_q", [P, batch], F32)
        mask_q8 = place("mask_q8", [P, batch], U8)
        work = at[0]
        pb = place("pb", [P, 2, BLK], F32)
        pt = place("pt", [P, 2, BLK], F32)
        at_hi = place("at_hi", [P, 2, BLK], F32R)
        at_lo = place("at_lo", [P, 2, BLK], F32R)
        qb2 = place("qb2", [P, SEQ, 2, S], F32)
        kk2 = place("kk2", [P, BLK], F32)
        wa, wb = at[0], at[0] + 65536
        assert wb + 49152 <= nc.sbuf_usable_end
        hid32 = place("hid32", [P, 2, BLK], F32, work)
        hid_hi = place("hid_hi", [P, 2, BLK], F32R, work + 4096)
        hid_lo = place("hid_lo", [P, 2, BLK], F32R, work + 8192)
        gate_in = place("gate_in", [P, BLK], F32, work + 12288)
        w_hi, w_lo = [], []
        for ph, (kind, layer) in enumerate(PHASES):
            cols = UP[kind, layer] + DOWN[kind, layer]
            base = wa if kind == "attn" else wb
            w_hi.append(place(f"w_hi{ph}", [P, cols], F32R, base))
            w_lo.append(place(f"w_lo{ph}", [P, cols], F32R, base + 4 * cols))
        free = wa + 8 * 3072
        qb = place("qb", [P, DC, SEQ, 2, S], F32, free)
        kk = place("kk", [P, DC, BLK], F32, free + 8192)
        vb = place("vb", [P, TILES, 2, PAIRS * VW], F32, free + 12288)
        rot = place("rot", [P, 2, 2, BLK], F32, free + 12288 + 8448)
        on = place("on", [P, SEQ, P], F32, free + 12288 + 8448 + 8192)
        assert free + 12288 + 8448 + 8192 + 4096 <= wb
        free3 = wa + 8 * 2048
        mask_k8 = place("mask_k8", [P, blocks * BLK], U8, free3)
        q0_sb = place("q0_sb", [P, DC, BLK], F32, free)
        v0_sb = place("v0_sb", [P, TILES, D], F32, free + 12288)
        mask_kf = place("mask_kf", [P, BLK], F32, free3 + 4096)
        mask_b = place("mask_b", [P, BLK], F32, free3 + 6144)
        v2_sb = place("v2_sb", [P, TILES, 1024], F32, wb + 32768)
        modw = place("modw", [P, sum(MOD_COLS.values())], F32, wb)
        cond = place("cond", [P, DC, batch], F32, work)
        cond_silu = place("cond_silu", [P, DC, batch], F32, work + 512)
        t1_g = place("t1_g", [P, DC, batch], F32, work + 1024)
        t1_h = place("t1_h", [P, DC, batch], F32, work + 1536)

        psum = ctx.enter_context(nc.psum_tensor("psum", [P, 8, 512], F32))
        A_BANK, S_BANK, T_BANK, O_BANK, W_BANK = 0, 2, 4, 5, 6
        acc_a = [psum[:, A_BANK + i, :] for i in range(2)]
        scores = [psum[:, S_BANK + i, :] for i in range(2)]
        probs_tp = psum[:, T_BANK, :]
        heads = psum[:, O_BANK, :]
        wide = psum[:, W_BANK:W_BANK + 2, :]
        mlp_back = psum[:, T_BANK:T_BANK + 2, :]

        def col(name, k=0, n=1):
            o = VEC[name][0] + k
            return vec[:, o:o + n]

        ident = col("ident", 0, P)

        def by_seq(ap):
            return ap.rearrange("p (b k) -> p b k", k=S)

        def over_tokens(per_seq):
            return per_seq.unsqueeze(2).to_broadcast([per_seq.shape[0], per_seq.shape[1], S])

        def modulation(slot, c, b):
            return over_tokens(mod[:, slot + c, bass.ds(b * SEQ, SEQ)])

        def run_blocks(eng, ph, stage_of):
            ahead, body = order_of(*PHASES[ph])
            for s, k, _ in ahead:
                stage_of(ph, s, k, 0)
            with eng.Fori(0, blocks - 1) as i:
                for s, k, is_next in body:
                    stage_of(ph, s, k, i + 1 if is_next else i)
            for s, k, is_next in body:
                if not is_next:
                    stage_of(ph, s, k, blocks - 1)

        def a_slot(ph, s, k):
            layer = PHASES[ph][1]
            if s == "turn":
                return k
            if layer == 0:
                return {"q": 2, "k": 4, "v": 6}[s] + k
            if layer == 3:
                return {"q": 2 + 2 * k, "k": 3 + 2 * k, "v": 6 + k}[s]
            if layer == 1:
                return {"q": 2 + 4 * k, "k": 4 + 4 * k, "v": 10 + k}[s]
            return {"v": 2 + k, "q": 10 + 2 * k, "k": 11 + 2 * k}[s]

        def wait_alone(eng, semaphore, value):
            eng.wait_ge(semaphore, value)
            eng.sem_inc(waits_passed, 1)

        def last_h_reader(ph, b):
            if PHASES[ph][0] == "mlp":
                return sem["s_full1"], n_at("s_full1", ph, b, 0)
            return sem["a_full1"], n_at("a_full1", ph, b, 0)

        block = ctx.enter_context(nc.Block())

        @block.sync
        def _(sp):
            for name in NAMES:
                sp.sem_inc(sem[name], CREDIT)
            sp.dma_start(vec[:, :], vec_in).then_inc(vec_loaded, 16)
            sp.dma_start(cond[:, :, :], cond_in).then_inc(vec_loaded, 16)
            o = 0
            for i, (name, cols) in enumerate(MOD_COLS.items()):
                sp.dma_start(modw[:, o:o + cols], modw_in[:, o:o + cols]).then_inc(modw_loaded[i], 16)
                o += cols
            sp.dma_start(xres[:, :, :], x_in.rearrange("t p d -> p t d")).then_inc(x_loaded, 16)
            sp.dma_start(mask_q8[:, :], mask_q_in).then_inc(mask_loaded, 16)
            for ph in range(phases):
                cols = (UP[PHASES[ph]] + DOWN[PHASES[ph]]) // blocks
                parts = -(-cols // 1024)
                part = cols // parts
                if ph == 6:
                    sp.wait_ge(sem["x_done"], n_at("x_done", 5, 0, 1))
                    sp.dma_start(mask_k8[:, :], mask_k_in.partition_broadcast(P)).then_inc(mask_loaded, 16)
                done = sum((UP[PHASES[q]] + DOWN[PHASES[q]]) // part_of(q, blocks) for q in range(ph))
                for i in range(blocks * parts):
                    n = done + i
                    if n >= 1:
                        sp.wait_ge(w_ready, n)
                    sp.dma_start(stage[:, 0:part], weights_in[ph][:, i * part:(i + 1) * part]).then_inc(w_staged, 16)
            last = phases - 1
            with sp.Fori(0, blocks) as b:
                sp.wait_ge(sem["x_done"], n_at("x_done", last, b, 1 + 1))
                sp.dma_start(out.rearrange("t p d -> p t d")[:, bass.ds(b * TILES, TILES), :],
                             xres[:, bass.ds(b * TILES, TILES), :]).then_inc(stored, 16)
            sp.wait_ge(stored, 16 * blocks)

        @block.tensor
        def _(pe):
            pe.wait_ge(vec_loaded, 32)
            woff = {}
            o = 0
            for name, cols in MOD_COLS.items():
                woff[name] = o
                o += cols

            def mod_product(name, rhs, banks):
                n_out = MOD_COLS[name] // DC // P
                for m in range(n_out):
                    dst = psum[:, banks + m // 8, (m % 8) * batch:(m % 8) * batch + batch]
                    for kc in range(DC):
                        w = woff[name] + kc * (MOD_COLS[name] // DC) + m * P
                        ins = nc.tensor.matmul(dst, modw[:, w:w + P], rhs[:, kc, :], start=kc == 0, stop=kc == DC - 1)
                ins.then_inc(mod_mm, 1)

            pe.wait_ge(modw_loaded[0], 16)
            mod_product("film", cond, 0)
            pe.wait_ge(modw_loaded[1], 16)
            mod_product("t1", cond, 1)
            pe.wait_ge(mod_act, 1)
            pe.wait_ge(modw_loaded[2], 16)
            mod_product("mod2", cond_silu, 3)
            pe.wait_ge(modw_loaded[3], 16)
            mod_product("mod3", cond_silu, 5)
            pe.wait_ge(mod_dve, 1)
            pe.wait_ge(modw_loaded[4], 16)
            mod_product("t2", t1_h, 2)

            def weight(ph, part, kc, o, n=P):
                key = PHASES[ph]
                if part == "up":
                    c = kc * (UP[key] // DC) + o
                else:
                    c = UP[key] + kc * D + o
                return w_hi[ph][:, c:c + n], w_lo[ph][:, c:c + n]

            def project(dst, pairs, start=True, stop=True):
                for j, ((s_hi, s_lo), (m_hi, m_lo)) in enumerate(pairs):
                    nc.tensor.matmul(dst, s_lo, m_hi, start=start and j == 0, stop=False)
                    nc.tensor.matmul(dst, s_hi, m_lo, start=False, stop=False)
                    ins = nc.tensor.matmul(dst, s_hi, m_hi, start=False, stop=stop and j == len(pairs) - 1)
                return ins

            def fill_a(ph, b, n):
                pe.wait_ge(sem[f"a_free{n % 2}"], n_at(f"a_free{n % 2}", ph, b, n // 2))
                return acc_a[n % 2]

            def up_rows(ph, b, n, o):
                ins = project(fill_a(ph, b, n), [(weight(ph, "up", kc, o), (h_hi[:, kc, :], h_lo[:, kc, :]))
                                                 for kc in range(DC)])
                ins.then_inc(sem[f"a_full{n % 2}"], 1)

            def stage_of(ph, s, k, b):
                kind, layer = PHASES[ph]
                c, j, slot = k // 4, k % 4, k % 2
                if s == "turn":
                    pe.wait_ge(sem["normed"], n_at("normed", ph, b, 1))
                    for m in range(DC):
                        dst = fill_a(ph, b, m)
                        for t in range(TILES):
                            ins = nc.tensor.transpose(dst[:, t * P:(t + 1) * P], xn[:, t, m * P:(m + 1) * P], ident)
                        ins.then_inc(sem[f"a_full{m}"], 1)
                elif s in ("q", "k") and kind == "attn":
                    n = a_slot(ph, s, k)
                    pe.wait_ge(sem["h"], n_at("h", ph, b, 2))
                    width = 1024 if layer == 2 else D
                    up_rows(ph, b, n, (0 if s == "q" else width) + k * P)
                    if layer == 1:
                        up_rows(ph, b, n + 1, (768 if s == "q" else 1024) + k * P)
                elif s == "v":
                    n = a_slot(ph, s, k)
                    pe.wait_ge(sem["h"], n_at("h", ph, b, 2))
                    dst = fill_a(ph, b, n)
                    if layer == 2:
                        t = k // 2
                        cols = slice(t * P, (t + 1) * P)
                        ins = project(dst, [((h_hi[:, kc, cols], h_lo[:, kc, cols]),
                                             weight(ph, "up", kc, 2048 + 512 * (k % 2), 512)) for kc in range(DC)])
                    else:
                        for u in range(2):
                            cols = slice((2 * k + u) * P, (2 * k + u + 1) * P)
                            ins = project(dst[:, u * D:(u + 1) * D],
                                          [((h_hi[:, kc, cols], h_lo[:, kc, cols]), weight(ph, "up", kc, 2 * D, D))
                                           for kc in range(DC)])
                    ins.then_inc(sem[f"a_full{n % 2}"], 1)
                elif s == "scores":
                    pe.wait_ge(sem[f"s_free{slot}"], n_at(f"s_free{slot}", ph, b, k // 2))
                    dst = scores[slot]
                    if layer == 0:
                        pe.wait_ge(sem["q"], n_at("q", ph, b, 2))
                        pe.wait_ge(sem["k"], n_at("k", ph, b, 2))
                        for g in range(SEQ):
                            tok = slice(g * S, (g + 1) * S)
                            half = slice((g % 2) * S, (g % 2) * S + S)
                            for kc in range(DC):
                                ins = nc.tensor.matmul(dst[half, (g // 2) * S:(g // 2 + 1) * S], q0_sb[:, kc, tok],
                                                       kk[:, kc, tok], start=kc == 0, stop=kc == DC - 1)
                    else:
                        if layer == 2:
                            rows, q_ap, k_ap = slice(0, P), qb2[:, :, :, :], kk2[:, :]
                            pe.wait_ge(sem["q"], n_at("q", ph, b, 2 * (k + 1)))
                            pe.wait_ge(sem["k"], n_at("k", ph, b, k + 1))
                        else:
                            rows, q_ap, k_ap = slice(32 * j, 32 * j + 32), qb[:, c, :, :, :], kk[:, c, :]
                            pe.wait_ge(sem["q"], n_at("q", ph, b, 2 * (c + 1)))
                            pe.wait_ge(sem["k"], n_at("k", ph, b, c + 1))
                        for g in range(SEQ):
                            tok = slice(g * S, (g + 1) * S)
                            ins = nc.tensor.matmul(dst[:, tok], q_ap[rows, g, :, :].rearrange("p h q -> p (h q)"), k_ap[rows, tok],
                                                   start=True, stop=True)
                    ins.then_inc(sem[f"s_full{slot}"], 1)
                elif s == "probs_t":
                    ready = "even" if layer in (0, 2) else "probs"
                    pe.wait_ge(sem[ready], n_at(ready, ph, b, k + 1))
                    pe.wait_ge(sem["probs_t"], n_at("probs_t", ph, b, k))
                    for t in range(TILES):
                        ins = nc.tensor.transpose(probs_tp[:, t * P:(t + 1) * P], pb[:, slot, t * P:(t + 1) * P], ident)
                    ins.then_inc(sem["t_full"], 1)
                elif s == "pv" and layer == 0:
                    pe.wait_ge(sem["probs_t"], n_at("probs_t", ph, b, 1))
                    pe.wait_ge(sem["v"], n_at("v", ph, b, 2))
                    pe.wait_ge(sem["x_done"], n_at("x_done", ph, b, 1))
                    for m in range(DC):
                        for t in range(TILES):
                            ins = nc.tensor.matmul(wide[:, m, t * P:(t + 1) * P], v0_sb[:, t, m * P:(m + 1) * P],
                                                   pt[:, 0, t * P:(t + 1) * P], start=True, stop=True)
                    ins.then_inc(sem["w_full"], 1)
                elif s == "pv" and layer in (1, 3):
                    pe.wait_ge(sem["probs_t"], n_at("probs_t", ph, b, k + 1))
                    pe.wait_ge(sem["v"], n_at("v", ph, b, 4))
                    pe.wait_ge(sem["o_free"], n_at("o_free", ph, b, k))
                    for t in range(TILES):
                        ins = nc.tensor.matmul(heads[:, t * 2 * VW:(t + 1) * 2 * VW], pt[:, slot, t * P:(t + 1) * P],
                                               vb[:, t, :, k * VW:(k + 1) * VW], start=True, stop=True)
                    ins.then_inc(sem["o_full"], 1)
                elif s in ("pv", "pv2"):
                    g = 0 if s == "pv" else 1
                    if g == 0:
                        pe.wait_ge(sem["probs_t"], n_at("probs_t", ph, b, k + 1))
                        pe.wait_ge(sem["v"], n_at("v", ph, b, 8))
                        wait_alone(pe, sem["o_free"], n_at("o_free", ph, b, k))
                    else:
                        wait_alone(pe, sem["pv1"], n_at("pv1", ph, b, k + 1))
                    rows = slice(g * S, (g + 1) * S)
                    for t in range(TILES):
                        for hd in range(2):
                            o = t * P + g * S
                            ins = nc.tensor.matmul(heads[hd * S:(hd + 1) * S, o:o + S],
                                                   v2_sb[rows, t, (2 * k + hd) * S:(2 * k + hd + 1) * S],
                                                   pt[rows, slot, t * P + hd * S:t * P + (hd + 1) * S],
                                                   start=True, stop=True)
                    ins.then_inc(sem["pv1" if g == 0 else "o_full"], 1)
                elif s == "merge":
                    pe.wait_ge(sem["o_free"], n_at("o_free", ph, b, PAIRS))
                    pe.wait_ge(sem["x_done"], n_at("x_done", ph, b, 1))
                    for g in range(SEQ):
                        ins = nc.tensor.transpose(wide[:, g // 4, (g % 4) * P:(g % 4 + 1) * P], on[:, g, :], ident)
                    ins.then_inc(sem["w_full"], 1)
                elif s == "proj" and layer == 2:
                    pe.wait_ge(sem["att"], n_at("att", ph, b, k + 1))
                    if k == 0:
                        pe.wait_ge(sem["x_done"], n_at("x_done", ph, b, 1))
                    for m in range(DC):
                        ins = project(wide[:, m, :], [(weight(ph, "down", k, m * P), (at_hi[:, slot, :], at_lo[:, slot, :]))],
                                      start=k == 0, stop=k == PAIRS - 1)
                    ins.then_inc(sem["proj"], 1)
                elif s == "proj":
                    pe.wait_ge(sem["att"], n_at("att", ph, b, 2))
                    pe.wait_ge(sem["w_free"], n_at("w_free", ph, b, 1))
                    for m in range(DC):
                        ins = project(wide[:, m, :], [(weight(ph, "down", kc, m * P), (at_hi[:, kc, :], at_lo[:, kc, :]))
                                                      for kc in range(DC)])
                    ins.then_inc(sem["w_full"], 1)
                elif s == "up":
                    pe.wait_ge(sem["h"], n_at("h", ph, b, 2))
                    if layer == 1:
                        todo = [(0, k, k), (1, k, HID + k)]
                    else:
                        todo = [(slot, k // 2, k)]
                    for sl, nth, m in todo:
                        pe.wait_ge(sem[f"s_free{sl}"], n_at(f"s_free{sl}", ph, b, nth))
                        ins = project(scores[sl], [(weight(ph, "up", kc, m * P), (h_hi[:, kc, :], h_lo[:, kc, :]))
                                                   for kc in range(DC)])
                        ins.then_inc(sem[f"s_full{sl}"], 1)
                elif s == "down":
                    pe.wait_ge(sem["hid"], n_at("hid", ph, b, k + 1))
                    if k == 0:
                        pe.wait_ge(sem["out_rows"], n_at("out_rows", ph, b, 0))
                    for m in range(DC):
                        ins = project(wide[:, m, :], [(weight(ph, "down", k, m * P), (hid_hi[:, slot, :], hid_lo[:, slot, :]))],
                                      start=k == 0, stop=k == HID - 1)
                    ins.then_inc(sem["down"], 1)
                elif s == "back":
                    pe.wait_ge(sem["out_rows"], n_at("out_rows", ph, b, 2))
                    if kind == "mlp":
                        pe.wait_ge(sem["x_done"], n_at("x_done", ph, b, 1))
                    dst = mlp_back if kind == "mlp" else wide
                    for t in range(TILES):
                        for m in range(DC):
                            o = (t % 2) * D + m * P
                            ins = nc.tensor.transpose(dst[:, t // 2, o:o + P], y[:, m, t * P:(t + 1) * P], ident)
                    ins.then_inc(sem["back" if kind == "mlp" else "w_full"], 1)

            for ph in range(phases):
                pe.wait_ge(sem["x_done"], n_at("x_done", ph, 0, 1))
                pe.wait_ge(w_ready, sum((UP[PHASES[q]] + DOWN[PHASES[q]]) // part_of(q, blocks) for q in range(ph + 1)))
                run_blocks(pe, ph, stage_of)

        @block.scalar
        def _(act):
            act.wait_ge(vec_loaded, 32)
            nc.scalar.activation(cond_silu[:, :, :], cond[:, :, :], ACT.Silu).then_inc(mod_act, 1)
            act.wait_ge(mod_mm, 2)
            for kc in range(DC):
                nc.scalar.activation(t1_g[:, kc, :], psum[:, 1, (2 + kc) * batch:(3 + kc) * batch], ACT.Silu,
                                     bias=col("t1_b", 2 + kc)).then_inc(mod_act, 1)

            def stage_of(ph, s, k, b):
                kind, layer = PHASES[ph]
                c, j, slot = k // 4, k % 4, k % 2
                if s == "turn":
                    for m in range(DC):
                        act.wait_ge(sem["modded"], n_at("modded", ph, b, m + 1))
                        act.wait_ge(*last_h_reader(ph, b))
                        nc.scalar.activation(h_hi[:, m, :], hm[:, m, :], ACT.Copy).then_inc(sem["h_hi"], 1)
                elif s in ("q", "k", "v") and kind == "attn":
                    n = a_slot(ph, s, k)
                    full, fre = sem[f"a_full{n % 2}"], sem[f"a_free{n % 2}"]
                    src = acc_a[n % 2]
                    if layer == 0:
                        act.wait_ge(full, n_at(f"a_full{n % 2}", ph, b, n // 2 + 1))
                        if s == "v":
                            act.wait_ge(sem["w_full"], n_at("w_full", ph, b, -2))
                            nc.scalar.activation(v0_sb[:, 2 * k:2 * k + 2, :], src.rearrange("p (t d) -> p t d", d=D),
                                                 ACT.Copy).then_inc(fre, 1)
                        else:
                            act.wait_ge(sem["s_full0"], n_at("s_full0", ph, b, 0))
                            dst = q0_sb if s == "q" else kk
                            nc.scalar.activation(dst[:, k, :], src, ACT.Identity, bias=col(f"{s}0", k)).then_inc(fre, 1)
                        act.wait_ge(fre, n_at(f"a_free{n % 2}", ph, b, n // 2 + 1))
                        act.sem_inc(sem[s], 1)
                    elif layer == 2:
                        act.wait_ge(full, n_at(f"a_full{n % 2}", ph, b, n // 2 + 1))
                        if s == "v":
                            act.wait_ge(sem["o_full"], n_at("o_full", ph, b, 0))
                            nc.scalar.activation(v2_sb[:, k // 2, 512 * (k % 2):512 * (k % 2) + 512], src,
                                                 ACT.Copy).then_inc(fre, 1)
                            act.wait_ge(fre, n_at(f"a_free{n % 2}", ph, b, n // 2 + 1))
                            act.sem_inc(sem["v"], 1)
                        elif s == "q":
                            before_slot = (k - 1) % 2
                            act.wait_ge(sem[f"s_full{before_slot}"],
                                        n_at(f"s_full{before_slot}", ph, b, 0 if k == 0 else (k - 1) // 2 + 1))
                            nc.scalar.activation(qb2[0:S, :, 0, :], by_seq(src[0:S, :]), ACT.Copy).then_inc(sem["q"], 1)
                            nc.scalar.activation(qb2[S:P, :, 1, :], by_seq(src[S:P, :]), ACT.Copy).then_inc(sem["q"], 1)
                            act.wait_ge(sem["q"], n_at("q", ph, b, 2 * (k + 1)))
                            act.sem_inc(fre, 1)
                        else:
                            nc.scalar.activation(kk2[:, :], src, ACT.Copy).then_inc(sem["k"], 1)
                            act.wait_ge(sem["k"], n_at("k", ph, b, k + 1))
                            act.sem_inc(fre, 1)
                    elif s == "v":
                        act.wait_ge(full, n_at(f"a_full{n % 2}", ph, b, n // 2 + 1))
                        act.wait_ge(sem["o_full"], n_at("o_full", ph, b, 0))
                        for g in range(2):
                            rows = slice(g * S, (g + 1) * S)
                            dst = vb[rows, 2 * k:2 * k + 2, g, :].rearrange("p t (r w) -> p t r w", w=VW)[:, :, :, 0:VW - 1]
                            nc.scalar.activation(dst, src[rows, :].rearrange("p (t r w) -> p t r w", t=2, w=VW - 1),
                                                 ACT.Copy).then_inc(sem["v"], 1)
                        act.wait_ge(sem["v"], n_at("v", ph, b, 2 * (k + 1)))
                        act.sem_inc(fre, 1)
                    elif s == "k" and layer == 3:
                        act.wait_ge(full, n_at(f"a_full{n % 2}", ph, b, n // 2 + 1))
                        act.wait_ge(sem["s_full1"], n_at("s_full1", ph, b, -2 if k == 0 else 0))
                        nc.scalar.activation(kk[:, k, :], src, ACT.Identity, bias=col("k3", k)).then_inc(sem["k"], 1)
                        act.wait_ge(sem["k"], n_at("k", ph, b, k + 1))
                        act.sem_inc(fre, 1)
                    elif s == "q":
                        act.wait_ge(sem["q32"], n_at("q32", ph, b, k + 1))
                        act.wait_ge(sem["s_full1"], n_at("s_full1", ph, b, -2 if k == 0 else 0))
                        for hd, parity in enumerate(("even", "odd")):
                            nc.scalar.activation(qb[:, k, :, hd, :], by_seq(rot[:, 0, 0, :]), ACT.Copy,
                                                 scale=col(parity)).then_inc(sem["q"], 1)
                elif s == "scores":
                    if layer == 0:
                        act.wait_ge(sem["shifted"], n_at("shifted", ph, b, 2))
                        for g in range(2):
                            rows = slice(g * S, (g + 1) * S)
                            ap = pb[rows, 0, :].rearrange("p (t g k) -> p t g k", g=2, k=S)[:, :, g, :]
                            ins = nc.scalar.activation(ap, ap, ACT.Exp, scale=SCORE_SCALE[0])
                            if g == 1:
                                ins.then_inc(sem["probs"], 1)
                    else:
                        act.wait_ge(sem["shifted"], n_at("shifted", ph, b, k + 1))
                        nc.scalar.activation(pb[:, slot, :], pb[:, slot, :], ACT.Exp,
                                             scale=SCORE_SCALE[layer]).then_inc(sem["probs"], 1)
                elif s == "probs_t":
                    act.wait_ge(sem["t_full"], n_at("t_full", ph, b, k + 1))
                    if layer == 0:
                        act.wait_ge(sem["w_full"], n_at("w_full", ph, b, -2))
                    else:
                        act.wait_ge(sem["o_full"], n_at("o_full", ph, b, k - 1))
                    nc.scalar.activation(pt[:, slot, :], probs_tp, ACT.Copy).then_inc(sem["probs_t"], 1)
                elif s in ("pv", "merge") and (layer == 0 or s == "merge"):
                    act.wait_ge(sem["w_full"], n_at("w_full", ph, b, 1))
                    for m in range(DC):
                        if layer == 0:
                            src = wide[:, m, :]
                            dst = at_hi[:, m, :]
                        else:
                            src = wide.rearrange("p w (g h q) -> p (w g) h q", h=2, q=S)[:, :, m, :]
                            dst = by_seq(at_hi[:, m, :])
                        nc.scalar.activation(dst, src, ACT.Identity, bias=col(f"v{layer}", m)).then_inc(sem["att_hi"], 1)
                elif s == "pv2":
                    act.wait_ge(sem["o_full"], n_at("o_full", ph, b, k + 1))
                    act.wait_ge(sem["proj"], n_at("proj", ph, b, k - 1))
                    nc.scalar.activation(at_hi[:, slot, :], heads, ACT.Copy).then_inc(sem["att_hi"], 1)
                elif s == "proj" and layer in (0, 1):
                    act.wait_ge(sem["w_full"], n_at("w_full", ph, b, 2))
                    for m in range(DC):
                        nc.scalar.activation(y[:, m, :], wide[:, m, :], ACT.Identity,
                                             bias=col(f"o{layer}", m)).then_inc(sem["out_rows"], 1)
                elif s == "up":
                    if layer == 1:
                        act.wait_ge(sem["s_full1"], n_at("s_full1", ph, b, k + 1))
                        act.wait_ge(sem["hid32"], n_at("hid32", ph, b, k))
                        nc.scalar.activation(gate_in[:, :], scores[1], ACT.Silu, bias=col("u1", HID + k)).then_inc(sem["gate_in"], 1)
                        act.wait_ge(sem["gate_in"], n_at("gate_in", ph, b, k + 1))
                        act.sem_inc(sem["s_free1"], 1)
                    else:
                        func = ACT.Gelu_apprx_tanh if layer == 3 else ACT.Gelu
                        act.wait_ge(sem[f"s_full{slot}"], n_at(f"s_full{slot}", ph, b, k // 2 + 1))
                        act.wait_ge(sem["hid"], n_at("hid", ph, b, k - 1))
                        nc.scalar.activation(hid32[:, slot, :], scores[slot], func, bias=col(f"u{layer}", k)).then_inc(sem["hid32"], 1)
                    act.wait_ge(sem["hid32"], n_at("hid32", ph, b, k + 1))
                    if layer != 1:
                        act.sem_inc(sem[f"s_free{slot}"], 1)
                    act.wait_ge(sem["down"], n_at("down", ph, b, k - 1))
                    nc.scalar.activation(hid_hi[:, slot, :], hid32[:, slot, :], ACT.Copy).then_inc(sem["hid_hi"], 1)
                elif s == "down" and k == HID - 1 and layer in (0, 1):
                    act.wait_ge(sem["down"], n_at("down", ph, b, HID))
                    act.wait_ge(sem["back"], n_at("back", ph, b, 0))
                    for m in range(DC):
                        nc.scalar.activation(y[:, m, :], wide[:, m, :], ACT.Identity,
                                             bias=col(f"d{layer}", m)).then_inc(sem["out_rows"], 1)

            for ph in range(phases):
                act.wait_ge(sem["x_done"], n_at("x_done", ph, 0, 1))
                run_blocks(act, ph, stage_of)

        @block.vector
        def _(dve):
            dve.wait_ge(vec_loaded, 32)

            def mod_bias(slots, first, n):
                nc.vector.tensor_tensor(mod[:, first:first + n, :],
                                        slots.rearrange("p (n b) -> p n b", b=batch)[:, 0:n, :],
                                        col("mod_b", first, n).unsqueeze(2).to_broadcast([P, n, batch]),
                                        ALU.add).then_inc(mod_dve, 1)

            def mod_scale(slot, norm):
                for c in range(DC):
                    ap = mod[:, slot + c, :]
                    if norm is None:
                        nc.vector.tensor_scalar(ap, ap, 1.0, None, ALU.add).then_inc(consts_ready, 1)
                    else:
                        nc.vector.tensor_scalar(ap, ap, 1.0, col("norm", norm + c), ALU.add, ALU.mult).then_inc(consts_ready, 1)

            dve.wait_ge(mod_act, 3)
            for kc in range(DC):
                nc.vector.scalar_tensor_tensor(t1_h[:, kc, :], psum[:, 1, kc * batch:(kc + 1) * batch], col("t1_b", kc),
                                               t1_g[:, kc, :], ALU.add, ALU.mult).then_inc(consts_ready, 1)
            dve.wait_ge(consts_ready, 2)
            dve.sem_inc(mod_dve, 1)
            full = 8 * batch
            dve.wait_ge(mod_mm, 5)
            mod_bias(psum[:, 0, 0:full], 0, 8)
            mod_bias(psum[:, 2, 0:full], 8, 8)
            mod_bias(psum[:, 3, 0:full], 16, 8)
            mod_bias(psum[:, 4, 0:full], 24, 4)
            mod_bias(psum[:, 5, 0:full], 28, 8)
            mod_bias(psum[:, 6, 0:full], 36, 4)
            for layer in range(4):
                nc.vector.memset(eps_t[:, layer, :], EPS[layer]).then_inc(mod_dve, 1)
            nc.vector.memset(half_t[:, :], -0.5).then_inc(mod_dve, 1)
            dve.wait_ge(mask_loaded, 16)
            dve.wait_ge(x_loaded, 16)
            nc.vector.tensor_copy(mask_q[:, :], mask_q8[:, :]).then_inc(mod_dve, 1)
            nc.vector.memset(pb[:, :, :], 0.0).then_inc(mod_dve, 1)
            dve.wait_ge(mod_dve, 1 + 6 + 5 + 1 + 1)
            for ph, norm in ((0, 0), (1, 2), (2, 4), (3, 6), (4, None), (5, None), (6, None), (7, None)):
                mod_scale(MOD[PHASES[ph]][0], norm)
            dve.wait_ge(consts_ready, 2 + 16)
            dve.sem_inc(sem["x_done"], 1)

            def stage_of(ph, s, k, b):
                kind, layer = PHASES[ph]
                c, j, slot = k // 4, k % 4, k % 2
                scale, shift, gate = MOD[PHASES[ph]]
                if s == "stats":
                    for t in range(TILES):
                        ins = nc.vector.bn_stats(st[:, t, :], xres[:, b * TILES + t, :])
                    ins.then_inc(sem["stats_raw"], 1)
                    wait_alone(dve, sem["stats_raw"], n_at("stats_raw", ph, b, 1))
                    for t in range(TILES):
                        ins = nc.vector.bn_aggr(mv[:, t, :], st[:, t, :])
                    ins.then_inc(sem["stats"], 1)
                    dve.wait_ge(sem["stats"], n_at("stats", ph, b, 1))
                    if layer < 2:
                        nc.vector.tensor_tensor(ms[:, :], mv[:, :, 0], mv[:, :, 0], ALU.mult).then_inc(sem["mean_sq"], 1)
                        dve.wait_ge(sem["mean_sq"], n_at("mean_sq", ph, b, 1))
                        nc.vector.tensor_tensor(ms[:, :], ms[:, :], mv[:, :, 1], ALU.add).then_inc(sem["rstd_in"], 1)
                    else:
                        nc.vector.tensor_copy(ms[:, :], mv[:, :, 1]).then_inc(sem["rstd_in"], 1)
                elif s == "norm":
                    dve.wait_ge(sem["rstd"], n_at("rstd", ph, b, 1))
                    for t in range(TILES):
                        if layer < 2:
                            ins = nc.vector.tensor_scalar(xn[:, t, :], xres[:, b * TILES + t, :], rstd[:, t:t + 1], None, ALU.mult)
                        else:
                            ins = nc.vector.tensor_scalar(xn[:, t, :], xres[:, b * TILES + t, :], mv[:, t, 0:1],
                                                          rstd[:, t:t + 1], ALU.subtract, ALU.mult)
                    ins.then_inc(sem["normed"], 1)
                elif s == "turn":
                    for m in range(DC):
                        n = n_at(f"a_full{m}", ph, b, 1)
                        dve.wait_ge(sem[f"a_full{m}"], n)
                        nc.vector.tensor_tensor(by_seq(hm[:, m, :]), by_seq(acc_a[m]), modulation(scale, m, b),
                                                ALU.mult).then_inc(sem[f"a_free{m}"], 1)
                    for m in range(DC):
                        dve.wait_ge(sem[f"a_free{m}"], n_at(f"a_free{m}", ph, b, 1))
                        nc.vector.tensor_tensor(by_seq(hm[:, m, :]), by_seq(hm[:, m, :]), modulation(shift, m, b),
                                                ALU.add).then_inc(sem["modded"], 1)
                    for m in range(DC):
                        dve.wait_ge(sem["h_hi"], n_at("h_hi", ph, b, m + 1))
                        nc.vector.tensor_tensor(h_lo[:, m, :], hm[:, m, :], h_hi[:, m, :].bitcast(F32),
                                                ALU.subtract).then_inc(sem["h"], 1)
                elif s in ("q", "k") and layer == 1:
                    n = a_slot(ph, s, k)
                    which = 0 if s == "q" else 1
                    nth = 2 * k + which + 1
                    if s == "q":
                        dve.wait_ge(sem["q"], n_at("q", ph, b, 2 * k))
                    else:
                        dve.wait_ge(sem["k"], n_at("k", ph, b, k))
                    for u, (bias, tab, cnt) in enumerate(((f"{s}1", "cos", "rot_a"), (f"{s}s1", "sin", "rot_b"))):
                        dve.wait_ge(sem[f"a_full{u}"], n_at(f"a_full{u}", ph, b, n // 2 + 1))
                        nc.vector.scalar_tensor_tensor(by_seq(rot[:, which, u, :]), by_seq(acc_a[u]), col(bias, k),
                                                       col(tab, 0, S).unsqueeze(1).to_broadcast([P, SEQ, S]),
                                                       ALU.add, ALU.mult).then_inc(sem[cnt], 1)
                        dve.wait_ge(sem[cnt], n_at(cnt, ph, b, nth))
                        dve.sem_inc(sem[f"a_free{u}"], 1)
                elif s == "q" and layer == 3:
                    n = a_slot(ph, s, k)
                    dve.wait_ge(sem[f"a_full{n % 2}"], n_at(f"a_full{n % 2}", ph, b, n // 2 + 1))
                    dve.wait_ge(sem["q"], n_at("q", ph, b, 2 * k))
                    dve.wait_ge(sem["mask_k"], n_at("mask_k", ph, b, 1))
                    nc.vector.scalar_tensor_tensor(rot[:, 0, 0, :], acc_a[n % 2], col("q3", k), mask_kf[:, :],
                                                   ALU.add, ALU.mult).then_inc(sem["q32"], 1)
                    dve.wait_ge(sem["q32"], n_at("q32", ph, b, k + 1))
                    dve.sem_inc(sem[f"a_free{n % 2}"], 1)
                elif s == "scores" and layer == 0:
                    dve.wait_ge(sem["s_full0"], n_at("s_full0", ph, b, 1))
                    sc = scores[0][:, 0:TILES * S].rearrange("p (t k) -> p t k", k=S)
                    nc.vector.tensor_reduce(mx[:, 0, 0:TILES], sc, AX.X, ALU.max).then_inc(sem["row_max"], 1)
                    dve.wait_ge(sem["row_max"], n_at("row_max", ph, b, 1))
                    dve.wait_ge(sem["t_full"], n_at("t_full", ph, b, 0))
                    for g in range(2):
                        rows = slice(g * S, (g + 1) * S)
                        ap = pb[rows, 0, :].rearrange("p (t g k) -> p t g k", g=2, k=S)[:, :, g, :]
                        nc.vector.tensor_tensor(ap, sc[rows], over_tokens(mx[rows, 0, 0:TILES]),
                                                ALU.subtract).then_inc(sem["shifted"], 1)
                    dve.wait_ge(sem["shifted"], n_at("shifted", ph, b, 2))
                    dve.sem_inc(sem["s_free0"], 1)
                elif s == "scores":
                    sc = by_seq(scores[slot])
                    dst = by_seq(pb[:, slot, :])
                    dve.wait_ge(sem[f"s_full{slot}"], n_at(f"s_full{slot}", ph, b, k // 2 + 1))
                    dve.wait_ge(sem["t_full"], n_at("t_full", ph, b, k - 1))
                    if layer == 3:
                        if k == 0:
                            dve.wait_ge(sem["mask"], n_at("mask", ph, b, 1))
                        nc.vector.tensor_tensor(pb[:, slot, :], scores[slot], mask_b[:, :], ALU.add).then_inc(sem["masked"], 1)
                        dve.wait_ge(sem["masked"], n_at("masked", ph, b, k + 1))
                        dve.sem_inc(sem[f"s_free{slot}"], 1)
                        sc = dst
                    nc.vector.tensor_reduce(mx[:, slot, :], sc, AX.X, ALU.max).then_inc(sem["row_max"], 1)
                    dve.wait_ge(sem["row_max"], n_at("row_max", ph, b, k + 1))
                    nc.vector.tensor_tensor(dst, sc, over_tokens(mx[:, slot, :]), ALU.subtract).then_inc(sem["shifted"], 1)
                    if layer != 3:
                        dve.wait_ge(sem["shifted"], n_at("shifted", ph, b, k + 1))
                        dve.sem_inc(sem[f"s_free{slot}"], 1)
                elif s == "even_out":
                    dve.wait_ge(sem["probs"], n_at("probs", ph, b, k + 1))
                    if layer == 0:
                        src, n = pb[:, 0, :].rearrange("p (t k) -> p t k", k=P), TILES
                    else:
                        src, n = by_seq(pb[:, slot, :]), SEQ
                    nc.vector.tensor_reduce(sm[:, slot, 0:n], src, AX.X, ALU.add).then_inc(sem["row_sum"], 1)
                    dve.wait_ge(sem["row_sum"], n_at("row_sum", ph, b, k + 1))
                    dve.wait_ge(sem["even"], n_at("even", ph, b, k - 1))
                    nc.vector.reciprocal(ri[:, slot, 0:n], sm[:, slot, 0:n]).then_inc(sem["row_inv"], 1)
                elif s == "pv" and layer in (1, 3):
                    dve.wait_ge(sem["o_full"], n_at("o_full", ph, b, k + 1))
                    o4 = heads[:, 0:TILES * 2 * VW].rearrange("p (g w) -> p g w", w=VW)
                    nc.vector.reciprocal(ri[:, slot, :], o4[:, :, VW - 1]).then_inc(sem["o_inv"], 1)
                    dve.wait_ge(sem["o_inv"], n_at("o_inv", ph, b, k + 1))
                    if k == 0:
                        dve.wait_ge(sem["w_full"], n_at("w_full", ph, b, -2))
                    for hd in range(2):
                        rows = slice(hd * S, (hd + 1) * S)
                        ins = nc.vector.tensor_tensor(on[rows, :, k * 16:(k + 1) * 16], o4[rows, :, hd * 16:(hd + 1) * 16],
                                                      ri[rows, slot, :].unsqueeze(2).to_broadcast([S, SEQ, 16]), ALU.mult)
                    ins.then_inc(sem["o_free"], 1)
                elif (s == "pv" and layer == 0) or s == "merge":
                    for m in range(DC):
                        if layer == 0:
                            src, hi, lo = wide[:, m, :], at_hi[:, m, :], at_lo[:, m, :]
                        else:
                            src = wide.rearrange("p w (g h q) -> p (w g) h q", h=2, q=S)[:, :, m, :]
                            hi, lo = by_seq(at_hi[:, m, :]), by_seq(at_lo[:, m, :])
                        dve.wait_ge(sem["att_hi"], n_at("att_hi", ph, b, m + 1 if layer == 0 else 2))
                        nc.vector.scalar_tensor_tensor(lo, src, col(f"v{layer}", m), hi.bitcast(F32), ALU.add,
                                                       ALU.subtract).then_inc(sem["att"], 1)
                    dve.wait_ge(sem["att"], n_at("att", ph, b, 2))
                    dve.sem_inc(sem["w_free"], 1)
                elif s == "pv2":
                    dve.wait_ge(sem["att_hi"], n_at("att_hi", ph, b, k + 1))
                    nc.vector.tensor_tensor(at_lo[:, slot, :], heads, at_hi[:, slot, :].bitcast(F32),
                                            ALU.subtract).then_inc(sem["att"], 1)
                    dve.wait_ge(sem["att"], n_at("att", ph, b, k + 1))
                    dve.sem_inc(sem["o_free"], 1)
                elif s == "up":
                    if layer == 1:
                        dve.wait_ge(sem["s_full0"], n_at("s_full0", ph, b, k + 1))
                        dve.wait_ge(sem["gate_in"], n_at("gate_in", ph, b, k + 1))
                        dve.wait_ge(sem["hid"], n_at("hid", ph, b, k - 1))
                        nc.vector.scalar_tensor_tensor(hid32[:, slot, :], scores[0], col("u1", k), gate_in[:, :],
                                                       ALU.add, ALU.mult).then_inc(sem["hid32"], 1)
                        dve.wait_ge(sem["hid32"], n_at("hid32", ph, b, k + 1))
                        dve.sem_inc(sem["s_free0"], 1)
                    dve.wait_ge(sem["hid_hi"], n_at("hid_hi", ph, b, k + 1))
                    nc.vector.tensor_tensor(hid_lo[:, slot, :], hid32[:, slot, :], hid_hi[:, slot, :].bitcast(F32),
                                            ALU.subtract).then_inc(sem["hid"], 1)
                elif gate is not None and ((s == "proj" and (layer == 3 or k == PAIRS - 1)) or (s == "down" and k == HID - 1)):
                    if kind == "mlp":
                        dve.wait_ge(sem["down"], n_at("down", ph, b, HID))
                        dve.wait_ge(sem["back"], n_at("back", ph, b, 0))
                    elif layer == 3:
                        dve.wait_ge(sem["w_full"], n_at("w_full", ph, b, 2))
                    else:
                        dve.wait_ge(sem["proj"], n_at("proj", ph, b, PAIRS))
                    bias = ("d" if kind == "mlp" else "o") + str(layer)
                    for m in range(DC):
                        nc.vector.scalar_tensor_tensor(by_seq(y[:, m, :]), by_seq(wide[:, m, :]), col(bias, m),
                                                       modulation(gate, m, b), ALU.add, ALU.mult).then_inc(sem["out_rows"], 1)
                elif s == "back":
                    if kind == "mlp":
                        dve.wait_ge(sem["back"], n_at("back", ph, b, 1))
                        src = mlp_back
                    else:
                        last = 3 if layer != 2 else 1
                        dve.wait_ge(sem["w_full"], n_at("w_full", ph, b, last))
                        src = wide
                    xs = xres[:, bass.ds(b * TILES, TILES), :].rearrange("p (w t) d -> p w (t d)", w=2)
                    nc.vector.tensor_tensor(xs, xs, src, ALU.add).then_inc(sem["x_done"], 1)

            for ph in range(phases):
                if ph and PHASES[ph][0] == "attn":
                    layer = PHASES[ph][1]
                    dve.wait_ge(sem["x_done"], n_at("x_done", ph, 0, 1))
                    if layer in (1, 3):
                        nc.vector.memset(vb[:, :, :, :], 0.0).then_inc(zeroed, 1)
                        dve.wait_ge(zeroed, 1 if layer == 1 else 5)
                        for g in range(2):
                            rows = slice(g * S, (g + 1) * S)
                            nc.vector.memset(vb[rows, :, g, :].rearrange("p t (r w) -> p t r w", w=VW)[:, :, :, VW - 1],
                                             1.0).then_inc(zeroed, 1)
                    else:
                        nc.vector.memset(qb2[:, :, :, :], 0.0).then_inc(zeroed, 1)
                dve.wait_ge(sem["x_done"], n_at("x_done", ph, 0, 1))
                run_blocks(dve, ph, stage_of)

        @block.gpsimd
        def _(pool):
            shares = [0]

            def split_static(ph, i, part):
                shares[0] += 1
                pool.wait_ge(w_staged, 16 * shares[0])
                nc.gpsimd.tensor_copy(w_hi[ph][:, i * part:(i + 1) * part], stage[:, 0:part]).then_inc(w_hi_done, 1)
                pool.wait_ge(w_hi_done, shares[0])
                nc.gpsimd.tensor_tensor(w_lo[ph][:, i * part:(i + 1) * part], stage[:, 0:part],
                                        w_hi[ph][:, i * part:(i + 1) * part].bitcast(F32), ALU.subtract).then_inc(w_ready, 1)

            def split_next(ph, b):
                if ph + 1 >= phases:
                    return
                nxt = ph + 1
                cols = (UP[PHASES[nxt]] + DOWN[PHASES[nxt]]) // blocks
                parts = -(-cols // 1024)
                part = cols // parts
                done = sum((UP[PHASES[q]] + DOWN[PHASES[q]]) // part_of(q, blocks) for q in range(nxt))
                for u in range(parts):
                    n = b * parts + (done + u + 1)
                    where = bass.ds(b * cols + u * part, part)
                    pool.wait_ge(w_staged, n * 16)
                    nc.gpsimd.tensor_copy(w_hi[nxt][:, where], stage[:, 0:part]).then_inc(w_hi_done, 1)
                    pool.wait_ge(w_hi_done, n)
                    nc.gpsimd.tensor_tensor(w_lo[nxt][:, where], stage[:, 0:part], w_hi[nxt][:, where].bitcast(F32),
                                            ALU.subtract).then_inc(w_ready, 1)

            part0 = part_of(0, blocks)
            for i in range((UP[PHASES[0]] + DOWN[PHASES[0]]) // part0):
                split_static(0, i, part0)

            def stage_of(ph, s, k, b):
                kind, layer = PHASES[ph]
                slot = k % 2
                if s == "stats":
                    pool.wait_ge(sem["rstd_in"], n_at("rstd_in", ph, b, 1))
                    nc.gpsimd.tensor_tensor(ms[:, :], ms[:, :], eps_t[:, layer, :], ALU.add).then_inc(sem["eps_added"], 1)
                    pool.wait_ge(sem["eps_added"], n_at("eps_added", ph, b, 1))
                    nc.gpsimd.tensor_tensor(rstd[:, :], ms[:, :], half_t[:, :], ALU.pow).then_inc(sem["rstd"], 1)
                    if layer == 3 and kind == "attn":
                        pool.wait_ge(sem["q32"], n_at("q32", ph, b, 0))
                        nc.gpsimd.tensor_copy(mask_kf[:, :], mask_k8[:, bass.ds(b * BLK, BLK)]).then_inc(sem["mask_k"], 1)
                elif s == "q" and k == 1 and layer == 3:
                    pool.wait_ge(sem["masked"], n_at("masked", ph, b, 0))
                    wait_alone(pool, sem["mask_k"], n_at("mask_k", ph, b, 1))
                    nc.gpsimd.tensor_scalar(mask_b[:, :], mask_kf[:, :], 1.0, MASKED, ALU.subtract, ALU.mult).then_inc(sem["mask_raw"], 1)
                    pool.wait_ge(sem["mask_raw"], n_at("mask_raw", ph, b, 1))
                    nc.gpsimd.tensor_tensor(by_seq(mask_b[:, :]), by_seq(mask_b[:, :]),
                                            over_tokens(mask_q[:, bass.ds(b * SEQ, SEQ)]), ALU.mult).then_inc(sem["mask"], 1)
                elif s in ("q", "k") and layer == 1:
                    which = 0 if s == "q" else 1
                    pool.wait_ge(sem["rot_b"], n_at("rot_b", ph, b, 2 * k + which + 1))
                    if s == "q":
                        nc.gpsimd.tensor_tensor(rot[:, 0, 0, :], rot[:, 0, 0, :], rot[:, 0, 1, :], ALU.add).then_inc(sem["q32"], 1)
                    else:
                        pool.wait_ge(sem["s_full1"], n_at("s_full1", ph, b, -2 if k == 0 else 0))
                        nc.gpsimd.tensor_tensor(kk[:, k, :], rot[:, 1, 0, :], rot[:, 1, 1, :], ALU.add).then_inc(sem["k"], 1)
                elif s == "even_out":
                    pool.wait_ge(sem["row_inv"], n_at("row_inv", ph, b, k + 1))
                    if layer == 0:
                        ap = pb[:, 0, :].rearrange("p (t k) -> p t k", k=P)
                        inv = ri[:, 0, 0:TILES].unsqueeze(2).to_broadcast([P, TILES, P])
                    else:
                        ap, inv = by_seq(pb[:, slot, :]), over_tokens(ri[:, slot, :])
                    nc.gpsimd.tensor_tensor(ap, ap, inv, ALU.mult).then_inc(sem["even"], 1)
                elif s == "back":
                    split_next(ph, b)

            for ph in range(phases):
                pool.wait_ge(sem["x_done"], n_at("x_done", ph, 0, 1))
                if PHASES[ph] == ("attn", 3):
                    pool.wait_ge(mask_loaded, 32)
                run_blocks(pool, ph, stage_of)


def part_of(ph, blocks):
    cols = (UP[PHASES[ph]] + DOWN[PHASES[ph]]) // blocks
    return cols // -(-cols // 1024)


def rows_first(w):
    return w.reshape(-1, P, w.shape[1]).transpose(1, 0, 2)


def lay_out(i):
    x = np.ascontiguousarray(i["x"])
    batch = x.shape[0]
    cond = np.ascontiguousarray(rows_first(np.ascontiguousarray(i["cond_1024"].T)))
    mask = np.ascontiguousarray(i["mask_BxS_bk1"])
    swap = np.arange(D).reshape(-1, 2)[:, ::-1].reshape(-1)
    heads = np.arange(D).reshape(8, 2, 16).transpose(1, 0, 2).reshape(-1)

    def weights(up, down):
        return np.concatenate([rows_first(up).reshape(P, -1), rows_first(down).reshape(P, -1)], axis=1)

    q1, k1, v1 = (i["L1_cond_w_qkv"][:, n * D:(n + 1) * D] for n in range(3))
    w = [
        weights(np.concatenate([i["L0_cond_q_w"], i["L0_cond_k_w"], i["L0_cond_v_w"]], 1), i["L0_cond_proj_w"]),
        weights(i["L0_cond_mlp_w1"], i["L0_cond_mlp_w2"]),
        weights(np.concatenate([q1, k1, v1, q1[:, swap], k1[:, swap]], 1), i["L1_cond_w_ao"][heads]),
        weights(i["L1_cond_w_fc"], i["L1_cond_w_fo"]),
        weights(i["L2_cond_W_qkv"], i["L2_cond_W_out"]),
        weights(i["L2_cond_W1"], i["L2_cond_W2"]),
        weights(i["L3_cond_qkv_w"].T, i["L3_cond_proj_w"].T[heads]),
        weights(i["L3_cond_fc1_w"].T, i["L3_cond_fc2_w"].T),
    ]
    modw = np.concatenate([rows_first(m).reshape(P, -1) for m in (
        np.concatenate([i["L0_cond_film1_w"], i["L0_cond_film2_w"]], 1), i["L1_cond_w_t1"], i["L2_cond_W_mod"],
        i["L3_cond_ada_w"].T, i["L1_cond_w_t2"])], axis=1)

    def cols(v):
        return v.reshape(-1, P).T

    bq1, bk1, bv1 = (i["L1_cond_b_qkv"][n * D:(n + 1) * D] for n in range(3))
    bq3, bk3, bv3 = (i["L3_cond_qkv_b"][n * D:(n + 1) * D] for n in range(3))
    pair = (np.arange(P) % 16) // 2
    freq = (1.0 / np.float32(10000.0) ** (np.arange(0, 16, 2, dtype=np.float32) / np.float32(16))).astype(np.float32)
    angle = np.arange(S, dtype=np.float32)[None, :] * freq[pair][:, None]
    sign = np.where(np.arange(P) % 2 == 0, -1, 1).astype(np.float32)[:, None]
    parity = ((np.arange(P) // 16) % 2).astype(np.float32)[:, None]
    vec = {
        "mod_b": np.concatenate([cols(i[n]) for n in ("L0_cond_film1_b", "L0_cond_film2_b", "L1_cond_b_t2",
                                                      "L2_cond_b_mod", "L3_cond_ada_b")], 1),
        "t1_b": cols(i["L1_cond_b_t1"]),
        "norm": np.concatenate([cols(i[n]) for n in ("L0_cond_norm1_w", "L0_cond_norm2_w", "L1_cond_g1", "L1_cond_g2")], 1),
        "q0": cols(i["L0_cond_q_b"]), "k0": cols(i["L0_cond_k_b"]), "v0": cols(i["L0_cond_v_b"]),
        "o0": cols(i["L0_cond_proj_b"]), "u0": cols(i["L0_cond_mlp_b1"]), "d0": cols(i["L0_cond_mlp_b2"]),
        "q1": cols(bq1), "k1": cols(bk1), "qs1": cols(bq1[swap]), "ks1": cols(bk1[swap]), "v1": cols(bv1[heads]),
        "o1": cols(i["L1_cond_b_ao"]), "u1": cols(i["L1_cond_b_fc"]), "d1": cols(i["L1_cond_b_fo"]),
        "o2": cols(i["L2_cond_b_out"]), "u2": cols(i["L2_cond_b1"]), "d2": cols(i["L2_cond_b2"]),
        "q3": cols(bq3), "k3": cols(bk3), "v3": cols(bv3[heads]), "o3": cols(i["L3_cond_proj_b"]),
        "u3": cols(i["L3_cond_fc1_b"]), "d3": cols(i["L3_cond_fc2_b"]),
        "even": 1 - parity, "odd": parity, "cos": np.cos(angle), "sin": np.sin(angle) * sign,
        "ident": np.eye(P, dtype=np.float32),
    }
    assert all(vec[n].shape == (P, VEC[n][1]) for n in VEC), {n: vec[n].shape for n in VEC}
    vecs = np.concatenate([vec[n].astype(np.float32, copy=False) for n in VEC], 1)
    arrays = {
        "x": x.reshape(-1, P, D), "cond": cond, "mask_k": mask.reshape(-1),
        "mask_q": np.concatenate([mask.T, mask.T], 0), "vec": vecs, "modw": modw,
    }
    arrays.update({f"w{n}": a for n, a in enumerate(w)})
    return {n: np.ascontiguousarray(a) for n, a in arrays.items()}, batch


def kernel(**inputs):
    import concourse.bacc as _bacc
    from concourse.bass_utils import run_bass_kernel_spmd as _run

    arrays, batch = lay_out({n: np.asarray(a) for n, a in inputs.items()})
    nc = _bacc.Bacc("TRN2", target_bir_lowering=False, num_devices=1)
    dram, sent = {}, {}
    for name, a in arrays.items():
        sent[f"in_{name}_dram"] = a
        dram[name] = nc.dram_tensor(f"in_{name}_dram", a.shape, mybir.dt.from_np(a.dtype), kind="ExternalInput").ap()
    out = nc.dram_tensor("out_0_dram", (batch * S // P, P, D), F32, kind="ExternalOutput").ap()
    build(nc, dram["x"], dram["cond"], dram["mask_k"], dram["mask_q"], dram["vec"], dram["modw"],
          [dram[f"w{n}"] for n in range(len(PHASES))], out, PHASE_LIMIT)
    r = _run(nc, [sent], core_ids=[0])
    return r.results[0]["out_0_dram"].reshape(batch, S, D)


PHASE_LIMIT = len(PHASES)
```

```python
from contextlib import ExitStack

import numpy as np

import concourse.bass as bass
from concourse import mybir

ALU = mybir.AluOpType
ACT = mybir.ActivationFunctionType
AX = mybir.AxisListType
F32 = mybir.dt.float32
F32R = mybir.dt.float32r
U8 = mybir.dt.uint8

P = 128
S = 64
D = 256
DC = D // P
BLK = 512
SEQ = BLK // S
TILES = BLK // P
PAIRS = 8
HID = 8
HW = 17
MASKED = 4e9
CREDIT = 2

PHASES = [(kind, layer) for layer in range(4) for kind in ("attn", "mlp")]
UP = {("attn", 0): DC * 768, ("mlp", 0): DC * 1024, ("attn", 1): DC * 1280, ("mlp", 1): DC * 2048,
      ("attn", 2): DC * 3072, ("mlp", 2): DC * 1024, ("attn", 3): DC * 768, ("mlp", 3): DC * 1024}
DOWN = {(kind, layer): (8 if kind == "mlp" or layer == 2 else 2) * D for kind, layer in PHASES}
EPS = (1e-6, float(np.finfo(np.float32).eps), 1e-5, 1e-6)
SCORE_SCALE = (1 / 16, 1 / 4, 1 / 8, 1 / 4)

MOD = {("attn", 0): (0, 2, None), ("mlp", 0): (4, 6, None), ("attn", 1): (10, 8, None), ("mlp", 1): (14, 12, None),
       ("attn", 2): (18, 16, 20), ("mlp", 2): (24, 22, 26), ("attn", 3): (30, 28, 32), ("mlp", 3): (36, 34, 38)}
MODS = 40
MOD_COLS = {"film": DC * 1024, "t1": DC * 512, "mod2": DC * 1536, "mod3": DC * 1536, "t2": DC * 1024}

VEC = {}
for _name, _n in (("mod_b", MODS), ("t1_b", 4), ("norm", 8),
                  ("q0", 2), ("k0", 2), ("v0", 2), ("o0", 2), ("u0", 8), ("d0", 2),
                  ("q1", 2), ("k1", 2), ("qs1", 2), ("ks1", 2), ("v1", 2), ("o1", 2), ("u1", 16), ("d1", 2),
                  ("o2", 2), ("u2", 8), ("d2", 2),
                  ("q3", 2), ("k3", 2), ("v3", 2), ("o3", 2), ("u3", 8), ("d3", 2),
                  ("even", 1), ("odd", 1), ("cos", S), ("sin", S), ("ident", P)):
    VEC[_name] = (sum(n for _, n in VEC.values()), _n)
VECS = sum(n for _, n in VEC.values())


def order_of(kind, layer):
    prev = lambda s, k=0: (s, k, -1)
    own = lambda s, k=0: (s, k, 0)
    nxt = lambda s, k=0: (s, k, 1)
    if kind == "mlp":
        return [own("up", 2), prev("back"), own("share"), own("down", 0), own("up", 3), own("down", 1), nxt("stats"),
                own("up", 4), own("down", 2), nxt("norm"), own("up", 5), own("down", 3), nxt("turn"),
                own("up", 6), own("down", 4), own("up", 7), own("down", 5), nxt("split"), own("down", 6),
                nxt("up", 0), own("down", 7), nxt("up", 1)]
    if layer == 0:
        return [own("scores"), nxt("stats"), own("v", 0), nxt("norm"), own("v", 1), own("share"), nxt("turn"),
                own("even_out"), prev("proj"), own("probs_t"), nxt("split"), prev("back"), nxt("q", 0), own("pv"),
                nxt("q", 1), nxt("k", 0), nxt("k", 1)]
    if layer in (1, 3):
        return [own("scores", 0), prev("probs_t", 7), own("q", 1), prev("pv", 6), own("share"),
                own("scores", 1), own("probs_t", 0), own("v", 0), prev("pv", 7), own("v", 1), nxt("stats"),
                own("scores", 2), own("probs_t", 1), prev("merge"), own("k", 1), own("pv", 0), nxt("norm"),
                own("scores", 3), own("probs_t", 2), prev("proj"), own("pv", 1), nxt("turn"),
                own("scores", 4), own("probs_t", 3), prev("back"), own("pv", 2), nxt("split"),
                own("scores", 5), own("probs_t", 4), own("pv", 3), nxt("q", 0),
                own("scores", 6), own("probs_t", 5), own("pv", 4), nxt("k", 0),
                own("scores", 7), own("probs_t", 6), own("pv", 5)]
    body = [own("scores", 0), prev("even_out", 7), own("q", 1), own("k", 1), prev("pv", 6), prev("pv2", 6),
            prev("probs_t", 7), prev("proj", 5), own("v", 0), prev("pv", 7), prev("pv2", 7), own("v", 1),
            own("scores", 1), own("even_out", 0), prev("proj", 6), own("v", 2), own("v", 3), own("share"),
            own("q", 2), own("k", 2), own("probs_t", 0), own("v", 4), prev("proj", 7), own("v", 5), own("v", 6),
            own("v", 7), prev("back")]
    for p in range(2, PAIRS):
        body += [own("scores", p), own("even_out", p - 1), own("pv", p - 2), own("pv2", p - 2)]
        body += [own("q", p + 1), own("k", p + 1)] if p < 7 else []
        body += {2: [nxt("stats")], 4: [nxt("norm")], 6: [nxt("turn")]}.get(p, [])
        body += [own("probs_t", p - 1)]
        body += [own("proj", p - 3)] if p >= 3 else []
    return body + [nxt("split"), nxt("q", 0), nxt("k", 0)]


def fills_of(kind, layer):
    body = order_of(kind, layer)
    fills = [("turn", 0), ("turn", 1)]
    for off in (1, 0, -1):
        for s, k, o in body:
            if o == off and s in ("q", "k", "v"):
                fills += [(s, k)] * (2 if layer == 1 and s != "v" else 1)
    return fills


def counts_of(kind, layer):
    c = dict(stats_raw=1, stats=1, mean_sq=1 if layer < 2 else 0, rstd_in=1, rstd=1, normed=1, eps_added=1, modded=2,
             h_hi=2, h=2, out_rows=2, x_done=1)
    if kind == "mlp":
        n = HID * (2 if layer == 1 else 1)
        c.update({"a_full0": 1, "a_full1": 1, "a_free0": 1, "a_free1": 1,
                  "s_full0": n // 2, "s_full1": n // 2, "s_free0": n // 2, "s_free1": n // 2,
                  "hid32": HID, "hid_hi": HID, "hid": HID, "down": HID, "gate_in": HID if layer == 1 else 0,
                  "back": 1})
        return c
    fills = {0: 8, 1: 12, 2: 26, 3: 8}[layer] // 2
    c.update({"a_full0": fills, "a_full1": fills, "a_free0": fills, "a_free1": fills})
    n = 1 if layer == 0 else PAIRS
    c.update({"s_full0": n - n // 2, "s_full1": n // 2, "s_free0": n - n // 2, "s_free1": n // 2,
              "row_max": n, "shifted": n * (2 if layer == 0 else 1), "probs": n, "t_full": n, "probs_t": n})
    if layer in (0, 2):
        c.update(row_sum=n, row_inv=n, even=n)
    if layer == 0:
        c.update(q=2, k=2, v=2, w_full=3, w_free=1, att_hi=2, att=2)
    if layer in (1, 3):
        c.update(o_full=n, o_inv=n // 2, o_free=n // 2, q=2 * 2, k=4 * 2, v=2 * 2, q32=2, w_full=3, w_free=1, att_hi=2, att=2)
    if layer == 1:
        c.update(rot_a=4, rot_b=4, k32=2)
    if layer == 3:
        c.update(masked=n)
    if layer == 2:
        c.update(q=n, k=n, v=8, pv1=n, o_full=n, o_free=n, att_hi=n, att=n, proj=n, w_full=1)
    return c


NAMES = sorted({name for ph in PHASES for name in counts_of(*ph)})


def build(nc, x_in, cond_in, mask_k_in, mask_q_in, vec_in, modw_in, weights_in, out, phases=len(PHASES)):
    batch = cond_in.shape[2]
    blocks = batch // SEQ
    tiles = blocks * TILES

    before = {name: [0] for name in NAMES}
    for ph in range(len(PHASES)):
        for name in NAMES:
            before[name].append(before[name][-1] + blocks * counts_of(*PHASES[ph]).get(name, 0))

    def n_at(name, ph, b, k):
        return b * counts_of(*PHASES[ph]).get(name, 0) + (CREDIT + before[name][ph] + k)

    with ExitStack() as ctx:
        sem = {name: ctx.enter_context(nc.semaphore(name)) for name in NAMES}
        x_loaded = ctx.enter_context(nc.semaphore("x_loaded"))
        vec_loaded = ctx.enter_context(nc.semaphore("vec_loaded"))
        modw_loaded = [ctx.enter_context(nc.semaphore(f"modw_loaded{i}")) for i in range(5)]
        mask_loaded = ctx.enter_context(nc.semaphore("mask_loaded"))
        w_staged = ctx.enter_context(nc.semaphore("w_staged"))
        w_hi_done = ctx.enter_context(nc.semaphore("w_hi_done"))
        w_ready = ctx.enter_context(nc.semaphore("w_ready"))
        consts_ready = ctx.enter_context(nc.semaphore("consts_ready"))
        prepared = ctx.enter_context(nc.semaphore("prepared"))
        mask_made = ctx.enter_context(nc.semaphore("mask_made"))
        mod_mm = ctx.enter_context(nc.semaphore("mod_mm"))
        mod_act = ctx.enter_context(nc.semaphore("mod_act"))
        mod_dve = ctx.enter_context(nc.semaphore("mod_dve"))
        waits_passed = ctx.enter_context(nc.semaphore("waits_passed"))
        stored = ctx.enter_context(nc.semaphore("stored"))

        at = [nc.sbuf_base + (-nc.sbuf_base) % 32]

        def place(name, shape, dt, where=None):
            size = int(np.prod(shape[1:])) * (1 if dt == U8 else 4)
            size += -size % 32
            offset = at[0] if where is None else where
            if where is None:
                at[0] += size
            assert offset + size <= nc.sbuf_usable_end, (name, offset, size)
            return nc.alloc_sbuf_tensor_at(name, shape, dt, offset=offset)

        xres = place("xres", [P, tiles, D], F32)
        mod = place("mod", [P, MODS, batch], F32)
        vec = place("vec", [P, VECS], F32)
        xn = place("xn", [P, TILES, D], F32)
        hm = place("hm", [P, DC, BLK], F32)
        h_hi = place("h_hi", [P, DC, BLK], F32R)
        h_lo = place("h_lo", [P, DC, BLK], F32R)
        y = place("y", [P, DC, BLK], F32)
        stage = place("stage", [P, 1024], F32)
        st = place("st", [P, TILES, 6], F32)
        mv = place("mv", [P, TILES, 2], F32)
        ms = place("ms", [P, TILES], F32)
        rstd = place("rstd", [P, TILES], F32)
        eps_t = place("eps_t", [P, 4, TILES], F32)
        half_t = place("half_t", [P, TILES], F32)
        mx = place("mx", [P, 2, SEQ], F32)
        sm = place("sm", [P, 2, SEQ], F32)
        ri = place("ri", [P, 2, SEQ], F32)
        mask_q8 = place("mask_q8", [P, batch], U8)
        work = at[0]
        pb = place("pb", [P, 2, BLK], F32)
        pt = place("pt", [P, 2, BLK], F32)
        at_hi = place("at_hi", [P, 2, BLK], F32R)
        at_lo = place("at_lo", [P, 2, BLK], F32R)
        rot_at = at[0]
        q2_sb = place("q2_sb", [P, 2, BLK], F32)
        k2_sb = place("k2_sb", [P, 2, BLK], F32)
        hid32 = place("hid32", [P, 2, BLK], F32)
        gate_in = place("gate_in", [P, BLK], F32)
        wa, wb = at[0], at[0] + 65536
        assert wb + 49152 <= nc.sbuf_usable_end
        hid_hi = place("hid_hi", [P, 2, BLK], F32R, rot_at)
        hid_lo = place("hid_lo", [P, 2, BLK], F32R, rot_at + 4096)
        w_hi, w_lo = [], []
        for ph, (kind, layer) in enumerate(PHASES):
            cols = UP[kind, layer] + DOWN[kind, layer]
            base = wa if kind == "attn" else wb
            w_hi.append(place(f"w_hi{ph}", [P, cols], F32R, base))
            w_lo.append(place(f"w_lo{ph}", [P, cols], F32R, base + 4 * cols))
        free = wa + 8 * 3072
        qb = place("qb", [P, DC, SEQ, 2, S], F32, free)
        kk = place("kk", [P, DC, BLK], F32, free + 8192)
        kx = place("kx", [P, DC, SEQ, 4, S], F32, free + 8192)
        vb = place("vb", [P, TILES, 2, 2 * PAIRS * HW], F32, free + 8192 + 16384)
        on = place("on", [P, SEQ, P], F32, free + 8192 + 16384 + 8704)
        rot = place("rot", [P, 2, 2, BLK], F32, rot_at)
        assert free + 8192 + 16384 + 8704 + 4096 <= wb
        free3 = wa + 8 * 2048
        mask_k8 = place("mask_k8", [P, blocks * BLK], U8, free3)
        q0_sb = place("q0_sb", [P, DC, BLK], F32, free)
        v0_sb = place("v0_sb", [P, TILES, D], F32, free + 12288)
        mask_bad = place("mask_bad", [P, blocks * BLK], U8, free3 + 4096)
        v2_sb = place("v2_sb", [P, TILES, 1024], F32, wb + 32768)
        modw = place("modw", [P, sum(MOD_COLS.values())], F32, wb)
        cond = place("cond", [P, DC, batch], F32, work)
        cond_silu = place("cond_silu", [P, DC, batch], F32, work + 512)
        t1_g = place("t1_g", [P, DC, batch], F32, work + 1024)
        t1_h = place("t1_h", [P, DC, batch], F32, work + 1536)

        psum = ctx.enter_context(nc.psum_tensor("psum", [P, 8, 512], F32))
        A_BANK, S_BANK, T_BANK, O_BANK, W_BANK = 0, 2, 4, 5, 6
        acc_a = [psum[:, A_BANK + i, :] for i in range(2)]
        scores = [psum[:, S_BANK + i, :] for i in range(2)]
        probs_tp = psum[:, T_BANK, :]
        heads = psum[:, O_BANK, :]
        wide = psum[:, W_BANK:W_BANK + 2, :]
        mlp_back = psum[:, T_BANK:T_BANK + 2, :]

        def col(name, k=0, n=1):
            o = VEC[name][0] + k
            return vec[:, o:o + n]

        ident = col("ident", 0, P)

        def by_seq(ap):
            return ap.rearrange("p (b k) -> p b k", k=S)

        def over_tokens(per_seq):
            return per_seq.unsqueeze(2).to_broadcast([per_seq.shape[0], per_seq.shape[1], S])

        def modulation(slot, c, b):
            return over_tokens(mod[:, slot + c, bass.ds(b * SEQ, SEQ)])

        def run_phases(stage_of, engine, before_loop=None):
            orders = [order_of(*key) for key in PHASES[:phases]]

            def stages(ph, offset):
                return [(s, k) for s, k, off in orders[ph] if off == offset]

            for s, k in stages(0, 1):
                stage_of(0, s, k, 0)
            for ph in range(phases):
                ending = stages(ph - 1, -1) if ph else []
                for s, k, off in ([(None, 0, -1)] if PHASES[ph][0] == "mlp" else []) + orders[ph]:
                    if off == -1:
                        for e_s, e_k in ending:
                            stage_of(ph - 1, e_s, e_k, blocks - 1)
                        ending = []
                    else:
                        stage_of(ph, s, k, off)
                if before_loop:
                    before_loop(ph)
                with engine.Fori(1, blocks - 1) as i:
                    for s, k, off in orders[ph]:
                        stage_of(ph, s, k, i + off)
                coming = stages(ph + 1, 1) if ph + 1 < phases else []
                for s, k, off in orders[ph]:
                    if off != 1:
                        stage_of(ph, s, k, blocks - 1 + off)
                    elif coming and coming[0][0] == s and s in ("stats", "norm", "turn", "split"):
                        stage_of(ph + 1, s, k, 0)
                        coming = coming[1:]
                for s, k in coming:
                    stage_of(ph + 1, s, k, 0)
            for s, k in stages(phases - 1, -1):
                stage_of(phases - 1, s, k, blocks - 1)

        def is_first(b):
            return isinstance(b, int) and b == 0

        def a_slot(ph, s, k):
            return fills_of(*PHASES[ph]).index((s, k))

        def wait_alone(eng, semaphore, value):
            eng.wait_ge(semaphore, value)
            eng.sem_inc(waits_passed, 1)

        def last_h_reader(ph, b):
            if PHASES[ph - 1 if ph and is_first(b) else ph][0] == "mlp":
                return sem["s_full1"], n_at("s_full1", ph, b, 0)
            return sem["a_full1"], n_at("a_full1", ph, b, 0)

        block = ctx.enter_context(nc.Block())

        @block.sync
        def _(sp):
            for name in NAMES:
                sp.sem_inc(sem[name], CREDIT)
            sp.dma_start(vec[:, :], vec_in).then_inc(vec_loaded, 16)
            sp.dma_start(cond[:, :, :], cond_in).then_inc(vec_loaded, 16)
            o = 0
            for i, (name, cols) in enumerate(MOD_COLS.items()):
                sp.dma_start(modw[:, o:o + cols], modw_in[:, o:o + cols]).then_inc(modw_loaded[i], 16)
                o += cols
            sp.dma_start(xres[:, :, :], x_in.rearrange("t p d -> p t d")).then_inc(x_loaded, 16)
            sp.dma_start(mask_q8[:, :], mask_q_in).then_inc(mask_loaded, 16)
            for ph in range(phases):
                cols = (UP[PHASES[ph]] + DOWN[PHASES[ph]]) // blocks
                parts = -(-cols // 1024)
                part = cols // parts
                if ph == 6:
                    sp.wait_ge(sem["x_done"], n_at("x_done", 5, 0, 1))
                    sp.dma_start(mask_k8[:, :], mask_k_in.partition_broadcast(P)).then_inc(mask_loaded, 16)
                done = sum((UP[PHASES[q]] + DOWN[PHASES[q]]) // part_of(q, blocks) for q in range(ph))
                for i in range(blocks * parts):
                    n = done + i
                    if n >= 1:
                        sp.wait_ge(w_ready, n)
                    sp.dma_start(stage[:, 0:part], weights_in[ph][:, i * part:(i + 1) * part]).then_inc(w_staged, 16)
            last = phases - 1
            with sp.Fori(0, blocks) as b:
                sp.wait_ge(sem["x_done"], n_at("x_done", last, b, 1 + 1))
                sp.dma_start(out.rearrange("t p d -> p t d")[:, bass.ds(b * TILES, TILES), :],
                             xres[:, bass.ds(b * TILES, TILES), :]).then_inc(stored, 16)
            sp.wait_ge(stored, 16 * blocks)

        @block.tensor
        def _(pe):
            pe.wait_ge(vec_loaded, 32)
            woff = {}
            o = 0
            for name, cols in MOD_COLS.items():
                woff[name] = o
                o += cols

            def mod_product(name, rhs, banks):
                n_out = MOD_COLS[name] // DC // P
                for m in range(n_out):
                    dst = psum[:, banks + m // 8, (m % 8) * batch:(m % 8) * batch + batch]
                    for kc in range(DC):
                        w = woff[name] + kc * (MOD_COLS[name] // DC) + m * P
                        ins = nc.tensor.matmul(dst, modw[:, w:w + P], rhs[:, kc, :], start=kc == 0, stop=kc == DC - 1)
                ins.then_inc(mod_mm, 1)

            pe.wait_ge(modw_loaded[0], 16)
            mod_product("film", cond, 0)
            pe.wait_ge(modw_loaded[1], 16)
            mod_product("t1", cond, 1)
            pe.wait_ge(mod_act, 1)
            pe.wait_ge(modw_loaded[2], 16)
            mod_product("mod2", cond_silu, 3)
            pe.wait_ge(modw_loaded[3], 16)
            mod_product("mod3", cond_silu, 5)
            pe.wait_ge(mod_dve, 1)
            pe.wait_ge(modw_loaded[4], 16)
            mod_product("t2", t1_h, 2)

            def weight(ph, part, kc, o, n=P):
                key = PHASES[ph]
                if part == "up":
                    c = kc * (UP[key] // DC) + o
                else:
                    c = UP[key] + kc * D + o
                return w_hi[ph][:, c:c + n], w_lo[ph][:, c:c + n]

            def project(dst, pairs, start=True, stop=True):
                for j, ((s_hi, s_lo), (m_hi, m_lo)) in enumerate(pairs):
                    nc.tensor.matmul(dst, s_lo, m_hi, start=start and j == 0, stop=False)
                    nc.tensor.matmul(dst, s_hi, m_lo, start=False, stop=False)
                    ins = nc.tensor.matmul(dst, s_hi, m_hi, start=False, stop=stop and j == len(pairs) - 1)
                return ins

            def fill_a(ph, b, n):
                pe.wait_ge(sem[f"a_free{n % 2}"], n_at(f"a_free{n % 2}", ph, b, n // 2))
                return acc_a[n % 2]

            def up_rows(ph, b, n, o):
                ins = project(fill_a(ph, b, n), [(weight(ph, "up", kc, o), (h_hi[:, kc, :], h_lo[:, kc, :]))
                                                 for kc in range(DC)])
                ins.then_inc(sem[f"a_full{n % 2}"], 1)

            def stage_of(ph, s, k, b):
                kind, layer = PHASES[ph]
                c, j, slot = k // 4, k % 4, k % 2
                if is_first(b) and (s, k) in (("q", 0), ("up", 0)):
                    pe.wait_ge(w_ready, sum((UP[PHASES[q]] + DOWN[PHASES[q]]) // part_of(q, blocks) for q in range(ph + 1)))
                if is_first(b) and (s, k) in (("probs_t", 0), ("down", 0)):
                    pe.wait_ge(sem["x_done"], n_at("x_done", ph, 0, 1))
                if s == "turn":
                    pe.wait_ge(sem["normed"], n_at("normed", ph, b, 1))
                    for m in range(DC):
                        dst = fill_a(ph, b, m)
                        for t in range(TILES):
                            ins = nc.tensor.transpose(dst[:, t * P:(t + 1) * P], xn[:, t, m * P:(m + 1) * P], ident)
                        ins.then_inc(sem[f"a_full{m}"], 1)
                elif s in ("q", "k") and kind == "attn":
                    n = a_slot(ph, s, k)
                    pe.wait_ge(sem["h"], n_at("h", ph, b, 2))
                    width = 1024 if layer == 2 else D
                    up_rows(ph, b, n, (0 if s == "q" else width) + k * P)
                    if layer == 1:
                        up_rows(ph, b, n + 1, (768 if s == "q" else 1024) + k * P)
                elif s == "v":
                    n = a_slot(ph, s, k)
                    pe.wait_ge(sem["h"], n_at("h", ph, b, 2))
                    dst = fill_a(ph, b, n)
                    if layer == 2:
                        t = k // 2
                        cols = slice(t * P, (t + 1) * P)
                        ins = project(dst, [((h_hi[:, kc, cols], h_lo[:, kc, cols]),
                                             weight(ph, "up", kc, 2048 + 512 * (k % 2), 512)) for kc in range(DC)])
                    else:
                        for u in range(2):
                            cols = slice((2 * k + u) * P, (2 * k + u + 1) * P)
                            ins = project(dst[:, u * D:(u + 1) * D],
                                          [((h_hi[:, kc, cols], h_lo[:, kc, cols]), weight(ph, "up", kc, 2 * D, D))
                                           for kc in range(DC)])
                    ins.then_inc(sem[f"a_full{n % 2}"], 1)
                elif s == "scores":
                    pe.wait_ge(sem[f"s_free{slot}"], n_at(f"s_free{slot}", ph, b, k // 2))
                    dst = scores[slot]
                    if layer == 0:
                        pe.wait_ge(sem["q"], n_at("q", ph, b, 2))
                        pe.wait_ge(sem["k"], n_at("k", ph, b, 2))
                        for g in range(SEQ):
                            tok = slice(g * S, (g + 1) * S)
                            half = slice((g % 2) * S, (g % 2) * S + S)
                            for kc in range(DC):
                                ins = nc.tensor.matmul(dst[half, (g // 2) * S:(g // 2 + 1) * S], q0_sb[:, kc, tok],
                                                       kk[:, kc, tok], start=kc == 0, stop=kc == DC - 1)
                    elif layer == 2:
                        pe.wait_ge(sem["q"], n_at("q", ph, b, k + 1))
                        wait_alone(pe, sem["k"], n_at("k", ph, b, k + 1))
                        for g in range(SEQ):
                            tok = slice(g * S, (g + 1) * S)
                            for hd in range(2):
                                rows = slice(hd * S, (hd + 1) * S)
                                ins = nc.tensor.matmul(dst[rows, tok], q2_sb[rows, slot, tok], k2_sb[rows, slot, tok],
                                                       start=True, stop=True)
                    else:
                        pe.wait_ge(sem["q"], n_at("q", ph, b, 2 * (c + 1)))
                        pe.wait_ge(sem["k"], n_at("k", ph, b, 4 * (c + 1)))
                        for g in range(2):
                            ins = nc.tensor.matmul(dst.rearrange("p (r g k) -> p r g k", g=2, k=S)[:, :, g, :],
                                                   qb[:, c, 2 * j + g, :, :].rearrange("p h q -> p (h q)"),
                                                   kx[:, c, 2 * j + g, :, :], start=True, stop=True)
                    ins.then_inc(sem[f"s_full{slot}"], 1)
                elif s == "probs_t":
                    ready = "even" if layer in (0, 2) else "probs"
                    pe.wait_ge(sem[ready], n_at(ready, ph, b, k + 1))
                    pe.wait_ge(sem["probs_t"], n_at("probs_t", ph, b, k))
                    for t in range(TILES):
                        ins = nc.tensor.transpose(probs_tp[:, t * P:(t + 1) * P], pb[:, slot, t * P:(t + 1) * P], ident)
                    ins.then_inc(sem["t_full"], 1)
                elif s == "pv" and layer == 0:
                    pe.wait_ge(sem["probs_t"], n_at("probs_t", ph, b, 1))
                    pe.wait_ge(sem["v"], n_at("v", ph, b, 2))
                    pe.wait_ge(sem["x_done"], n_at("x_done", ph, b, 1))
                    for m in range(DC):
                        for t in range(TILES):
                            ins = nc.tensor.matmul(wide[:, m, t * P:(t + 1) * P], v0_sb[:, t, m * P:(m + 1) * P],
                                                   pt[:, 0, t * P:(t + 1) * P], start=True, stop=True)
                    ins.then_inc(sem["w_full"], 1)
                elif s == "pv" and layer in (1, 3):
                    pe.wait_ge(sem["probs_t"], n_at("probs_t", ph, b, k + 1))
                    pe.wait_ge(sem["v"], n_at("v", ph, b, 4))
                    if slot == 0:
                        pe.wait_ge(sem["o_free"], n_at("o_free", ph, b, k // 2))
                    dst = heads[:, slot * 2 * 4 * HW:(slot + 1) * 2 * 4 * HW].rearrange("p (g r w) -> p g r w", g=2, w=HW)
                    for r in range(4):
                        for hd in range(2):
                            head = 8 * c + 2 * r + hd
                            ins = nc.tensor.matmul(dst[hd * S:(hd + 1) * S, :, r, :],
                                                   pt[:, slot, r * P + hd * S:r * P + (hd + 1) * S],
                                                   vb[:, j, :, head * HW:(head + 1) * HW], start=True, stop=True)
                    ins.then_inc(sem["o_full"], 1)
                elif s in ("pv", "pv2"):
                    g = 0 if s == "pv" else 1
                    if g == 0:
                        pe.wait_ge(sem["probs_t"], n_at("probs_t", ph, b, k + 1))
                        pe.wait_ge(sem["v"], n_at("v", ph, b, 8))
                        wait_alone(pe, sem["o_free"], n_at("o_free", ph, b, k))
                    else:
                        wait_alone(pe, sem["pv1"], n_at("pv1", ph, b, k + 1))
                    rows = slice(g * S, (g + 1) * S)
                    for t in range(TILES):
                        for hd in range(2):
                            o = t * P + g * S
                            ins = nc.tensor.matmul(heads[hd * S:(hd + 1) * S, o:o + S],
                                                   v2_sb[rows, t, (2 * k + hd) * S:(2 * k + hd + 1) * S],
                                                   pt[rows, slot, t * P + hd * S:t * P + (hd + 1) * S],
                                                   start=True, stop=True)
                    ins.then_inc(sem["pv1" if g == 0 else "o_full"], 1)
                elif s == "merge":
                    pe.wait_ge(sem["o_free"], n_at("o_free", ph, b, PAIRS // 2))
                    pe.wait_ge(sem["x_done"], n_at("x_done", ph, b, 1))
                    for g in range(SEQ):
                        ins = nc.tensor.transpose(wide[:, g // 4, (g % 4) * P:(g % 4 + 1) * P], on[:, g, :], ident)
                    ins.then_inc(sem["w_full"], 1)
                elif s == "proj" and layer == 2:
                    pe.wait_ge(sem["att"], n_at("att", ph, b, k + 1))
                    if k == 0:
                        pe.wait_ge(sem["x_done"], n_at("x_done", ph, b, 1))
                    for m in range(DC):
                        ins = project(wide[:, m, :], [(weight(ph, "down", k, m * P), (at_hi[:, slot, :], at_lo[:, slot, :]))],
                                      start=k == 0, stop=k == PAIRS - 1)
                    ins.then_inc(sem["proj"], 1)
                elif s == "proj":
                    pe.wait_ge(sem["att"], n_at("att", ph, b, 2))
                    pe.wait_ge(sem["w_free"], n_at("w_free", ph, b, 1))
                    for m in range(DC):
                        ins = project(wide[:, m, :], [(weight(ph, "down", kc, m * P), (at_hi[:, kc, :], at_lo[:, kc, :]))
                                                      for kc in range(DC)])
                    ins.then_inc(sem["w_full"], 1)
                elif s == "up":
                    pe.wait_ge(sem["h"], n_at("h", ph, b, 2))
                    if layer == 1:
                        todo = [(0, k, k), (1, k, HID + k)]
                    else:
                        todo = [(slot, k // 2, k)]
                    for sl, nth, m in todo:
                        pe.wait_ge(sem[f"s_free{sl}"], n_at(f"s_free{sl}", ph, b, nth))
                        ins = project(scores[sl], [(weight(ph, "up", kc, m * P), (h_hi[:, kc, :], h_lo[:, kc, :]))
                                                   for kc in range(DC)])
                        ins.then_inc(sem[f"s_full{sl}"], 1)
                elif s == "down":
                    pe.wait_ge(sem["hid"], n_at("hid", ph, b, k + 1))
                    if k == 0:
                        pe.wait_ge(sem["out_rows"], n_at("out_rows", ph, b, 0))
                    for m in range(DC):
                        ins = project(wide[:, m, :], [(weight(ph, "down", k, m * P), (hid_hi[:, slot, :], hid_lo[:, slot, :]))],
                                      start=k == 0, stop=k == HID - 1)
                    ins.then_inc(sem["down"], 1)
                elif s == "back":
                    pe.wait_ge(sem["out_rows"], n_at("out_rows", ph, b, 2))
                    if kind == "mlp":
                        pe.wait_ge(sem["x_done"], n_at("x_done", ph, b, 1))
                    dst = mlp_back if kind == "mlp" else wide
                    for t in range(TILES):
                        for m in range(DC):
                            o = (t % 2) * D + m * P
                            ins = nc.tensor.transpose(dst[:, t // 2, o:o + P], y[:, m, t * P:(t + 1) * P], ident)
                    ins.then_inc(sem["back" if kind == "mlp" else "w_full"], 1)

            pe.wait_ge(sem["x_done"], n_at("x_done", 0, 0, 1))
            run_phases(stage_of, pe)

        @block.scalar
        def _(act):
            act.wait_ge(vec_loaded, 32)
            nc.scalar.activation(cond_silu[:, :, :], cond[:, :, :], ACT.Silu).then_inc(mod_act, 1)
            act.wait_ge(mod_mm, 2)
            for kc in range(DC):
                nc.scalar.activation(t1_g[:, kc, :], psum[:, 1, (2 + kc) * batch:(3 + kc) * batch], ACT.Silu,
                                     bias=col("t1_b", 2 + kc)).then_inc(mod_act, 1)

            def stage_of(ph, s, k, b):
                kind, layer = PHASES[ph]
                c, j, slot = k // 4, k % 4, k % 2
                if is_first(b) and (s, k) == ("k", 0) and layer in (1, 3):
                    act.wait_ge(prepared, 4 if layer == 1 else 8)
                if s == "split":
                    for m in range(DC):
                        act.wait_ge(sem["modded"], n_at("modded", ph, b, m + 1))
                        act.wait_ge(*last_h_reader(ph, b))
                        nc.scalar.activation(h_hi[:, m, :], hm[:, m, :], ACT.Copy).then_inc(sem["h_hi"], 1)
                elif s in ("q", "k", "v") and kind == "attn":
                    n = a_slot(ph, s, k)
                    full, fre = sem[f"a_full{n % 2}"], sem[f"a_free{n % 2}"]
                    src = acc_a[n % 2]
                    if layer == 0:
                        act.wait_ge(full, n_at(f"a_full{n % 2}", ph, b, n // 2 + 1))
                        if s == "v":
                            act.wait_ge(sem["w_full"], n_at("w_full", ph, b, -2))
                            nc.scalar.activation(v0_sb[:, 2 * k:2 * k + 2, :], src.rearrange("p (t d) -> p t d", d=D),
                                                 ACT.Copy).then_inc(fre, 1)
                        else:
                            act.wait_ge(sem["s_full0"], n_at("s_full0", ph, b, 0))
                            dst = q0_sb if s == "q" else kk
                            nc.scalar.activation(dst[:, k, :], src, ACT.Identity, bias=col(f"{s}0", k)).then_inc(fre, 1)
                        act.wait_ge(fre, n_at(f"a_free{n % 2}", ph, b, n // 2 + 1))
                        act.sem_inc(sem[s], 1)
                    elif layer == 2:
                        act.wait_ge(full, n_at(f"a_full{n % 2}", ph, b, n // 2 + 1))
                        if s == "v":
                            act.wait_ge(sem["o_full"], n_at("o_full", ph, b, 0))
                            nc.scalar.activation(v2_sb[:, k // 2, 512 * (k % 2):512 * (k % 2) + 512], src,
                                                 ACT.Copy).then_inc(fre, 1)
                            act.wait_ge(fre, n_at(f"a_free{n % 2}", ph, b, n // 2 + 1))
                            act.sem_inc(sem["v"], 1)
                        else:
                            act.wait_ge(sem[f"s_full{slot}"], n_at(f"s_full{slot}", ph, b, k // 2))
                            dst = q2_sb if s == "q" else k2_sb
                            nc.scalar.activation(dst[:, slot, :], src, ACT.Copy).then_inc(sem[s], 1)
                            act.wait_ge(sem[s], n_at(s, ph, b, k + 1))
                            act.sem_inc(fre, 1)
                    elif s == "v":
                        act.wait_ge(full, n_at(f"a_full{n % 2}", ph, b, n // 2 + 1))
                        act.wait_ge(sem["o_full"], n_at("o_full", ph, b, 0))
                        for g in range(2):
                            rows = slice(g * S, (g + 1) * S)
                            dst = vb[rows, 2 * k:2 * k + 2, g, :].rearrange("p t (r w) -> p t r w", w=HW)[:, :, :, 0:HW - 1]
                            nc.scalar.activation(dst, src[rows, :].rearrange("p (t r w) -> p t r w", t=2, w=HW - 1),
                                                 ACT.Copy).then_inc(sem["v"], 1)
                        act.wait_ge(sem["v"], n_at("v", ph, b, 2 * (k + 1)))
                        act.sem_inc(fre, 1)
                    elif s == "k" and layer == 3:
                        act.wait_ge(full, n_at(f"a_full{n % 2}", ph, b, n // 2 + 1))
                        act.wait_ge(sem["s_full1"], n_at("s_full1", ph, b, -2 if k == 0 else 0))
                        for r in range(4):
                            rows = slice(32 * r, 32 * r + 32)
                            nc.scalar.activation(kx[rows, k, :, r, :], by_seq(src[rows, :]), ACT.Identity,
                                                 bias=col("k3", k)[rows, :]).then_inc(sem["k"], 1)
                        act.wait_ge(sem["k"], n_at("k", ph, b, 4 * (k + 1)))
                        act.sem_inc(fre, 1)
                    elif s == "k":
                        act.wait_ge(sem["k32"], n_at("k32", ph, b, k + 1))
                        act.wait_ge(sem["s_full1"], n_at("s_full1", ph, b, -2 if k == 0 else 0))
                        for r in range(4):
                            rows = slice(32 * r, 32 * r + 32)
                            nc.scalar.activation(kx[rows, k, :, r, :], by_seq(rot[rows, 1, 0, :]),
                                                 ACT.Copy).then_inc(sem["k"], 1)
                    elif s == "q":
                        act.wait_ge(sem["q32"], n_at("q32", ph, b, k + 1))
                        act.wait_ge(sem["s_full1"], n_at("s_full1", ph, b, -2 if k == 0 else 0))
                        for hd, parity in enumerate(("even", "odd")):
                            nc.scalar.activation(qb[:, k, :, hd, :], by_seq(rot[:, 0, 0, :]), ACT.Copy,
                                                 scale=col(parity)).then_inc(sem["q"], 1)
                elif s == "scores":
                    if layer == 0:
                        act.wait_ge(sem["shifted"], n_at("shifted", ph, b, 2))
                        for g in range(2):
                            rows = slice(g * S, (g + 1) * S)
                            ap = pb[rows, 0, :].rearrange("p (t g k) -> p t g k", g=2, k=S)[:, :, g, :]
                            ins = nc.scalar.activation(ap, ap, ACT.Exp, scale=SCORE_SCALE[0])
                            if g == 1:
                                ins.then_inc(sem["probs"], 1)
                    else:
                        act.wait_ge(sem["shifted"], n_at("shifted", ph, b, k + 1))
                        nc.scalar.activation(pb[:, slot, :], pb[:, slot, :], ACT.Exp,
                                             scale=SCORE_SCALE[layer]).then_inc(sem["probs"], 1)
                elif s == "probs_t":
                    act.wait_ge(sem["t_full"], n_at("t_full", ph, b, k + 1))
                    if layer == 0:
                        act.wait_ge(sem["w_full"], n_at("w_full", ph, b, -2))
                    else:
                        act.wait_ge(sem["o_full"], n_at("o_full", ph, b, k - 1))
                    nc.scalar.activation(pt[:, slot, :], probs_tp, ACT.Copy).then_inc(sem["probs_t"], 1)
                elif s in ("pv", "merge") and (layer == 0 or s == "merge"):
                    act.wait_ge(sem["w_full"], n_at("w_full", ph, b, 1))
                    for m in range(DC):
                        if layer == 0:
                            src = wide[:, m, :]
                            dst = at_hi[:, m, :]
                        else:
                            src = wide.rearrange("p w (g h q) -> p (w g) h q", h=2, q=S)[:, :, m, :]
                            dst = by_seq(at_hi[:, m, :])
                        nc.scalar.activation(dst, src, ACT.Identity, bias=col(f"v{layer}", m)).then_inc(sem["att_hi"], 1)
                elif s == "pv2":
                    act.wait_ge(sem["o_full"], n_at("o_full", ph, b, k + 1))
                    act.wait_ge(sem["proj"], n_at("proj", ph, b, k - 1))
                    nc.scalar.activation(at_hi[:, slot, :], heads, ACT.Copy).then_inc(sem["att_hi"], 1)
                elif s == "proj" and layer in (0, 1):
                    act.wait_ge(sem["w_full"], n_at("w_full", ph, b, 2))
                    for m in range(DC):
                        nc.scalar.activation(y[:, m, :], wide[:, m, :], ACT.Identity,
                                             bias=col(f"o{layer}", m)).then_inc(sem["out_rows"], 1)
                elif s == "up":
                    if layer == 1:
                        act.wait_ge(sem["s_full1"], n_at("s_full1", ph, b, k + 1))
                        act.wait_ge(sem["hid32"], n_at("hid32", ph, b, k))
                        nc.scalar.activation(gate_in[:, :], scores[1], ACT.Silu, bias=col("u1", HID + k)).then_inc(sem["gate_in"], 1)
                        act.wait_ge(sem["gate_in"], n_at("gate_in", ph, b, k + 1))
                        act.sem_inc(sem["s_free1"], 1)
                    else:
                        func = ACT.Gelu_apprx_tanh if layer == 3 else ACT.Gelu
                        act.wait_ge(sem[f"s_full{slot}"], n_at(f"s_full{slot}", ph, b, k // 2 + 1))
                        act.wait_ge(sem["hid"], n_at("hid", ph, b, k - 1))
                        nc.scalar.activation(hid32[:, slot, :], scores[slot], func, bias=col(f"u{layer}", k)).then_inc(sem["hid32"], 1)
                    act.wait_ge(sem["hid32"], n_at("hid32", ph, b, k + 1))
                    if layer != 1:
                        act.sem_inc(sem[f"s_free{slot}"], 1)
                    act.wait_ge(sem["down"], n_at("down", ph, b, k - 1))
                    nc.scalar.activation(hid_hi[:, slot, :], hid32[:, slot, :], ACT.Copy).then_inc(sem["hid_hi"], 1)
                elif s == "down" and k == HID - 1 and layer in (0, 1):
                    act.wait_ge(sem["down"], n_at("down", ph, b, HID))
                    act.wait_ge(sem["back"], n_at("back", ph, b, 0))
                    for m in range(DC):
                        nc.scalar.activation(y[:, m, :], wide[:, m, :], ACT.Identity,
                                             bias=col(f"d{layer}", m)).then_inc(sem["out_rows"], 1)

            act.wait_ge(sem["x_done"], n_at("x_done", 0, 0, 1))
            run_phases(stage_of, act)

        @block.vector
        def _(dve):
            dve.wait_ge(vec_loaded, 32)

            def mod_bias(slots, first, n):
                nc.vector.tensor_tensor(mod[:, first:first + n, :],
                                        slots.rearrange("p (n b) -> p n b", b=batch)[:, 0:n, :],
                                        col("mod_b", first, n).unsqueeze(2).to_broadcast([P, n, batch]),
                                        ALU.add).then_inc(mod_dve, 1)

            def mod_scale(slot, norm):
                for c in range(DC):
                    ap = mod[:, slot + c, :]
                    if norm is None:
                        nc.vector.tensor_scalar(ap, ap, 1.0, None, ALU.add).then_inc(consts_ready, 1)
                    else:
                        nc.vector.tensor_scalar(ap, ap, 1.0, col("norm", norm + c), ALU.add, ALU.mult).then_inc(consts_ready, 1)

            dve.wait_ge(mod_act, 3)
            for kc in range(DC):
                nc.vector.scalar_tensor_tensor(t1_h[:, kc, :], psum[:, 1, kc * batch:(kc + 1) * batch], col("t1_b", kc),
                                               t1_g[:, kc, :], ALU.add, ALU.mult).then_inc(consts_ready, 1)
            dve.wait_ge(consts_ready, 2)
            dve.sem_inc(mod_dve, 1)
            full = 8 * batch
            dve.wait_ge(mod_mm, 5)
            mod_bias(psum[:, 0, 0:full], 0, 8)
            mod_bias(psum[:, 2, 0:full], 8, 8)
            mod_bias(psum[:, 3, 0:full], 16, 8)
            mod_bias(psum[:, 4, 0:full], 24, 4)
            mod_bias(psum[:, 5, 0:full], 28, 8)
            mod_bias(psum[:, 6, 0:full], 36, 4)
            for layer in range(4):
                nc.vector.memset(eps_t[:, layer, :], EPS[layer]).then_inc(mod_dve, 1)
            nc.vector.memset(half_t[:, :], -0.5).then_inc(mod_dve, 1)
            dve.wait_ge(mask_loaded, 16)
            dve.wait_ge(x_loaded, 16)
            nc.vector.memset(pb[:, :, :], 0.0).then_inc(mod_dve, 1)
            dve.wait_ge(mod_dve, 1 + 6 + 5 + 1)
            for ph, norm in ((0, 0), (1, 2), (2, 4), (3, 6), (4, None), (5, None), (6, None), (7, None)):
                mod_scale(MOD[PHASES[ph]][0], norm)
            dve.wait_ge(consts_ready, 2 + 16)
            dve.sem_inc(sem["x_done"], 1)

            def stage_of(ph, s, k, b):
                kind, layer = PHASES[ph]
                c, j, slot = k // 4, k % 4, k % 2
                scale, shift, gate = MOD[PHASES[ph]]
                if s == "share" and PHASES[ph] == ("mlp", 2) and isinstance(b, int) and b == blocks - 1:
                    dve.wait_ge(mask_loaded, 32)
                    nc.vector.tensor_tensor(by_seq(mask_bad[:, :]), over_tokens(mask_q8[:, :]), by_seq(mask_k8[:, :]),
                                            ALU.is_gt).then_inc(mask_made, 1)
                    dve.wait_ge(mask_made, 1)
                elif s == "stats":
                    if ph and isinstance(b, int) and b < 2:
                        dve.wait_ge(sem["x_done"], n_at("x_done", ph - 1, b + 1, 1))
                    for t in range(TILES):
                        ins = nc.vector.bn_stats(st[:, t, :], xres[:, b * TILES + t, :])
                    ins.then_inc(sem["stats_raw"], 1)
                    wait_alone(dve, sem["stats_raw"], n_at("stats_raw", ph, b, 1))
                    for t in range(TILES):
                        ins = nc.vector.bn_aggr(mv[:, t, :], st[:, t, :])
                    ins.then_inc(sem["stats"], 1)
                    dve.wait_ge(sem["stats"], n_at("stats", ph, b, 1))
                    if layer < 2:
                        nc.vector.tensor_tensor(ms[:, :], mv[:, :, 0], mv[:, :, 0], ALU.mult).then_inc(sem["mean_sq"], 1)
                        dve.wait_ge(sem["mean_sq"], n_at("mean_sq", ph, b, 1))
                        nc.vector.tensor_tensor(ms[:, :], ms[:, :], mv[:, :, 1], ALU.add).then_inc(sem["rstd_in"], 1)
                    else:
                        nc.vector.tensor_copy(ms[:, :], mv[:, :, 1]).then_inc(sem["rstd_in"], 1)
                elif s == "norm":
                    dve.wait_ge(sem["rstd"], n_at("rstd", ph, b, 1))
                    for t in range(TILES):
                        if layer < 2:
                            ins = nc.vector.tensor_scalar(xn[:, t, :], xres[:, b * TILES + t, :], rstd[:, t:t + 1], None, ALU.mult)
                        else:
                            ins = nc.vector.tensor_scalar(xn[:, t, :], xres[:, b * TILES + t, :], mv[:, t, 0:1],
                                                          rstd[:, t:t + 1], ALU.subtract, ALU.mult)
                    ins.then_inc(sem["normed"], 1)
                elif s == "turn":
                    for m in range(DC):
                        n = n_at(f"a_full{m}", ph, b, 1)
                        dve.wait_ge(sem[f"a_full{m}"], n)
                        nc.vector.tensor_tensor(by_seq(hm[:, m, :]), by_seq(acc_a[m]), modulation(scale, m, b),
                                                ALU.mult).then_inc(sem[f"a_free{m}"], 1)
                    for m in range(DC):
                        dve.wait_ge(sem[f"a_free{m}"], n_at(f"a_free{m}", ph, b, 1))
                        nc.vector.tensor_tensor(by_seq(hm[:, m, :]), by_seq(hm[:, m, :]), modulation(shift, m, b),
                                                ALU.add).then_inc(sem["modded"], 1)
                elif s == "split":
                    for m in range(DC):
                        dve.wait_ge(sem["h_hi"], n_at("h_hi", ph, b, m + 1))
                        nc.vector.tensor_tensor(h_lo[:, m, :], hm[:, m, :], h_hi[:, m, :].bitcast(F32),
                                                ALU.subtract).then_inc(sem["h"], 1)
                elif s in ("q", "k") and layer == 1:
                    n = a_slot(ph, s, k)
                    which = 0 if s == "q" else 1
                    nth = 2 * k + which + 1
                    if s == "q":
                        dve.wait_ge(sem["q"], n_at("q", ph, b, 2 * k))
                    else:
                        dve.wait_ge(sem["k"], n_at("k", ph, b, 4 * k))
                    for u, (bias, tab, cnt) in enumerate(((f"{s}1", "cos", "rot_a"), (f"{s}s1", "sin", "rot_b"))):
                        dve.wait_ge(sem[f"a_full{u}"], n_at(f"a_full{u}", ph, b, n // 2 + 1))
                        nc.vector.scalar_tensor_tensor(by_seq(rot[:, which, u, :]), by_seq(acc_a[u]), col(bias, k),
                                                       col(tab, 0, S).unsqueeze(1).to_broadcast([P, SEQ, S]),
                                                       ALU.add, ALU.mult).then_inc(sem[cnt], 1)
                        dve.wait_ge(sem[cnt], n_at(cnt, ph, b, nth))
                        dve.sem_inc(sem[f"a_free{u}"], 1)
                elif s == "q" and layer == 3:
                    n = a_slot(ph, s, k)
                    dve.wait_ge(sem[f"a_full{n % 2}"], n_at(f"a_full{n % 2}", ph, b, n // 2 + 1))
                    dve.wait_ge(sem["q"], n_at("q", ph, b, 2 * k))
                    nc.vector.scalar_tensor_tensor(rot[:, 0, 0, :], acc_a[n % 2], col("q3", k), mask_k8[:, bass.ds(b * BLK, BLK)],
                                                   ALU.add, ALU.mult).then_inc(sem["q32"], 1)
                    dve.wait_ge(sem["q32"], n_at("q32", ph, b, k + 1))
                    dve.sem_inc(sem[f"a_free{n % 2}"], 1)
                elif s == "scores" and layer == 0:
                    dve.wait_ge(sem["s_full0"], n_at("s_full0", ph, b, 1))
                    sc = scores[0][:, 0:TILES * S].rearrange("p (t k) -> p t k", k=S)
                    nc.vector.tensor_reduce(mx[:, 0, 0:TILES], sc, AX.X, ALU.max).then_inc(sem["row_max"], 1)
                    dve.wait_ge(sem["row_max"], n_at("row_max", ph, b, 1))
                    dve.wait_ge(sem["t_full"], n_at("t_full", ph, b, 0))
                    for g in range(2):
                        rows = slice(g * S, (g + 1) * S)
                        ap = pb[rows, 0, :].rearrange("p (t g k) -> p t g k", g=2, k=S)[:, :, g, :]
                        nc.vector.tensor_tensor(ap, sc[rows], over_tokens(mx[rows, 0, 0:TILES]),
                                                ALU.subtract).then_inc(sem["shifted"], 1)
                    dve.wait_ge(sem["shifted"], n_at("shifted", ph, b, 2))
                    dve.sem_inc(sem["s_free0"], 1)
                elif s == "scores":
                    sc = by_seq(scores[slot])
                    dst = by_seq(pb[:, slot, :])
                    dve.wait_ge(sem[f"s_full{slot}"], n_at(f"s_full{slot}", ph, b, k // 2 + 1))
                    dve.wait_ge(sem["t_full"], n_at("t_full", ph, b, k - 1))
                    if layer == 3:
                        nc.vector.scalar_tensor_tensor(pb[:, slot, :].rearrange("p (r w) -> p r w", w=P),
                                                       mask_bad[:, bass.ds(b * BLK + j * P, P)].unsqueeze(1).to_broadcast([P, 4, P]),
                                                       -MASKED, scores[slot].rearrange("p (r w) -> p r w", w=P),
                                                       ALU.mult, ALU.add).then_inc(sem["masked"], 1)
                        dve.wait_ge(sem["masked"], n_at("masked", ph, b, k + 1))
                        dve.sem_inc(sem[f"s_free{slot}"], 1)
                        sc = dst
                    nc.vector.tensor_reduce(mx[:, slot, :], sc, AX.X, ALU.max).then_inc(sem["row_max"], 1)
                    dve.wait_ge(sem["row_max"], n_at("row_max", ph, b, k + 1))
                    nc.vector.tensor_tensor(dst, sc, over_tokens(mx[:, slot, :]), ALU.subtract).then_inc(sem["shifted"], 1)
                    if layer != 3:
                        dve.wait_ge(sem["shifted"], n_at("shifted", ph, b, k + 1))
                        dve.sem_inc(sem[f"s_free{slot}"], 1)
                elif s == "even_out":
                    dve.wait_ge(sem["probs"], n_at("probs", ph, b, k + 1))
                    if layer == 0:
                        src, n = pb[:, 0, :].rearrange("p (t k) -> p t k", k=P), TILES
                    else:
                        src, n = by_seq(pb[:, slot, :]), SEQ
                    nc.vector.tensor_reduce(sm[:, slot, 0:n], src, AX.X, ALU.add).then_inc(sem["row_sum"], 1)
                    dve.wait_ge(sem["row_sum"], n_at("row_sum", ph, b, k + 1))
                    dve.wait_ge(sem["even"], n_at("even", ph, b, k - 1))
                    nc.vector.reciprocal(ri[:, slot, 0:n], sm[:, slot, 0:n]).then_inc(sem["row_inv"], 1)
                elif s == "pv" and layer in (1, 3):
                    if slot == 0:
                        return
                    dve.wait_ge(sem["o_full"], n_at("o_full", ph, b, k + 1))
                    o4 = heads[:, 0:2 * SEQ * HW].rearrange("p (g r w) -> p g r w", g=4, w=HW)
                    inv = ri[:, :, :].rearrange("p a (b r) -> p (a b) r", r=4)
                    nc.vector.reciprocal(inv, o4[:, :, :, HW - 1]).then_inc(sem["o_inv"], 1)
                    dve.wait_ge(sem["o_inv"], n_at("o_inv", ph, b, k // 2 + 1))
                    if k == 1:
                        dve.wait_ge(sem["w_full"], n_at("w_full", ph, b, -2))
                    u = (k // 2) % 2
                    nc.vector.tensor_tensor(on[:, 4 * u:4 * u + 4, c * S:(c + 1) * S].rearrange("p g (r w) -> p g r w", r=4),
                                            o4[:, :, :, 0:HW - 1], inv.unsqueeze(3).to_broadcast([P, 4, 4, 16]),
                                            ALU.mult).then_inc(sem["o_free"], 1)
                elif (s == "pv" and layer == 0) or s == "merge":
                    for m in range(DC):
                        if layer == 0:
                            src, hi, lo = wide[:, m, :], at_hi[:, m, :], at_lo[:, m, :]
                        else:
                            src = wide.rearrange("p w (g h q) -> p (w g) h q", h=2, q=S)[:, :, m, :]
                            hi, lo = by_seq(at_hi[:, m, :]), by_seq(at_lo[:, m, :])
                        dve.wait_ge(sem["att_hi"], n_at("att_hi", ph, b, m + 1 if layer == 0 else 2))
                        nc.vector.scalar_tensor_tensor(lo, src, col(f"v{layer}", m), hi.bitcast(F32), ALU.add,
                                                       ALU.subtract).then_inc(sem["att"], 1)
                    dve.wait_ge(sem["att"], n_at("att", ph, b, 2))
                    dve.sem_inc(sem["w_free"], 1)
                elif s == "pv2":
                    dve.wait_ge(sem["att_hi"], n_at("att_hi", ph, b, k + 1))
                    nc.vector.tensor_tensor(at_lo[:, slot, :], heads, at_hi[:, slot, :].bitcast(F32),
                                            ALU.subtract).then_inc(sem["att"], 1)
                    dve.wait_ge(sem["att"], n_at("att", ph, b, k + 1))
                    dve.sem_inc(sem["o_free"], 1)
                elif s == "up":
                    if layer == 1:
                        dve.wait_ge(sem["s_full0"], n_at("s_full0", ph, b, k + 1))
                        dve.wait_ge(sem["gate_in"], n_at("gate_in", ph, b, k + 1))
                        dve.wait_ge(sem["hid"], n_at("hid", ph, b, k - 1))
                        nc.vector.scalar_tensor_tensor(hid32[:, slot, :], scores[0], col("u1", k), gate_in[:, :],
                                                       ALU.add, ALU.mult).then_inc(sem["hid32"], 1)
                        dve.wait_ge(sem["hid32"], n_at("hid32", ph, b, k + 1))
                        dve.sem_inc(sem["s_free0"], 1)
                    dve.wait_ge(sem["hid_hi"], n_at("hid_hi", ph, b, k + 1))
                    nc.vector.tensor_tensor(hid_lo[:, slot, :], hid32[:, slot, :], hid_hi[:, slot, :].bitcast(F32),
                                            ALU.subtract).then_inc(sem["hid"], 1)
                elif gate is not None and ((s == "proj" and (layer == 3 or k == PAIRS - 1)) or (s == "down" and k == HID - 1)):
                    if kind == "mlp":
                        dve.wait_ge(sem["down"], n_at("down", ph, b, HID))
                        dve.wait_ge(sem["back"], n_at("back", ph, b, 0))
                    elif layer == 3:
                        dve.wait_ge(sem["w_full"], n_at("w_full", ph, b, 2))
                    else:
                        dve.wait_ge(sem["proj"], n_at("proj", ph, b, PAIRS))
                    bias = ("d" if kind == "mlp" else "o") + str(layer)
                    for m in range(DC):
                        nc.vector.scalar_tensor_tensor(by_seq(y[:, m, :]), by_seq(wide[:, m, :]), col(bias, m),
                                                       modulation(gate, m, b), ALU.add, ALU.mult).then_inc(sem["out_rows"], 1)
                elif s == "back":
                    if kind == "mlp":
                        dve.wait_ge(sem["back"], n_at("back", ph, b, 1))
                        src = mlp_back
                    else:
                        last = 3 if layer != 2 else 1
                        dve.wait_ge(sem["w_full"], n_at("w_full", ph, b, last))
                        src = wide
                    xs = xres[:, bass.ds(b * TILES, TILES), :].rearrange("p (w t) d -> p w (t d)", w=2)
                    nc.vector.tensor_tensor(xs, xs, src, ALU.add).then_inc(sem["x_done"], 1)

            dve.wait_ge(sem["x_done"], n_at("x_done", 0, 0, 1))
            run_phases(stage_of, dve, lambda ph: dve.wait_ge(sem["x_done"], n_at("x_done", ph, 0, 1)))

        @block.gpsimd
        def _(pool):
            shares = [0]

            def split_static(ph, i, part):
                shares[0] += 1
                pool.wait_ge(w_staged, 16 * shares[0])
                nc.gpsimd.tensor_copy(w_hi[ph][:, i * part:(i + 1) * part], stage[:, 0:part]).then_inc(w_hi_done, 1)
                pool.wait_ge(w_hi_done, shares[0])
                nc.gpsimd.tensor_tensor(w_lo[ph][:, i * part:(i + 1) * part], stage[:, 0:part],
                                        w_hi[ph][:, i * part:(i + 1) * part].bitcast(F32), ALU.subtract).then_inc(w_ready, 1)

            def split_next(ph, b):
                if ph + 1 >= phases:
                    return
                nxt = ph + 1
                cols = (UP[PHASES[nxt]] + DOWN[PHASES[nxt]]) // blocks
                parts = -(-cols // 1024)
                part = cols // parts
                done = sum((UP[PHASES[q]] + DOWN[PHASES[q]]) // part_of(q, blocks) for q in range(nxt))
                for u in range(parts):
                    n = b * parts + (done + u + 1)
                    where = bass.ds(b * cols + u * part, part)
                    pool.wait_ge(w_staged, n * 16)
                    nc.gpsimd.tensor_copy(w_hi[nxt][:, where], stage[:, 0:part]).then_inc(w_hi_done, 1)
                    pool.wait_ge(w_hi_done, n)
                    nc.gpsimd.tensor_tensor(w_lo[nxt][:, where], stage[:, 0:part], w_hi[nxt][:, where].bitcast(F32),
                                            ALU.subtract).then_inc(w_ready, 1)

            def prepare_attention():
                nc.gpsimd.memset(kx[:, :, :, :, :], 0.0).then_inc(prepared, 1)
                nc.gpsimd.memset(vb[:, :, :, :], 0.0).then_inc(prepared, 1)
                prepares[0] += 2
                pool.wait_ge(prepared, prepares[0])
                for g in range(2):
                    rows = slice(g * S, (g + 1) * S)
                    nc.gpsimd.memset(vb[rows, :, g, :].rearrange("p t (r w) -> p t r w", w=HW)[:, :, :, HW - 1],
                                     1.0).then_inc(prepared, 1)
                    prepares[0] += 1
                    pool.wait_ge(prepared, prepares[0])

            prepares = [0]
            part0 = part_of(0, blocks)
            for i in range((UP[PHASES[0]] + DOWN[PHASES[0]]) // part0):
                split_static(0, i, part0)

            def stage_of(ph, s, k, b):
                kind, layer = PHASES[ph]
                slot = k % 2
                if s == "stats":
                    pool.wait_ge(sem["rstd_in"], n_at("rstd_in", ph, b, 1))
                    nc.gpsimd.tensor_tensor(ms[:, :], ms[:, :], eps_t[:, layer, :], ALU.add).then_inc(sem["eps_added"], 1)
                    pool.wait_ge(sem["eps_added"], n_at("eps_added", ph, b, 1))
                    nc.gpsimd.tensor_tensor(rstd[:, :], ms[:, :], half_t[:, :], ALU.pow).then_inc(sem["rstd"], 1)
                elif s in ("q", "k") and layer == 1:
                    which = 0 if s == "q" else 1
                    pool.wait_ge(sem["rot_b"], n_at("rot_b", ph, b, 2 * k + which + 1))
                    if s == "q":
                        nc.gpsimd.tensor_tensor(rot[:, 0, 0, :], rot[:, 0, 0, :], rot[:, 0, 1, :], ALU.add).then_inc(sem["q32"], 1)
                    else:
                        nc.gpsimd.tensor_tensor(rot[:, 1, 0, :], rot[:, 1, 0, :], rot[:, 1, 1, :], ALU.add).then_inc(sem["k32"], 1)
                elif s == "even_out":
                    pool.wait_ge(sem["row_inv"], n_at("row_inv", ph, b, k + 1))
                    if layer == 0:
                        ap = pb[:, 0, :].rearrange("p (t k) -> p t k", k=P)
                        inv = ri[:, 0, 0:TILES].unsqueeze(2).to_broadcast([P, TILES, P])
                    else:
                        ap, inv = by_seq(pb[:, slot, :]), over_tokens(ri[:, slot, :])
                    nc.gpsimd.tensor_tensor(ap, ap, inv, ALU.mult).then_inc(sem["even"], 1)
                elif s == "share":
                    if is_first(b):
                        pool.wait_ge(sem["x_done"], n_at("x_done", ph, 0, 1))
                        if PHASES[ph + 1:ph + 2] in ([("attn", 1)], [("attn", 3)]):
                            prepare_attention()
                    split_next(ph, b)

            run_phases(stage_of, pool)


def part_of(ph, blocks):
    cols = (UP[PHASES[ph]] + DOWN[PHASES[ph]]) // blocks
    return cols // -(-cols // 1024)


def rows_first(w):
    return w.reshape(-1, P, w.shape[1]).transpose(1, 0, 2)


def lay_out(i):
    x = np.ascontiguousarray(i["x"])
    batch = x.shape[0]
    cond = np.ascontiguousarray(rows_first(np.ascontiguousarray(i["cond_1024"].T)))
    mask = np.ascontiguousarray(i["mask_BxS_bk1"])
    swap = np.arange(D).reshape(-1, 2)[:, ::-1].reshape(-1)
    heads = np.arange(D).reshape(8, 2, 16).transpose(1, 0, 2).reshape(-1)

    def weights(up, down):
        return np.concatenate([rows_first(up).reshape(P, -1), rows_first(down).reshape(P, -1)], axis=1)

    q1, k1, v1 = (i["L1_cond_w_qkv"][:, n * D:(n + 1) * D] for n in range(3))
    w = [
        weights(np.concatenate([i["L0_cond_q_w"], i["L0_cond_k_w"], i["L0_cond_v_w"]], 1), i["L0_cond_proj_w"]),
        weights(i["L0_cond_mlp_w1"], i["L0_cond_mlp_w2"]),
        weights(np.concatenate([q1, k1, v1, q1[:, swap], k1[:, swap]], 1), i["L1_cond_w_ao"][heads]),
        weights(i["L1_cond_w_fc"], i["L1_cond_w_fo"]),
        weights(i["L2_cond_W_qkv"], i["L2_cond_W_out"]),
        weights(i["L2_cond_W1"], i["L2_cond_W2"]),
        weights(i["L3_cond_qkv_w"].T, i["L3_cond_proj_w"].T[heads]),
        weights(i["L3_cond_fc1_w"].T, i["L3_cond_fc2_w"].T),
    ]
    modw = np.concatenate([rows_first(m).reshape(P, -1) for m in (
        np.concatenate([i["L0_cond_film1_w"], i["L0_cond_film2_w"]], 1), i["L1_cond_w_t1"], i["L2_cond_W_mod"],
        i["L3_cond_ada_w"].T, i["L1_cond_w_t2"])], axis=1)

    def cols(v):
        return v.reshape(-1, P).T

    bq1, bk1, bv1 = (i["L1_cond_b_qkv"][n * D:(n + 1) * D] for n in range(3))
    bq3, bk3, bv3 = (i["L3_cond_qkv_b"][n * D:(n + 1) * D] for n in range(3))
    pair = (np.arange(P) % 16) // 2
    freq = (1.0 / np.float32(10000.0) ** (np.arange(0, 16, 2, dtype=np.float32) / np.float32(16))).astype(np.float32)
    angle = np.arange(S, dtype=np.float32)[None, :] * freq[pair][:, None]
    sign = np.where(np.arange(P) % 2 == 0, -1, 1).astype(np.float32)[:, None]
    parity = ((np.arange(P) // 16) % 2).astype(np.float32)[:, None]
    vec = {
        "mod_b": np.concatenate([cols(i[n]) for n in ("L0_cond_film1_b", "L0_cond_film2_b", "L1_cond_b_t2",
                                                      "L2_cond_b_mod", "L3_cond_ada_b")], 1),
        "t1_b": cols(i["L1_cond_b_t1"]),
        "norm": np.concatenate([cols(i[n]) for n in ("L0_cond_norm1_w", "L0_cond_norm2_w", "L1_cond_g1", "L1_cond_g2")], 1),
        "q0": cols(i["L0_cond_q_b"]), "k0": cols(i["L0_cond_k_b"]), "v0": cols(i["L0_cond_v_b"]),
        "o0": cols(i["L0_cond_proj_b"]), "u0": cols(i["L0_cond_mlp_b1"]), "d0": cols(i["L0_cond_mlp_b2"]),
        "q1": cols(bq1), "k1": cols(bk1), "qs1": cols(bq1[swap]), "ks1": cols(bk1[swap]), "v1": cols(bv1[heads]),
        "o1": cols(i["L1_cond_b_ao"]), "u1": cols(i["L1_cond_b_fc"]), "d1": cols(i["L1_cond_b_fo"]),
        "o2": cols(i["L2_cond_b_out"]), "u2": cols(i["L2_cond_b1"]), "d2": cols(i["L2_cond_b2"]),
        "q3": cols(bq3), "k3": cols(bk3), "v3": cols(bv3[heads]), "o3": cols(i["L3_cond_proj_b"]),
        "u3": cols(i["L3_cond_fc1_b"]), "d3": cols(i["L3_cond_fc2_b"]),
        "even": 1 - parity, "odd": parity, "cos": np.cos(angle), "sin": np.sin(angle) * sign,
        "ident": np.eye(P, dtype=np.float32),
    }
    assert all(vec[n].shape == (P, VEC[n][1]) for n in VEC), {n: vec[n].shape for n in VEC}
    vecs = np.concatenate([vec[n].astype(np.float32, copy=False) for n in VEC], 1)
    arrays = {
        "x": x.reshape(-1, P, D), "cond": cond, "mask_k": mask.reshape(-1),
        "mask_q": np.concatenate([mask.T, mask.T], 0), "vec": vecs, "modw": modw,
    }
    arrays.update({f"w{n}": a for n, a in enumerate(w)})
    return {n: np.ascontiguousarray(a) for n, a in arrays.items()}, batch


def kernel(**inputs):
    import concourse.bacc as _bacc
    from concourse.bass_utils import run_bass_kernel_spmd as _run

    arrays, batch = lay_out({n: np.asarray(a) for n, a in inputs.items()})
    nc = _bacc.Bacc("TRN2", target_bir_lowering=False, num_devices=1, dynamic_dma_scratch_size=2048)
    dram, sent = {}, {}
    for name, a in arrays.items():
        sent[f"in_{name}_dram"] = a
        dram[name] = nc.dram_tensor(f"in_{name}_dram", a.shape, mybir.dt.from_np(a.dtype), kind="ExternalInput").ap()
    out = nc.dram_tensor("out_0_dram", (batch * S // P, P, D), F32, kind="ExternalOutput").ap()
    build(nc, dram["x"], dram["cond"], dram["mask_k"], dram["mask_q"], dram["vec"], dram["modw"],
          [dram[f"w{n}"] for n in range(len(PHASES))], out, PHASE_LIMIT)
    r = _run(nc, [sent], core_ids=[0])
    return r.results[0]["out_0_dram"].reshape(batch, S, D)


PHASE_LIMIT = len(PHASES)
```

```python
from contextlib import ExitStack

import numpy as np

import concourse.bass as bass
from concourse import mybir

ALU = mybir.AluOpType
ACT = mybir.ActivationFunctionType
AX = mybir.AxisListType
F32 = mybir.dt.float32
F32R = mybir.dt.float32r
U8 = mybir.dt.uint8

P = 128
S = 64
D = 256
DC = D // P
BLK = 512
SEQ = BLK // S
TILES = BLK // P
PAIRS = 8
HID = 8
HW = 17
MASKED = 4e9
CREDIT = 2

PHASES = [(kind, layer) for layer in range(4) for kind in ("attn", "mlp")]
UP = {("attn", 0): DC * 768, ("mlp", 0): DC * 1024, ("attn", 1): DC * 1280, ("mlp", 1): DC * 2048,
      ("attn", 2): DC * 3072, ("mlp", 2): DC * 1024, ("attn", 3): DC * 768, ("mlp", 3): DC * 1024}
DOWN = {(kind, layer): (8 if kind == "mlp" or layer == 2 else 2) * D for kind, layer in PHASES}
EPS = (1e-6, float(np.finfo(np.float32).eps), 1e-5, 1e-6)
SCORE_SCALE = (1 / 16, 1 / 4, 1 / 8, 1 / 4)

MOD = {("attn", 0): (0, 2, None), ("mlp", 0): (4, 6, None), ("attn", 1): (10, 8, None), ("mlp", 1): (14, 12, None),
       ("attn", 2): (18, 16, 20), ("mlp", 2): (24, 22, 26), ("attn", 3): (30, 28, 32), ("mlp", 3): (36, 34, 38)}
MODS = 40
MOD_COLS = {"film": DC * 1024, "t1": DC * 512, "mod2": DC * 1536, "mod3": DC * 1536, "t2": DC * 1024}

VEC = {}
for _name, _n in (("mod_b", MODS), ("t1_b", 4), ("norm", 8),
                  ("q0", 2), ("k0", 2), ("v0", 2), ("o0", 2), ("u0", 8), ("d0", 2),
                  ("q1", 2), ("k1", 2), ("qs1", 2), ("ks1", 2), ("v1", 2), ("o1", 2), ("u1", 16), ("d1", 2),
                  ("o2", 2), ("u2", 8), ("d2", 2),
                  ("q3", 2), ("k3", 2), ("v3", 2), ("o3", 2), ("u3", 8), ("d3", 2),
                  ("even", 1), ("odd", 1), ("cos", S), ("sin", S), ("ident", P)):
    VEC[_name] = (sum(n for _, n in VEC.values()), _n)
VECS = sum(n for _, n in VEC.values())


def order_of(kind, layer):
    prev = lambda s, k=0: (s, k, -1)
    own = lambda s, k=0: (s, k, 0)
    nxt = lambda s, k=0: (s, k, 1)
    if kind == "mlp":
        return [own("up", 2), own("down", 0), nxt("stats"), prev("back"), own("share"), own("up", 3), nxt("norm"),
                own("down", 1), own("up", 4), own("down", 2), own("up", 5), own("down", 3), nxt("turn"),
                own("up", 6), own("down", 4), nxt("split"), own("up", 7), own("down", 5), own("down", 6),
                nxt("up", 0), own("down", 7), nxt("up", 1)]
    if layer == 0:
        return [prev("probs_t"), nxt("stats"), own("scores"), prev("pv"), nxt("norm"), own("v", 0), own("v", 1),
                nxt("turn"), nxt("split"), prev("proj"), nxt("q", 0), nxt("q", 1), prev("back"), nxt("k", 0),
                nxt("k", 1), own("divide"), own("share")]
    if layer in (1, 3):
        return [own("scores", 0), prev("probs_t", 7), own("q", 1), own("q_out", 1), prev("pv", 6), own("share"),
                own("scores", 1), own("probs_t", 0), own("v", 0), prev("pv", 7), own("v_out", 0), own("v", 1),
                own("v_out", 1), nxt("stats"),
                own("scores", 2), nxt("norm"), own("probs_t", 1), prev("merge"), own("k", 1), own("k_out", 1), own("pv", 0),
                own("scores", 3), own("probs_t", 2), prev("proj"), own("pv", 1), nxt("turn"),
                own("scores", 4), own("probs_t", 3), prev("back"), nxt("split"), own("pv", 2),
                own("scores", 5), own("probs_t", 4), own("pv", 3), nxt("k", 0), nxt("k_out", 0),
                own("scores", 6), own("probs_t", 5), own("pv", 4), nxt("q", 0), nxt("q_out", 0),
                own("scores", 7), own("pv", 5), own("probs_t", 6)]
    body = [prev("divide", 7), own("scores", 0), own("q", 1), prev("pv", 6), own("k", 1), prev("pv2", 6),
            prev("probs_t", 7), own("v", 0), prev("proj", 5), prev("pv", 7), own("v", 1), prev("pv2", 7),
            own("divide", 0), own("scores", 1), own("v", 2), own("v", 3), prev("proj", 6), own("probs_t", 0),
            own("q", 2), own("share"), own("k", 2), own("v", 4), prev("proj", 7), own("v", 5), own("v", 6),
            prev("back"), own("v", 7)]
    for p in range(2, PAIRS):
        body += [own("divide", p - 1), own("scores", p)]
        if p < 7:
            body += [own("q", p + 1), own("pv", p - 2), own("k", p + 1)] + ([nxt("turn")] if p == 6 else [])
            body += [own("pv2", p - 2), own("probs_t", p - 1)]
        else:
            body += [own("pv", 5), nxt("q", 0), own("pv2", 5), nxt("k", 0), own("probs_t", 6)]
        body += {3: [nxt("stats")], 4: [nxt("norm")], 6: [nxt("split")]}.get(p, [])
        body += [own("proj", p - 3)] if p >= 3 else []
    return body


TABLE_AFTER = [("pv", 0), ("v", 0), ("v", 1), ("proj", 0), ("back", 0), ("share", 0)]
TABLE_BANKS = (3, 5)
UP_AFTER = {0: [("pv", 0), ("proj", 0)], 1: [("merge", 0), ("proj", 0)],
            2: [("probs_t", 7), ("proj", 7)], 3: [("merge", 0), ("proj", 0)]}
W0_PARTS = 4


def fills_of(kind, layer):
    body = order_of(kind, layer)
    fills = [("turn", 0), ("turn", 1)]
    for off in (1, 0, -1):
        for s, k, o in body:
            if o == off and s in ("q", "k", "v"):
                fills += [(s, k)] * (2 if layer == 1 and s != "v" else 1)
    return fills


def counts_of(kind, layer):
    c = dict(stats_raw=1, stats=1, mean_sq=1 if layer < 2 else 0, rstd_in=1, rstd=1, normed=1, eps_added=1, modded=2,
             h_hi=2, h=2, out_rows=2, x_done=1)
    if kind == "mlp":
        n = HID * (2 if layer == 1 else 1)
        c.update({"a_full0": 1, "a_full1": 1, "a_free0": 1, "a_free1": 1,
                  "s_full0": n // 2, "s_full1": n // 2, "s_free0": n // 2, "s_free1": n // 2,
                  "hid32": HID, "hid_hi": HID, "hid": HID, "down": HID, "gate_in": HID if layer == 1 else 0,
                  "back": 1})
        return c
    fills = {0: 8, 1: 12, 2: 26, 3: 8}[layer] // 2
    c.update({"a_full0": fills, "a_full1": fills, "a_free0": fills, "a_free1": fills})
    n = 1 if layer == 0 else PAIRS
    c.update({"s_full0": n - n // 2, "s_full1": n // 2, "s_free0": n - n // 2, "s_free1": n // 2,
              "row_max": n, "shifted": n * (2 if layer == 0 else 1), "probs": n, "t_full": n, "probs_t": n})
    if layer in (0, 2):
        c.update(row_sum=n, row_inv=n, divided=n)
    if layer == 0:
        c.update(q=2, k=2, v=2, w_full=3, w_free=1, att_hi=2, att=2)
    if layer in (1, 3):
        c.update(o_full=n, o_inv=n // 2, o_free=n // 2, q=2 * 2, k=4 * 2, v=2 * 2, q32=2, w_full=3, w_free=1, att_hi=2, att=2)
    if layer == 1:
        c.update(rot_a=4, rot_b=4, k32=2)
    if layer == 3:
        c.update(masked=n)
    if layer == 2:
        c.update(q=n, k=n, v=8, pv1=n, o_full=n, o_free=n, att_hi=n, att=n, proj=n, w_full=1)
    return c


NAMES = sorted({name for ph in PHASES for name in counts_of(*ph)})


def build(nc, x_in, cond_in, mask_k_in, mask_q_in, vec_in, modw_in, weights_in, out, phases=len(PHASES)):
    batch = cond_in.shape[2]
    blocks = batch // SEQ
    tiles = blocks * TILES

    before = {name: [0] for name in NAMES}
    for ph in range(len(PHASES)):
        for name in NAMES:
            before[name].append(before[name][-1] + blocks * counts_of(*PHASES[ph]).get(name, 0))

    def n_at(name, ph, b, k):
        return b * counts_of(*PHASES[ph]).get(name, 0) + (CREDIT + before[name][ph] + k)

    with ExitStack() as ctx:
        sem = {name: ctx.enter_context(nc.semaphore(name)) for name in NAMES}
        x_first_loaded = ctx.enter_context(nc.semaphore("x_first_loaded"))
        x_rest_loaded = ctx.enter_context(nc.semaphore("x_rest_loaded"))
        vec_loaded = ctx.enter_context(nc.semaphore("vec_loaded"))
        modw_loaded = {name: ctx.enter_context(nc.semaphore(f"modw_{name}_loaded")) for name in MOD_COLS}
        w0_staged = ctx.enter_context(nc.semaphore("w0_staged"))
        w0_hi_done = ctx.enter_context(nc.semaphore("w0_hi_done"))
        w0_ready = ctx.enter_context(nc.semaphore("w0_ready"))
        t1_ready = ctx.enter_context(nc.semaphore("t1_ready"))
        mask_loaded = ctx.enter_context(nc.semaphore("mask_loaded"))
        w_staged = ctx.enter_context(nc.semaphore("w_staged"))
        w_hi_done = ctx.enter_context(nc.semaphore("w_hi_done"))
        w_ready = ctx.enter_context(nc.semaphore("w_ready"))
        consts_ready = ctx.enter_context(nc.semaphore("consts_ready"))
        prepared = ctx.enter_context(nc.semaphore("prepared"))
        mask_made = ctx.enter_context(nc.semaphore("mask_made"))
        mod_mm = ctx.enter_context(nc.semaphore("mod_mm"))
        mod_act = ctx.enter_context(nc.semaphore("mod_act"))
        mod_dve = ctx.enter_context(nc.semaphore("mod_dve"))
        waits_passed = ctx.enter_context(nc.semaphore("waits_passed"))
        stored = ctx.enter_context(nc.semaphore("stored"))

        at = [nc.sbuf_base + (-nc.sbuf_base) % 32]

        def place(name, shape, dt, where=None):
            size = int(np.prod(shape[1:])) * (1 if dt == U8 else 4)
            size += -size % 32
            offset = at[0] if where is None else where
            if where is None:
                at[0] += size
            assert offset + size <= nc.sbuf_usable_end, (name, offset, size)
            return nc.alloc_sbuf_tensor_at(name, shape, dt, offset=offset)

        xres = place("xres", [P, tiles, D], F32)
        mod = place("mod", [P, MODS, batch], F32)
        vec = place("vec", [P, VECS], F32)
        xn = place("xn", [P, TILES, D], F32)
        hm = place("hm", [P, DC, BLK], F32)
        h_hi = place("h_hi", [P, DC, BLK], F32R)
        h_lo = place("h_lo", [P, DC, BLK], F32R)
        y = place("y", [P, DC, BLK], F32)
        stage = place("stage", [P, 1024], F32)
        st = place("st", [P, TILES, 6], F32)
        mv = place("mv", [P, TILES, 2], F32)
        ms = place("ms", [P, TILES], F32)
        rstd = place("rstd", [P, TILES], F32)
        eps_t = place("eps_t", [P, 4, TILES], F32)
        half_t = place("half_t", [P, TILES], F32)
        mx = place("mx", [P, 2, SEQ], F32)
        sm = place("sm", [P, 2, SEQ], F32)
        ri = place("ri", [P, 2, SEQ], F32)
        mask_q8 = place("mask_q8", [P, batch], U8)
        pb = place("pb", [P, 2, BLK], F32)
        pt = place("pt", [P, 2, BLK], F32)
        at_hi = place("at_hi", [P, 2, BLK], F32R)
        at_lo = place("at_lo", [P, 2, BLK], F32R)
        rot_at = at[0]
        q2_sb = place("q2_sb", [P, 2, BLK], F32)
        k2_sb = place("k2_sb", [P, 2, BLK], F32)
        hid32 = place("hid32", [P, 2, BLK], F32)
        hid_hi = place("hid_hi", [P, 2, BLK], F32R)
        hid_lo = place("hid_lo", [P, 2, BLK], F32R)
        gate_at = at[0]
        gate_in = place("gate_in", [P, BLK], F32)
        wa, wb = at[0], at[0] + 65536
        assert wb + 49152 <= nc.sbuf_usable_end
        w_hi, w_lo = [], []
        for ph, (kind, layer) in enumerate(PHASES):
            cols = UP[kind, layer] + DOWN[kind, layer]
            base = wa if kind == "attn" else wb
            w_hi.append(place(f"w_hi{ph}", [P, cols], F32R, base))
            w_lo.append(place(f"w_lo{ph}", [P, cols], F32R, base + 4 * cols))
        free = wa + 8 * 3072
        qb = place("qb", [P, DC, SEQ, 2, S], F32, free)
        kk = place("kk", [P, DC, BLK], F32, free + 8192)
        kx = place("kx", [P, DC, SEQ, 4, S], F32, free + 8192)
        vb = place("vb", [P, TILES, 2, 2 * PAIRS * HW], F32, free + 8192 + 16384)
        on = place("on", [P, SEQ, P], F32, free + 8192 + 16384 + 8704)
        rot = place("rot", [P, 2, 2, BLK], F32, rot_at)
        assert free + 8192 + 16384 + 8704 + 4096 <= wb
        free3 = wa + 8 * 2048
        mask_k8 = place("mask_k8", [P, blocks * BLK], U8, free3)
        q0_sb = place("q0_sb", [P, DC, BLK], F32, free)
        v0_sb = place("v0_sb", [P, TILES, D], F32, free + 12288)
        mask_bad = place("mask_bad", [P, blocks * BLK], U8, free3 + 4096)
        v2_sb = place("v2_sb", [P, TILES, 1024], F32, wb + 32768)
        modw = {name: place(f"modw_{name}", [P, MOD_COLS[name]], F32, where) for name, where in (
            ("film", wb), ("t1", wb + 32768), ("t2", wb + 36864), ("mod2", wa + 40960), ("mod3", wa + 53248))}
        w0_staged_sb = place("w0_staged_sb", [P, UP["attn", 0] + DOWN["attn", 0]], F32, free)
        cond = place("cond", [P, DC, batch], F32, gate_at)
        cond_silu = place("cond_silu", [P, DC, batch], F32, gate_at + 512)
        t1_g = place("t1_g", [P, DC, batch], F32, gate_at + 1024)
        t1_h = place("t1_h", [P, DC, batch], F32, gate_at + 1536)

        psum = ctx.enter_context(nc.psum_tensor("psum", [P, 8, 512], F32))
        A_BANK, S_BANK, T_BANK, O_BANK, W_BANK = 0, 2, 4, 5, 6
        acc_a = [psum[:, A_BANK + i, :] for i in range(2)]
        scores = [psum[:, S_BANK + i, :] for i in range(2)]
        probs_tp = psum[:, T_BANK, :]
        heads = psum[:, O_BANK, :]
        wide = psum[:, W_BANK:W_BANK + 2, :]
        mlp_back = psum[:, T_BANK:T_BANK + 2, :]

        def col(name, k=0, n=1):
            o = VEC[name][0] + k
            return vec[:, o:o + n]

        ident = col("ident", 0, P)

        def by_seq(ap):
            return ap.rearrange("p (b k) -> p b k", k=S)

        def over_tokens(per_seq):
            return per_seq.unsqueeze(2).to_broadcast([per_seq.shape[0], per_seq.shape[1], S])

        def modulation(slot, c, b):
            return over_tokens(mod[:, slot + c, bass.ds(b * SEQ, SEQ)])

        def run_phases(stage_of, engine, before_loop=None):
            orders = [order_of(*key) for key in PHASES[:phases]]

            def stages(ph, offset):
                return [(s, k) for s, k, off in orders[ph] if off == offset]

            for s, k in stages(0, 1):
                stage_of(0, s, k, 0)
            for ph in range(phases):
                ending = stages(ph - 1, -1) if ph else []
                for s, k, off in ([(None, 0, -1)] if PHASES[ph][0] == "mlp" else []) + orders[ph]:
                    if off == -1:
                        for e_s, e_k in ending:
                            stage_of(ph - 1, e_s, e_k, blocks - 1)
                            if PHASES[ph][0] == "mlp" and (e_s, e_k) in UP_AFTER[PHASES[ph - 1][1]]:
                                stage_of(ph, "up", UP_AFTER[PHASES[ph - 1][1]].index((e_s, e_k)), 0)
                        ending = []
                    else:
                        stage_of(ph, s, k, off)
                if before_loop:
                    before_loop(ph)
                with engine.Fori(1, blocks - 1) as i:
                    for s, k, off in orders[ph]:
                        stage_of(ph, s, k, i + off)
                coming = stages(ph + 1, 1) if ph + 1 < phases else []
                for s, k, off in orders[ph]:
                    if PHASES[ph][0] == "mlp" and (s, k) == ("down", 6):
                        for c_s, c_k in coming:
                            stage_of(ph + 1, c_s, c_k, 0)
                        coming = []
                    if off != 1:
                        stage_of(ph, s, k, blocks - 1 + off)
                        if ph == 0 and (s, k) in TABLE_AFTER:
                            stage_of(0, "table", TABLE_AFTER.index((s, k)), blocks - 1)
                    elif coming and coming[0][0] == s and s in ("stats", "norm", "turn", "split"):
                        stage_of(ph + 1, s, k, 0)
                        coming = coming[1:]
            for s, k in stages(phases - 1, -1):
                stage_of(phases - 1, s, k, blocks - 1)

        def shares_before(ph):
            return sum((UP[PHASES[q]] + DOWN[PHASES[q]]) // part_of(q, blocks) for q in range(1, ph))

        def pool_helps(ph):
            return PHASES[ph] in (("attn", 1), ("attn", 3))

        def is_first(b):
            return isinstance(b, int) and b == 0

        def a_slot(ph, s, k):
            return fills_of(*PHASES[ph]).index((s, k))

        def rotation(ph, s, k):
            fills = [f for f in fills_of(*PHASES[ph])[2::2] if f[0] in ("q", "k")]
            return fills.index((s, k)) + 1

        def wait_alone(eng, semaphore, value):
            eng.wait_ge(semaphore, value)
            eng.sem_inc(waits_passed, 1)

        def last_h_reader(ph, b):
            kind, layer = PHASES[ph - 1 if ph and is_first(b) else ph]
            name = "a_full1" if kind == "attn" else "s_full0" if layer == 1 else "s_full1"
            return sem[name], n_at(name, ph, b, 0)

        block = ctx.enter_context(nc.Block())

        @block.sync
        def _(sp):
            for name in NAMES:
                sp.sem_inc(sem[name], CREDIT)
            x_src = x_in.rearrange("t p d -> p t d")
            modw_src, o = {}, 0
            for name, cols in MOD_COLS.items():
                modw_src[name] = modw_in[:, o:o + cols]
                o += cols
            sp.dma_start(cond[:, :, :], cond_in).then_inc(vec_loaded, 16)
            sp.dma_start(vec[:, :], vec_in).then_inc(vec_loaded, 16)
            sp.dma_start(xres[:, 0:TILES, :], x_src[:, 0:TILES, :]).then_inc(x_first_loaded, 16)
            sp.dma_start(modw["film"][:, :], modw_src["film"]).then_inc(modw_loaded["film"], 16)
            sp.dma_start(w0_staged_sb[:, :], weights_in[0]).then_inc(w0_staged, 16)
            sp.dma_start(xres[:, TILES:tiles, :], x_src[:, TILES:tiles, :]).then_inc(x_rest_loaded, 16)
            if phases > 1:
                sp.dma_start(stage[:, 0:part_of(1, blocks)], weights_in[1][:, 0:part_of(1, blocks)]).then_inc(w_staged, 16)
            for name in ("t1", "mod2", "t2", "mod3"):
                sp.dma_start(modw[name][:, :], modw_src[name]).then_inc(modw_loaded[name], 16)
            sp.dma_start(mask_q8[:, :], mask_q_in).then_inc(mask_loaded, 16)
            for ph in range(1, phases):
                cols = (UP[PHASES[ph]] + DOWN[PHASES[ph]]) // blocks
                parts = -(-cols // 1024)
                part = cols // parts
                if ph == 6:
                    sp.wait_ge(sem["x_done"], n_at("x_done", 5, 0, 1))
                    sp.dma_start(mask_k8[:, :], mask_k_in.partition_broadcast(P)).then_inc(mask_loaded, 16)
                for i in range(blocks * parts):
                    n = shares_before(ph) + i
                    if n == 0:
                        continue
                    sp.wait_ge(w_ready, n)
                    sp.dma_start(stage[:, 0:part], weights_in[ph][:, i * part:(i + 1) * part]).then_inc(w_staged, 16)
            last = phases - 1
            with sp.Fori(0, blocks) as b:
                sp.wait_ge(sem["x_done"], n_at("x_done", last, b, 1 + 1))
                sp.dma_start(out.rearrange("t p d -> p t d")[:, bass.ds(b * TILES, TILES), :],
                             xres[:, bass.ds(b * TILES, TILES), :]).then_inc(stored, 16)
            sp.wait_ge(stored, 16 * blocks)

        @block.tensor
        def _(pe):
            def mod_product(name, rhs, bank, first, n_out):
                for m in range(n_out):
                    dst = psum[:, bank, m * batch:(m + 1) * batch]
                    for kc in range(DC):
                        w = kc * (MOD_COLS[name] // DC) + (first + m) * P
                        ins = nc.tensor.matmul(dst, modw[name][:, w:w + P], rhs[:, kc, :], start=kc == 0, stop=kc == DC - 1)
                ins.then_inc(mod_mm, 1)

            pe.wait_ge(vec_loaded, 32)
            pe.wait_ge(modw_loaded["film"], 16)
            mod_product("film", cond, 0, 0, 8)

            def table_part(n):
                if n == 0:
                    pe.wait_ge(modw_loaded["t1"], 16)
                    mod_product("t1", cond, TABLE_BANKS[0], 0, 4)
                elif n == 1:
                    pe.wait_ge(mod_act, 1)
                    pe.wait_ge(modw_loaded["mod2"], 16)
                    mod_product("mod2", cond_silu, TABLE_BANKS[1], 0, 8)
                elif n == 2:
                    pe.wait_ge(t1_ready, 2)
                    pe.wait_ge(modw_loaded["t2"], 16)
                    mod_product("t2", t1_h, TABLE_BANKS[0], 0, 8)
                elif n == 3:
                    pe.wait_ge(mod_dve, 2)
                    mod_product("mod2", cond_silu, TABLE_BANKS[1], 8, 4)
                elif n == 4:
                    pe.wait_ge(mod_dve, 3)
                    pe.wait_ge(modw_loaded["mod3"], 16)
                    mod_product("mod3", cond_silu, TABLE_BANKS[0], 0, 8)
                else:
                    pe.wait_ge(mod_dve, 4)
                    mod_product("mod3", cond_silu, TABLE_BANKS[1], 8, 4)

            def weight(ph, part, kc, o, n=P):
                key = PHASES[ph]
                if part == "up":
                    c = kc * (UP[key] // DC) + o
                else:
                    c = UP[key] + kc * D + o
                return w_hi[ph][:, c:c + n], w_lo[ph][:, c:c + n]

            def project(dst, pairs, start=True, stop=True):
                for j, ((s_hi, s_lo), (m_hi, m_lo)) in enumerate(pairs):
                    nc.tensor.matmul(dst, s_lo, m_hi, start=start and j == 0, stop=False)
                    nc.tensor.matmul(dst, s_hi, m_lo, start=False, stop=False)
                    ins = nc.tensor.matmul(dst, s_hi, m_hi, start=False, stop=stop and j == len(pairs) - 1)
                return ins

            def fill_a(ph, b, n):
                pe.wait_ge(sem[f"a_free{n % 2}"], n_at(f"a_free{n % 2}", ph, b, n // 2))
                return acc_a[n % 2]

            def up_rows(ph, b, n, o):
                ins = project(fill_a(ph, b, n), [(weight(ph, "up", kc, o), (h_hi[:, kc, :], h_lo[:, kc, :]))
                                                 for kc in range(DC)])
                ins.then_inc(sem[f"a_full{n % 2}"], 1)

            def stage_of(ph, s, k, b):
                kind, layer = PHASES[ph]
                c, j, slot = k // 4, k % 4, k % 2
                if s == "table":
                    table_part(k)
                if is_first(b) and (s, k) in (("q", 0), ("k", 0), ("up", 0)):
                    if ph == 0:
                        pe.wait_ge(w0_ready, W0_PARTS)
                    else:
                        pe.wait_ge(w_ready, shares_before(ph + 1))
                    if ph == 1:
                        pe.wait_ge(mod_dve, 6)
                if is_first(b) and (s, k) in (("probs_t", 0), ("down", 0)):
                    pe.wait_ge(sem["x_done"], n_at("x_done", ph, 0, 1))
                if s == "turn":
                    pe.wait_ge(sem["normed"], n_at("normed", ph, b, 1))
                    for m in range(DC):
                        dst = fill_a(ph, b, m)
                        for t in range(TILES):
                            ins = nc.tensor.transpose(dst[:, t * P:(t + 1) * P], xn[:, t, m * P:(m + 1) * P], ident)
                        ins.then_inc(sem[f"a_full{m}"], 1)
                elif s in ("q", "k") and kind == "attn":
                    n = a_slot(ph, s, k)
                    pe.wait_ge(sem["h"], n_at("h", ph, b, 2))
                    width = 1024 if layer == 2 else D
                    up_rows(ph, b, n, (0 if s == "q" else width) + k * P)
                    if layer == 1:
                        up_rows(ph, b, n + 1, (768 if s == "q" else 1024) + k * P)
                elif s == "v":
                    n = a_slot(ph, s, k)
                    pe.wait_ge(sem["h"], n_at("h", ph, b, 2))
                    dst = fill_a(ph, b, n)
                    if layer == 2:
                        t = k // 2
                        cols = slice(t * P, (t + 1) * P)
                        ins = project(dst, [((h_hi[:, kc, cols], h_lo[:, kc, cols]),
                                             weight(ph, "up", kc, 2048 + 512 * (k % 2), 512)) for kc in range(DC)])
                    else:
                        for u in range(2):
                            cols = slice((2 * k + u) * P, (2 * k + u + 1) * P)
                            ins = project(dst[:, u * D:(u + 1) * D],
                                          [((h_hi[:, kc, cols], h_lo[:, kc, cols]), weight(ph, "up", kc, 2 * D, D))
                                           for kc in range(DC)])
                    ins.then_inc(sem[f"a_full{n % 2}"], 1)
                elif s == "scores":
                    pe.wait_ge(sem[f"s_free{slot}"], n_at(f"s_free{slot}", ph, b, k // 2))
                    dst = scores[slot]
                    if layer == 0:
                        pe.wait_ge(sem["q"], n_at("q", ph, b, 2))
                        pe.wait_ge(sem["k"], n_at("k", ph, b, 2))
                        for g in range(SEQ):
                            tok = slice(g * S, (g + 1) * S)
                            half = slice((g % 2) * S, (g % 2) * S + S)
                            for kc in range(DC):
                                ins = nc.tensor.matmul(dst[half, (g // 2) * S:(g // 2 + 1) * S], q0_sb[:, kc, tok],
                                                       kk[:, kc, tok], start=kc == 0, stop=kc == DC - 1)
                    elif layer == 2:
                        pe.wait_ge(sem["q"], n_at("q", ph, b, k + 1))
                        wait_alone(pe, sem["k"], n_at("k", ph, b, k + 1))
                        for g in range(SEQ):
                            tok = slice(g * S, (g + 1) * S)
                            for hd in range(2):
                                rows = slice(hd * S, (hd + 1) * S)
                                ins = nc.tensor.matmul(dst[rows, tok], q2_sb[rows, slot, tok], k2_sb[rows, slot, tok],
                                                       start=True, stop=True)
                    else:
                        pe.wait_ge(sem["q"], n_at("q", ph, b, 2 * (c + 1)))
                        pe.wait_ge(sem["k"], n_at("k", ph, b, 4 * (c + 1)))
                        for g in range(2):
                            ins = nc.tensor.matmul(dst.rearrange("p (r g k) -> p r g k", g=2, k=S)[:, :, g, :],
                                                   qb[:, c, 2 * j + g, :, :].rearrange("p h q -> p (h q)"),
                                                   kx[:, c, 2 * j + g, :, :], start=True, stop=True)
                    ins.then_inc(sem[f"s_full{slot}"], 1)
                elif s == "probs_t":
                    ready = "divided" if layer in (0, 2) else "probs"
                    pe.wait_ge(sem[ready], n_at(ready, ph, b, k + 1))
                    pe.wait_ge(sem["probs_t"], n_at("probs_t", ph, b, k))
                    for t in range(TILES):
                        ins = nc.tensor.transpose(probs_tp[:, t * P:(t + 1) * P], pb[:, slot, t * P:(t + 1) * P], ident)
                    ins.then_inc(sem["t_full"], 1)
                elif s == "pv" and layer == 0:
                    pe.wait_ge(sem["probs_t"], n_at("probs_t", ph, b, 1))
                    pe.wait_ge(sem["v"], n_at("v", ph, b, 2))
                    pe.wait_ge(sem["x_done"], n_at("x_done", ph, b, 1))
                    for m in range(DC):
                        for t in range(TILES):
                            ins = nc.tensor.matmul(wide[:, m, t * P:(t + 1) * P], v0_sb[:, t, m * P:(m + 1) * P],
                                                   pt[:, 0, t * P:(t + 1) * P], start=True, stop=True)
                    ins.then_inc(sem["w_full"], 1)
                elif s == "pv" and layer in (1, 3):
                    pe.wait_ge(sem["probs_t"], n_at("probs_t", ph, b, k + 1))
                    pe.wait_ge(sem["v"], n_at("v", ph, b, 4))
                    if slot == 0:
                        pe.wait_ge(sem["o_free"], n_at("o_free", ph, b, k // 2))
                    dst = heads[:, slot * 2 * 4 * HW:(slot + 1) * 2 * 4 * HW].rearrange("p (g r w) -> p g r w", g=2, w=HW)
                    for r in range(4):
                        for hd in range(2):
                            head = 8 * c + 2 * r + hd
                            ins = nc.tensor.matmul(dst[hd * S:(hd + 1) * S, :, r, :],
                                                   pt[:, slot, r * P + hd * S:r * P + (hd + 1) * S],
                                                   vb[:, j, :, head * HW:(head + 1) * HW], start=True, stop=True)
                    ins.then_inc(sem["o_full"], 1)
                elif s in ("pv", "pv2"):
                    g = 0 if s == "pv" else 1
                    if g == 0:
                        pe.wait_ge(sem["probs_t"], n_at("probs_t", ph, b, k + 1))
                        pe.wait_ge(sem["v"], n_at("v", ph, b, 8))
                        wait_alone(pe, sem["o_free"], n_at("o_free", ph, b, k))
                    else:
                        wait_alone(pe, sem["pv1"], n_at("pv1", ph, b, k + 1))
                    rows = slice(g * S, (g + 1) * S)
                    for t in range(TILES):
                        for hd in range(2):
                            o = t * P + g * S
                            ins = nc.tensor.matmul(heads[hd * S:(hd + 1) * S, o:o + S],
                                                   v2_sb[rows, t, (2 * k + hd) * S:(2 * k + hd + 1) * S],
                                                   pt[rows, slot, t * P + hd * S:t * P + (hd + 1) * S],
                                                   start=True, stop=True)
                    ins.then_inc(sem["pv1" if g == 0 else "o_full"], 1)
                elif s == "merge":
                    pe.wait_ge(sem["o_free"], n_at("o_free", ph, b, PAIRS // 2))
                    pe.wait_ge(sem["x_done"], n_at("x_done", ph, b, 1))
                    for g in range(SEQ):
                        ins = nc.tensor.transpose(wide[:, g // 4, (g % 4) * P:(g % 4 + 1) * P], on[:, g, :], ident)
                    ins.then_inc(sem["w_full"], 1)
                elif s == "proj" and layer == 2:
                    pe.wait_ge(sem["att"], n_at("att", ph, b, k + 1))
                    if k == 0:
                        pe.wait_ge(sem["x_done"], n_at("x_done", ph, b, 1))
                    for m in range(DC):
                        ins = project(wide[:, m, :], [(weight(ph, "down", k, m * P), (at_hi[:, slot, :], at_lo[:, slot, :]))],
                                      start=k == 0, stop=k == PAIRS - 1)
                    ins.then_inc(sem["proj"], 1)
                elif s == "proj":
                    pe.wait_ge(sem["att"], n_at("att", ph, b, 2))
                    pe.wait_ge(sem["w_free"], n_at("w_free", ph, b, 1))
                    for m in range(DC):
                        ins = project(wide[:, m, :], [(weight(ph, "down", kc, m * P), (at_hi[:, kc, :], at_lo[:, kc, :]))
                                                      for kc in range(DC)])
                    ins.then_inc(sem["w_full"], 1)
                elif s == "up":
                    pe.wait_ge(sem["h"], n_at("h", ph, b, 2))
                    if layer == 1:
                        todo = [(1, k, HID + k), (0, k, k)]
                    else:
                        todo = [(slot, k // 2, k)]
                    for sl, nth, m in todo:
                        pe.wait_ge(sem[f"s_free{sl}"], n_at(f"s_free{sl}", ph, b, nth))
                        ins = project(scores[sl], [(weight(ph, "up", kc, m * P), (h_hi[:, kc, :], h_lo[:, kc, :]))
                                                   for kc in range(DC)])
                        ins.then_inc(sem[f"s_full{sl}"], 1)
                elif s == "down":
                    pe.wait_ge(sem["hid"], n_at("hid", ph, b, k + 1))
                    if k == 0:
                        pe.wait_ge(sem["out_rows"], n_at("out_rows", ph, b, 0))
                    for m in range(DC):
                        ins = project(wide[:, m, :], [(weight(ph, "down", k, m * P), (hid_hi[:, slot, :], hid_lo[:, slot, :]))],
                                      start=k == 0, stop=k == HID - 1)
                    ins.then_inc(sem["down"], 1)
                elif s == "back":
                    pe.wait_ge(sem["out_rows"], n_at("out_rows", ph, b, 2))
                    if kind == "mlp":
                        pe.wait_ge(sem["x_done"], n_at("x_done", ph, b, 1))
                    dst = mlp_back if kind == "mlp" else wide
                    for t in range(TILES):
                        for m in range(DC):
                            o = (t % 2) * D + m * P
                            ins = nc.tensor.transpose(dst[:, t // 2, o:o + P], y[:, m, t * P:(t + 1) * P], ident)
                    ins.then_inc(sem["back" if kind == "mlp" else "w_full"], 1)

            pe.wait_ge(sem["x_done"], n_at("x_done", 0, 0, 1))
            run_phases(stage_of, pe)

        @block.scalar
        def _(act):
            act.wait_ge(w0_staged, 16)
            part = w0_staged_sb.shape[1] // W0_PARTS
            for n in range(W0_PARTS):
                where = slice(n * part, (n + 1) * part)
                nc.scalar.activation(w_hi[0][:, where], w0_staged_sb[:, where], ACT.Copy).then_inc(w0_hi_done, 1)

            def table_part(n):
                if n == 0:
                    nc.scalar.activation(cond_silu[:, :, :], cond[:, :, :], ACT.Silu).then_inc(mod_act, 1)
                    act.wait_ge(mod_mm, 2)
                    for kc in range(DC):
                        nc.scalar.activation(t1_g[:, kc, :], psum[:, TABLE_BANKS[0], (2 + kc) * batch:(3 + kc) * batch],
                                             ACT.Silu, bias=col("t1_b", 2 + kc)).then_inc(mod_act, 1)

            def stage_of(ph, s, k, b):
                kind, layer = PHASES[ph]
                c, j, slot = k // 4, k % 4, k % 2
                if s == "table":
                    table_part(k)
                if is_first(b) and (s, k) == ("k_out", 0):
                    act.wait_ge(prepared, 4 if layer == 1 else 8)
                if s == "split":
                    for m in range(DC):
                        act.wait_ge(sem["modded"], n_at("modded", ph, b, m + 1))
                        act.wait_ge(*last_h_reader(ph, b))
                        nc.scalar.activation(h_hi[:, m, :], hm[:, m, :], ACT.Copy).then_inc(sem["h_hi"], 1)
                elif (s in ("q", "k", "v") if layer in (0, 2) else s in ("q_out", "k_out", "v_out")) and kind == "attn":
                    n = a_slot(ph, s[0], k)
                    full, fre = sem[f"a_full{n % 2}"], sem[f"a_free{n % 2}"]
                    src = acc_a[n % 2]
                    if layer == 0:
                        act.wait_ge(full, n_at(f"a_full{n % 2}", ph, b, n // 2 + 1))
                        if s == "v":
                            act.wait_ge(sem["w_full"], n_at("w_full", ph, b, -2))
                            nc.scalar.activation(v0_sb[:, 2 * k:2 * k + 2, :], src.rearrange("p (t d) -> p t d", d=D),
                                                 ACT.Copy).then_inc(fre, 1)
                        else:
                            act.wait_ge(sem["s_full0"], n_at("s_full0", ph, b, 0))
                            dst = q0_sb if s == "q" else kk
                            nc.scalar.activation(dst[:, k, :], src, ACT.Identity, bias=col(f"{s}0", k)).then_inc(fre, 1)
                        act.wait_ge(fre, n_at(f"a_free{n % 2}", ph, b, n // 2 + 1))
                        act.sem_inc(sem[s], 1)
                    elif layer == 2:
                        act.wait_ge(full, n_at(f"a_full{n % 2}", ph, b, n // 2 + 1))
                        if s == "v":
                            act.wait_ge(sem["o_full"], n_at("o_full", ph, b, 0))
                            nc.scalar.activation(v2_sb[:, k // 2, 512 * (k % 2):512 * (k % 2) + 512], src,
                                                 ACT.Copy).then_inc(fre, 1)
                            act.wait_ge(fre, n_at(f"a_free{n % 2}", ph, b, n // 2 + 1))
                            act.sem_inc(sem["v"], 1)
                        else:
                            act.wait_ge(sem[f"s_full{slot}"], n_at(f"s_full{slot}", ph, b, k // 2))
                            dst = q2_sb if s == "q" else k2_sb
                            nc.scalar.activation(dst[:, slot, :], src, ACT.Copy).then_inc(sem[s], 1)
                            act.wait_ge(sem[s], n_at(s, ph, b, k + 1))
                            act.sem_inc(fre, 1)
                    elif s == "v_out":
                        act.wait_ge(full, n_at(f"a_full{n % 2}", ph, b, n // 2 + 1))
                        act.wait_ge(sem["o_full"], n_at("o_full", ph, b, 0))
                        for g in range(2):
                            rows = slice(g * S, (g + 1) * S)
                            dst = vb[rows, 2 * k:2 * k + 2, g, :].rearrange("p t (r w) -> p t r w", w=HW)[:, :, :, 0:HW - 1]
                            nc.scalar.activation(dst, src[rows, :].rearrange("p (t r w) -> p t r w", t=2, w=HW - 1),
                                                 ACT.Copy).then_inc(sem["v"], 1)
                        act.wait_ge(sem["v"], n_at("v", ph, b, 2 * (k + 1)))
                        act.sem_inc(fre, 1)
                    elif s == "k_out" and layer == 3:
                        act.wait_ge(full, n_at(f"a_full{n % 2}", ph, b, n // 2 + 1))
                        act.wait_ge(sem["s_full1"], n_at("s_full1", ph, b, -2 if k == 0 else 0))
                        for r in range(4):
                            rows = slice(32 * r, 32 * r + 32)
                            nc.scalar.activation(kx[rows, k, :, r, :], by_seq(src[rows, :]), ACT.Identity,
                                                 bias=col("k3", k)[rows, :]).then_inc(sem["k"], 1)
                        act.wait_ge(sem["k"], n_at("k", ph, b, 4 * (k + 1)))
                        act.sem_inc(fre, 1)
                    elif s == "k_out":
                        act.wait_ge(sem["k32"], n_at("k32", ph, b, k + 1))
                        act.wait_ge(sem["s_full1"], n_at("s_full1", ph, b, -2 if k == 0 else 0))
                        for r in range(4):
                            rows = slice(32 * r, 32 * r + 32)
                            nc.scalar.activation(kx[rows, k, :, r, :], by_seq(rot[rows, 1, 0, :]),
                                                 ACT.Copy).then_inc(sem["k"], 1)
                    elif s == "q_out":
                        act.wait_ge(sem["q32"], n_at("q32", ph, b, k + 1))
                        act.wait_ge(sem["s_full1"], n_at("s_full1", ph, b, -2 if k == 0 else 0))
                        for hd, parity in enumerate(("even", "odd")):
                            nc.scalar.activation(qb[:, k, :, hd, :], by_seq(rot[:, 0, 0, :]), ACT.Copy,
                                                 scale=col(parity)).then_inc(sem["q"], 1)
                elif s == "scores":
                    if layer == 0:
                        act.wait_ge(sem["shifted"], n_at("shifted", ph, b, 2))
                        for g in range(2):
                            rows = slice(g * S, (g + 1) * S)
                            ap = pb[rows, 0, :].rearrange("p (t g k) -> p t g k", g=2, k=S)[:, :, g, :]
                            ins = nc.scalar.activation(ap, ap, ACT.Exp, scale=SCORE_SCALE[0])
                            if g == 1:
                                ins.then_inc(sem["probs"], 1)
                    else:
                        act.wait_ge(sem["shifted"], n_at("shifted", ph, b, k + 1))
                        nc.scalar.activation(pb[:, slot, :], pb[:, slot, :], ACT.Exp,
                                             scale=SCORE_SCALE[layer]).then_inc(sem["probs"], 1)
                elif s == "probs_t":
                    act.wait_ge(sem["t_full"], n_at("t_full", ph, b, k + 1))
                    if layer == 0:
                        act.wait_ge(sem["w_full"], n_at("w_full", ph, b, -2))
                    else:
                        act.wait_ge(sem["o_full"], n_at("o_full", ph, b, k - 1))
                    nc.scalar.activation(pt[:, slot, :], probs_tp, ACT.Copy).then_inc(sem["probs_t"], 1)
                elif s in ("pv", "merge") and (layer == 0 or s == "merge"):
                    act.wait_ge(sem["w_full"], n_at("w_full", ph, b, 1))
                    for m in range(DC):
                        if layer == 0:
                            src = wide[:, m, :]
                            dst = at_hi[:, m, :]
                        else:
                            src = wide.rearrange("p w (g h q) -> p (w g) h q", h=2, q=S)[:, :, m, :]
                            dst = by_seq(at_hi[:, m, :])
                        nc.scalar.activation(dst, src, ACT.Identity, bias=col(f"v{layer}", m)).then_inc(sem["att_hi"], 1)
                elif s == "pv2":
                    act.wait_ge(sem["o_full"], n_at("o_full", ph, b, k + 1))
                    act.wait_ge(sem["proj"], n_at("proj", ph, b, k - 1))
                    nc.scalar.activation(at_hi[:, slot, :], heads, ACT.Copy).then_inc(sem["att_hi"], 1)
                elif s == "proj" and layer in (0, 1):
                    act.wait_ge(sem["w_full"], n_at("w_full", ph, b, 2))
                    for m in range(DC):
                        nc.scalar.activation(y[:, m, :], wide[:, m, :], ACT.Identity,
                                             bias=col(f"o{layer}", m)).then_inc(sem["out_rows"], 1)
                elif s == "up":
                    if layer == 1:
                        act.wait_ge(sem["s_full1"], n_at("s_full1", ph, b, k + 1))
                        act.wait_ge(sem["hid32"], n_at("hid32", ph, b, k))
                        nc.scalar.activation(gate_in[:, :], scores[1], ACT.Silu, bias=col("u1", HID + k)).then_inc(sem["gate_in"], 1)
                        act.wait_ge(sem["gate_in"], n_at("gate_in", ph, b, k + 1))
                        act.sem_inc(sem["s_free1"], 1)
                    else:
                        func = ACT.Gelu_apprx_tanh if layer == 3 else ACT.Gelu
                        act.wait_ge(sem[f"s_full{slot}"], n_at(f"s_full{slot}", ph, b, k // 2 + 1))
                        act.wait_ge(sem["hid"], n_at("hid", ph, b, k - 1))
                        nc.scalar.activation(hid32[:, slot, :], scores[slot], func, bias=col(f"u{layer}", k)).then_inc(sem["hid32"], 1)
                    act.wait_ge(sem["hid32"], n_at("hid32", ph, b, k + 1))
                    if layer != 1:
                        act.sem_inc(sem[f"s_free{slot}"], 1)
                    act.wait_ge(sem["down"], n_at("down", ph, b, k - 1))
                    nc.scalar.activation(hid_hi[:, slot, :], hid32[:, slot, :], ACT.Copy).then_inc(sem["hid_hi"], 1)
                elif s == "down" and k == HID - 1 and layer in (0, 1):
                    act.wait_ge(sem["down"], n_at("down", ph, b, HID))
                    act.wait_ge(sem["back"], n_at("back", ph, b, 0))
                    for m in range(DC):
                        nc.scalar.activation(y[:, m, :], wide[:, m, :], ACT.Identity,
                                             bias=col(f"d{layer}", m)).then_inc(sem["out_rows"], 1)

            run_phases(stage_of, act)

        @block.vector
        def _(dve):
            dve.wait_ge(vec_loaded, 32)

            def mod_bias(slots, first, n):
                nc.vector.tensor_tensor(mod[:, first:first + n, :],
                                        slots.rearrange("p (n b) -> p n b", b=batch)[:, 0:n, :],
                                        col("mod_b", first, n).unsqueeze(2).to_broadcast([P, n, batch]),
                                        ALU.add).then_inc(mod_dve, 1)

            def mod_scale(slot, norm):
                for c in range(DC):
                    ap = mod[:, slot + c, :]
                    if norm is None:
                        nc.vector.tensor_scalar(ap, ap, 1.0, None, ALU.add).then_inc(consts_ready, 1)
                    else:
                        nc.vector.tensor_scalar(ap, ap, 1.0, col("norm", norm + c), ALU.add, ALU.mult).then_inc(consts_ready, 1)

            for layer in range(4):
                nc.vector.memset(eps_t[:, layer, :], EPS[layer]).then_inc(consts_ready, 1)
            nc.vector.memset(half_t[:, :], -0.5).then_inc(consts_ready, 1)
            nc.vector.memset(pb[:, :, :], 0.0).then_inc(consts_ready, 1)
            full = 8 * batch
            dve.wait_ge(consts_ready, 6)

            def layer0_table():
                dve.wait_ge(mod_mm, 1)
                mod_bias(psum[:, 0, 0:full], 0, 8)
                dve.wait_ge(mod_dve, 1)
                for ph, norm in ((0, 0), (1, 2)):
                    mod_scale(MOD[PHASES[ph]][0], norm)
                dve.wait_ge(consts_ready, 6 + 4)
                dve.sem_inc(sem["x_done"], 1)

            def first_weights_lo():
                part = w0_staged_sb.shape[1] // W0_PARTS
                for n in range(W0_PARTS):
                    where = slice(n * part, (n + 1) * part)
                    dve.wait_ge(w0_hi_done, n + 1)
                    nc.vector.tensor_tensor(w_lo[0][:, where], w0_staged_sb[:, where], w_hi[0][:, where].bitcast(F32),
                                            ALU.subtract).then_inc(w0_ready, 1)

            def table_part(n):
                first, second = (psum[:, bank, 0:full] for bank in TABLE_BANKS)
                if n == 0:
                    dve.wait_ge(mod_act, 3)
                    for kc in range(DC):
                        nc.vector.scalar_tensor_tensor(t1_h[:, kc, :], first[:, kc * batch:(kc + 1) * batch], col("t1_b", kc),
                                                       t1_g[:, kc, :], ALU.add, ALU.mult).then_inc(t1_ready, 1)
                    return
                dve.wait_ge(mod_mm, n + 2)
                if n == 1:
                    mod_bias(second, 16, 8)
                elif n == 2:
                    mod_bias(first, 8, 8)
                elif n == 3:
                    mod_bias(second, 24, 4)
                elif n == 4:
                    mod_bias(first, 28, 8)
                else:
                    mod_bias(second, 36, 4)
                    dve.wait_ge(mod_dve, 6)
                    for ph, norm in ((2, 4), (3, 6), (4, None), (5, None), (6, None), (7, None)):
                        mod_scale(MOD[PHASES[ph]][0], norm)
                    dve.wait_ge(consts_ready, 10 + 12)

            def stage_of(ph, s, k, b):
                kind, layer = PHASES[ph]
                c, j, slot = k // 4, k % 4, k % 2
                scale, shift, gate = MOD[PHASES[ph]]
                if s == "table":
                    table_part(k)
                if ph == 0 and is_first(b) and s == "turn":
                    layer0_table()
                if ph == 0 and is_first(b) and s == "split":
                    first_weights_lo()
                if s == "share" and PHASES[ph] == ("mlp", 2) and isinstance(b, int) and b == blocks - 1:
                    dve.wait_ge(mask_loaded, 32)
                    nc.vector.tensor_tensor(by_seq(mask_bad[:, :]), over_tokens(mask_q8[:, :]), by_seq(mask_k8[:, :]),
                                            ALU.is_gt).then_inc(mask_made, 1)
                    dve.wait_ge(mask_made, 1)
                elif s == "stats":
                    if ph == 0 and isinstance(b, int):
                        dve.wait_ge(x_first_loaded if b == 0 else x_rest_loaded, 16)
                    if ph and isinstance(b, int) and b < 2:
                        dve.wait_ge(sem["x_done"], n_at("x_done", ph - 1, b + 1, 1))
                    for t in range(TILES):
                        ins = nc.vector.bn_stats(st[:, t, :], xres[:, b * TILES + t, :])
                    ins.then_inc(sem["stats_raw"], 1)
                    wait_alone(dve, sem["stats_raw"], n_at("stats_raw", ph, b, 1))
                    for t in range(TILES):
                        ins = nc.vector.bn_aggr(mv[:, t, :], st[:, t, :])
                    ins.then_inc(sem["stats"], 1)
                    dve.wait_ge(sem["stats"], n_at("stats", ph, b, 1))
                    if layer < 2:
                        nc.vector.tensor_tensor(ms[:, :], mv[:, :, 0], mv[:, :, 0], ALU.mult).then_inc(sem["mean_sq"], 1)
                        dve.wait_ge(sem["mean_sq"], n_at("mean_sq", ph, b, 1))
                        nc.vector.tensor_tensor(ms[:, :], ms[:, :], mv[:, :, 1], ALU.add).then_inc(sem["rstd_in"], 1)
                    else:
                        nc.vector.tensor_copy(ms[:, :], mv[:, :, 1]).then_inc(sem["rstd_in"], 1)
                elif s == "norm":
                    dve.wait_ge(sem["rstd"], n_at("rstd", ph, b, 1))
                    for t in range(TILES):
                        if layer < 2:
                            ins = nc.vector.tensor_scalar(xn[:, t, :], xres[:, b * TILES + t, :], rstd[:, t:t + 1], None, ALU.mult)
                        else:
                            ins = nc.vector.tensor_scalar(xn[:, t, :], xres[:, b * TILES + t, :], mv[:, t, 0:1],
                                                          rstd[:, t:t + 1], ALU.subtract, ALU.mult)
                    ins.then_inc(sem["normed"], 1)
                elif s == "turn":
                    dve.wait_ge(sem["h"], n_at("h", ph, b, 0))
                    for m in range(DC):
                        n = n_at(f"a_full{m}", ph, b, 1)
                        dve.wait_ge(sem[f"a_full{m}"], n)
                        nc.vector.tensor_tensor(by_seq(hm[:, m, :]), by_seq(acc_a[m]), modulation(scale, m, b),
                                                ALU.mult).then_inc(sem[f"a_free{m}"], 1)
                    for m in range(DC if not pool_helps(ph) else 0):
                        dve.wait_ge(sem[f"a_free{m}"], n_at(f"a_free{m}", ph, b, 1))
                        nc.vector.tensor_tensor(by_seq(hm[:, m, :]), by_seq(hm[:, m, :]), modulation(shift, m, b),
                                                ALU.add).then_inc(sem["modded"], 1)
                elif s == "split":
                    for m in range(DC):
                        dve.wait_ge(sem["h_hi"], n_at("h_hi", ph, b, m + 1))
                        nc.vector.tensor_tensor(h_lo[:, m, :], hm[:, m, :], h_hi[:, m, :].bitcast(F32),
                                                ALU.subtract).then_inc(sem["h"], 1)
                elif s in ("q", "k") and layer == 1:
                    n = a_slot(ph, s, k)
                    which = 0 if s == "q" else 1
                    nth = rotation(ph, s, k)
                    if s == "q":
                        dve.wait_ge(sem["q"], n_at("q", ph, b, 2 * k))
                    else:
                        dve.wait_ge(sem["k"], n_at("k", ph, b, 4 * k))
                    for u, (bias, tab, cnt) in enumerate(((f"{s}1", "cos", "rot_a"), (f"{s}s1", "sin", "rot_b"))):
                        dve.wait_ge(sem[f"a_full{u}"], n_at(f"a_full{u}", ph, b, n // 2 + 1))
                        nc.vector.scalar_tensor_tensor(by_seq(rot[:, which, u, :]), by_seq(acc_a[u]), col(bias, k),
                                                       col(tab, 0, S).unsqueeze(1).to_broadcast([P, SEQ, S]),
                                                       ALU.add, ALU.mult).then_inc(sem[cnt], 1)
                        dve.wait_ge(sem[cnt], n_at(cnt, ph, b, nth))
                        dve.sem_inc(sem[f"a_free{u}"], 1)
                elif s == "q" and layer == 3:
                    n = a_slot(ph, s, k)
                    dve.wait_ge(sem[f"a_full{n % 2}"], n_at(f"a_full{n % 2}", ph, b, n // 2 + 1))
                    dve.wait_ge(sem["q"], n_at("q", ph, b, 2 * k))
                    nc.vector.scalar_tensor_tensor(rot[:, 0, 0, :], acc_a[n % 2], col("q3", k), mask_k8[:, bass.ds(b * BLK, BLK)],
                                                   ALU.add, ALU.mult).then_inc(sem["q32"], 1)
                    dve.wait_ge(sem["q32"], n_at("q32", ph, b, k + 1))
                    dve.sem_inc(sem[f"a_free{n % 2}"], 1)
                elif s == "scores" and layer == 0:
                    dve.wait_ge(sem["s_full0"], n_at("s_full0", ph, b, 1))
                    sc = scores[0][:, 0:TILES * S].rearrange("p (t k) -> p t k", k=S)
                    nc.vector.tensor_reduce(mx[:, 0, 0:TILES], sc, AX.X, ALU.max).then_inc(sem["row_max"], 1)
                    dve.wait_ge(sem["row_max"], n_at("row_max", ph, b, 1))
                    dve.wait_ge(sem["t_full"], n_at("t_full", ph, b, 0))
                    for g in range(2):
                        rows = slice(g * S, (g + 1) * S)
                        ap = pb[rows, 0, :].rearrange("p (t g k) -> p t g k", g=2, k=S)[:, :, g, :]
                        nc.vector.tensor_tensor(ap, sc[rows], over_tokens(mx[rows, 0, 0:TILES]),
                                                ALU.subtract).then_inc(sem["shifted"], 1)
                    dve.wait_ge(sem["shifted"], n_at("shifted", ph, b, 2))
                    dve.sem_inc(sem["s_free0"], 1)
                elif s == "scores":
                    sc = by_seq(scores[slot])
                    dst = by_seq(pb[:, slot, :])
                    dve.wait_ge(sem[f"s_full{slot}"], n_at(f"s_full{slot}", ph, b, k // 2 + 1))
                    dve.wait_ge(sem["t_full"], n_at("t_full", ph, b, k - 1))
                    if layer == 3:
                        nc.vector.scalar_tensor_tensor(pb[:, slot, :].rearrange("p (r w) -> p r w", w=P),
                                                       mask_bad[:, bass.ds(b * BLK + j * P, P)].unsqueeze(1).to_broadcast([P, 4, P]),
                                                       -MASKED, scores[slot].rearrange("p (r w) -> p r w", w=P),
                                                       ALU.mult, ALU.add).then_inc(sem["masked"], 1)
                        dve.wait_ge(sem["masked"], n_at("masked", ph, b, k + 1))
                        dve.sem_inc(sem[f"s_free{slot}"], 1)
                        sc = dst
                    nc.vector.tensor_reduce(mx[:, slot, :], sc, AX.X, ALU.max).then_inc(sem["row_max"], 1)
                    dve.wait_ge(sem["row_max"], n_at("row_max", ph, b, k + 1))
                    nc.vector.tensor_tensor(dst, sc, over_tokens(mx[:, slot, :]), ALU.subtract).then_inc(sem["shifted"], 1)
                    if layer != 3:
                        dve.wait_ge(sem["shifted"], n_at("shifted", ph, b, k + 1))
                        dve.sem_inc(sem[f"s_free{slot}"], 1)
                elif s == "divide":
                    dve.wait_ge(sem["probs"], n_at("probs", ph, b, k + 1))
                    if layer == 0:
                        src, n = pb[:, 0, :].rearrange("p (t k) -> p t k", k=P), TILES
                    else:
                        src, n = by_seq(pb[:, slot, :]), SEQ
                    nc.vector.tensor_reduce(sm[:, slot, 0:n], src, AX.X, ALU.add).then_inc(sem["row_sum"], 1)
                    dve.wait_ge(sem["row_sum"], n_at("row_sum", ph, b, k + 1))
                    dve.wait_ge(sem["divided"], n_at("divided", ph, b, k - 1))
                    nc.vector.reciprocal(ri[:, slot, 0:n], sm[:, slot, 0:n]).then_inc(sem["row_inv"], 1)
                elif s == "pv" and layer in (1, 3):
                    if slot == 0:
                        return
                    dve.wait_ge(sem["o_full"], n_at("o_full", ph, b, k + 1))
                    o4 = heads[:, 0:2 * SEQ * HW].rearrange("p (g r w) -> p g r w", g=4, w=HW)
                    inv = ri[:, :, :].rearrange("p a (b r) -> p (a b) r", r=4)
                    nc.vector.reciprocal(inv, o4[:, :, :, HW - 1]).then_inc(sem["o_inv"], 1)
                    dve.wait_ge(sem["o_inv"], n_at("o_inv", ph, b, k // 2 + 1))
                    if k == 1:
                        dve.wait_ge(sem["w_full"], n_at("w_full", ph, b, -2))
                    u = (k // 2) % 2
                    nc.vector.tensor_tensor(on[:, 4 * u:4 * u + 4, c * S:(c + 1) * S].rearrange("p g (r w) -> p g r w", r=4),
                                            o4[:, :, :, 0:HW - 1], inv.unsqueeze(3).to_broadcast([P, 4, 4, 16]),
                                            ALU.mult).then_inc(sem["o_free"], 1)
                elif (s == "pv" and layer == 0) or s == "merge":
                    for m in range(DC):
                        if layer == 0:
                            src, hi, lo = wide[:, m, :], at_hi[:, m, :], at_lo[:, m, :]
                        else:
                            src = wide.rearrange("p w (g h q) -> p (w g) h q", h=2, q=S)[:, :, m, :]
                            hi, lo = by_seq(at_hi[:, m, :]), by_seq(at_lo[:, m, :])
                        dve.wait_ge(sem["att_hi"], n_at("att_hi", ph, b, m + 1 if layer == 0 else 2))
                        nc.vector.scalar_tensor_tensor(lo, src, col(f"v{layer}", m), hi.bitcast(F32), ALU.add,
                                                       ALU.subtract).then_inc(sem["att"], 1)
                    dve.wait_ge(sem["att"], n_at("att", ph, b, 2))
                    dve.sem_inc(sem["w_free"], 1)
                elif s == "pv2":
                    dve.wait_ge(sem["att_hi"], n_at("att_hi", ph, b, k + 1))
                    nc.vector.tensor_tensor(at_lo[:, slot, :], heads, at_hi[:, slot, :].bitcast(F32),
                                            ALU.subtract).then_inc(sem["att"], 1)
                    dve.wait_ge(sem["att"], n_at("att", ph, b, k + 1))
                    dve.sem_inc(sem["o_free"], 1)
                elif s == "up":
                    if layer == 1:
                        dve.wait_ge(sem["s_full0"], n_at("s_full0", ph, b, k + 1))
                        dve.wait_ge(sem["gate_in"], n_at("gate_in", ph, b, k + 1))
                        dve.wait_ge(sem["hid"], n_at("hid", ph, b, k - 1))
                        nc.vector.scalar_tensor_tensor(hid32[:, slot, :], scores[0], col("u1", k), gate_in[:, :],
                                                       ALU.add, ALU.mult).then_inc(sem["hid32"], 1)
                        dve.wait_ge(sem["hid32"], n_at("hid32", ph, b, k + 1))
                        dve.sem_inc(sem["s_free0"], 1)
                    dve.wait_ge(sem["hid_hi"], n_at("hid_hi", ph, b, k + 1))
                    nc.vector.tensor_tensor(hid_lo[:, slot, :], hid32[:, slot, :], hid_hi[:, slot, :].bitcast(F32),
                                            ALU.subtract).then_inc(sem["hid"], 1)
                elif gate is not None and ((s == "proj" and (layer == 3 or k == PAIRS - 1)) or (s == "down" and k == HID - 1)):
                    if kind == "mlp":
                        dve.wait_ge(sem["down"], n_at("down", ph, b, HID))
                        dve.wait_ge(sem["back"], n_at("back", ph, b, 0))
                    elif layer == 3:
                        dve.wait_ge(sem["w_full"], n_at("w_full", ph, b, 2))
                    else:
                        dve.wait_ge(sem["proj"], n_at("proj", ph, b, PAIRS))
                    bias = ("d" if kind == "mlp" else "o") + str(layer)
                    for m in range(DC):
                        nc.vector.scalar_tensor_tensor(by_seq(y[:, m, :]), by_seq(wide[:, m, :]), col(bias, m),
                                                       modulation(gate, m, b), ALU.add, ALU.mult).then_inc(sem["out_rows"], 1)
                elif s == "back":
                    if kind == "mlp":
                        dve.wait_ge(sem["back"], n_at("back", ph, b, 1))
                        src = mlp_back
                    else:
                        last = 3 if layer != 2 else 1
                        dve.wait_ge(sem["w_full"], n_at("w_full", ph, b, last))
                        src = wide
                    xs = xres[:, bass.ds(b * TILES, TILES), :].rearrange("p (w t) d -> p w (t d)", w=2)
                    nc.vector.tensor_tensor(xs, xs, src, ALU.add).then_inc(sem["x_done"], 1)

            run_phases(stage_of, dve, lambda ph: dve.wait_ge(sem["x_done"], n_at("x_done", ph, 0, 1)))

        @block.gpsimd
        def _(pool):
            def split_next(ph, b):
                if ph + 1 >= phases:
                    return
                nxt = ph + 1
                cols = (UP[PHASES[nxt]] + DOWN[PHASES[nxt]]) // blocks
                parts = -(-cols // 1024)
                part = cols // parts
                done = shares_before(nxt)
                for u in range(parts):
                    n = b * parts + (done + u + 1)
                    where = bass.ds(b * cols + u * part, part)
                    pool.wait_ge(w_staged, n * 16)
                    nc.gpsimd.tensor_copy(w_hi[nxt][:, where], stage[:, 0:part]).then_inc(w_hi_done, 1)
                    pool.wait_ge(w_hi_done, n)
                    nc.gpsimd.tensor_tensor(w_lo[nxt][:, where], stage[:, 0:part], w_hi[nxt][:, where].bitcast(F32),
                                            ALU.subtract).then_inc(w_ready, 1)

            def prepare_attention():
                nc.gpsimd.memset(kx[:, :, :, :, :], 0.0).then_inc(prepared, 1)
                nc.gpsimd.memset(vb[:, :, :, :], 0.0).then_inc(prepared, 1)
                prepares[0] += 2
                pool.wait_ge(prepared, prepares[0])
                for g in range(2):
                    rows = slice(g * S, (g + 1) * S)
                    nc.gpsimd.memset(vb[rows, :, g, :].rearrange("p t (r w) -> p t r w", w=HW)[:, :, :, HW - 1],
                                     1.0).then_inc(prepared, 1)
                    prepares[0] += 1
                    pool.wait_ge(prepared, prepares[0])

            prepares = [0]
            def stage_of(ph, s, k, b):
                kind, layer = PHASES[ph]
                slot = k % 2
                if s == "stats":
                    pool.wait_ge(sem["rstd_in"], n_at("rstd_in", ph, b, 1))
                    nc.gpsimd.tensor_tensor(ms[:, :], ms[:, :], eps_t[:, layer, :], ALU.add).then_inc(sem["eps_added"], 1)
                    pool.wait_ge(sem["eps_added"], n_at("eps_added", ph, b, 1))
                    nc.gpsimd.tensor_tensor(rstd[:, :], ms[:, :], half_t[:, :], ALU.pow).then_inc(sem["rstd"], 1)
                elif s == "turn" and pool_helps(ph):
                    for m in range(DC):
                        pool.wait_ge(sem[f"a_free{m}"], n_at(f"a_free{m}", ph, b, 1))
                        nc.gpsimd.tensor_tensor(by_seq(hm[:, m, :]), by_seq(hm[:, m, :]), modulation(MOD[PHASES[ph]][1], m, b),
                                                ALU.add).then_inc(sem["modded"], 1)
                elif s in ("q", "k") and layer == 1:
                    pool.wait_ge(sem["rot_b"], n_at("rot_b", ph, b, rotation(ph, s, k)))
                    if s == "q":
                        nc.gpsimd.tensor_tensor(rot[:, 0, 0, :], rot[:, 0, 0, :], rot[:, 0, 1, :], ALU.add).then_inc(sem["q32"], 1)
                    else:
                        nc.gpsimd.tensor_tensor(rot[:, 1, 0, :], rot[:, 1, 0, :], rot[:, 1, 1, :], ALU.add).then_inc(sem["k32"], 1)
                elif s == "divide":
                    pool.wait_ge(sem["row_inv"], n_at("row_inv", ph, b, k + 1))
                    if layer == 0:
                        ap = pb[:, 0, :].rearrange("p (t k) -> p t k", k=P)
                        inv = ri[:, 0, 0:TILES].unsqueeze(2).to_broadcast([P, TILES, P])
                    else:
                        ap, inv = by_seq(pb[:, slot, :]), over_tokens(ri[:, slot, :])
                    nc.gpsimd.tensor_tensor(ap, ap, inv, ALU.mult).then_inc(sem["divided"], 1)
                elif s == "share":
                    if is_first(b):
                        pool.wait_ge(sem["x_done"], n_at("x_done", ph, 0, 1))
                        if PHASES[ph + 1:ph + 2] in ([("attn", 1)], [("attn", 3)]):
                            prepare_attention()
                    split_next(ph, b)

            run_phases(stage_of, pool)


def part_of(ph, blocks):
    cols = (UP[PHASES[ph]] + DOWN[PHASES[ph]]) // blocks
    return cols // -(-cols // 1024)


def rows_first(w):
    return w.reshape(-1, P, w.shape[1]).transpose(1, 0, 2)


def lay_out(i):
    x = np.ascontiguousarray(i["x"])
    batch = x.shape[0]
    cond = np.ascontiguousarray(rows_first(np.ascontiguousarray(i["cond_1024"].T)))
    mask = np.ascontiguousarray(i["mask_BxS_bk1"])
    swap = np.arange(D).reshape(-1, 2)[:, ::-1].reshape(-1)
    heads = np.arange(D).reshape(8, 2, 16).transpose(1, 0, 2).reshape(-1)

    def weights(up, down):
        return np.concatenate([rows_first(up).reshape(P, -1), rows_first(down).reshape(P, -1)], axis=1)

    q1, k1, v1 = (i["L1_cond_w_qkv"][:, n * D:(n + 1) * D] for n in range(3))
    w = [
        weights(np.concatenate([i["L0_cond_q_w"], i["L0_cond_k_w"], i["L0_cond_v_w"]], 1), i["L0_cond_proj_w"]),
        weights(i["L0_cond_mlp_w1"], i["L0_cond_mlp_w2"]),
        weights(np.concatenate([q1, k1, v1, q1[:, swap], k1[:, swap]], 1), i["L1_cond_w_ao"][heads]),
        weights(i["L1_cond_w_fc"], i["L1_cond_w_fo"]),
        weights(i["L2_cond_W_qkv"], i["L2_cond_W_out"]),
        weights(i["L2_cond_W1"], i["L2_cond_W2"]),
        weights(i["L3_cond_qkv_w"].T, i["L3_cond_proj_w"].T[heads]),
        weights(i["L3_cond_fc1_w"].T, i["L3_cond_fc2_w"].T),
    ]
    modw = np.concatenate([rows_first(m).reshape(P, -1) for m in (
        np.concatenate([i["L0_cond_film1_w"], i["L0_cond_film2_w"]], 1), i["L1_cond_w_t1"], i["L2_cond_W_mod"],
        i["L3_cond_ada_w"].T, i["L1_cond_w_t2"])], axis=1)

    def cols(v):
        return v.reshape(-1, P).T

    bq1, bk1, bv1 = (i["L1_cond_b_qkv"][n * D:(n + 1) * D] for n in range(3))
    bq3, bk3, bv3 = (i["L3_cond_qkv_b"][n * D:(n + 1) * D] for n in range(3))
    pair = (np.arange(P) % 16) // 2
    freq = (1.0 / np.float32(10000.0) ** (np.arange(0, 16, 2, dtype=np.float32) / np.float32(16))).astype(np.float32)
    angle = np.arange(S, dtype=np.float32)[None, :] * freq[pair][:, None]
    sign = np.where(np.arange(P) % 2 == 0, -1, 1).astype(np.float32)[:, None]
    parity = ((np.arange(P) // 16) % 2).astype(np.float32)[:, None]
    vec = {
        "mod_b": np.concatenate([cols(i[n]) for n in ("L0_cond_film1_b", "L0_cond_film2_b", "L1_cond_b_t2",
                                                      "L2_cond_b_mod", "L3_cond_ada_b")], 1),
        "t1_b": cols(i["L1_cond_b_t1"]),
        "norm": np.concatenate([cols(i[n]) for n in ("L0_cond_norm1_w", "L0_cond_norm2_w", "L1_cond_g1", "L1_cond_g2")], 1),
        "q0": cols(i["L0_cond_q_b"]), "k0": cols(i["L0_cond_k_b"]), "v0": cols(i["L0_cond_v_b"]),
        "o0": cols(i["L0_cond_proj_b"]), "u0": cols(i["L0_cond_mlp_b1"]), "d0": cols(i["L0_cond_mlp_b2"]),
        "q1": cols(bq1), "k1": cols(bk1), "qs1": cols(bq1[swap]), "ks1": cols(bk1[swap]), "v1": cols(bv1[heads]),
        "o1": cols(i["L1_cond_b_ao"]), "u1": cols(i["L1_cond_b_fc"]), "d1": cols(i["L1_cond_b_fo"]),
        "o2": cols(i["L2_cond_b_out"]), "u2": cols(i["L2_cond_b1"]), "d2": cols(i["L2_cond_b2"]),
        "q3": cols(bq3), "k3": cols(bk3), "v3": cols(bv3[heads]), "o3": cols(i["L3_cond_proj_b"]),
        "u3": cols(i["L3_cond_fc1_b"]), "d3": cols(i["L3_cond_fc2_b"]),
        "even": 1 - parity, "odd": parity, "cos": np.cos(angle), "sin": np.sin(angle) * sign,
        "ident": np.eye(P, dtype=np.float32),
    }
    assert all(vec[n].shape == (P, VEC[n][1]) for n in VEC), {n: vec[n].shape for n in VEC}
    vecs = np.concatenate([vec[n].astype(np.float32, copy=False) for n in VEC], 1)
    arrays = {
        "x": x.reshape(-1, P, D), "cond": cond, "mask_k": mask.reshape(-1),
        "mask_q": np.concatenate([mask.T, mask.T], 0), "vec": vecs, "modw": modw,
    }
    arrays.update({f"w{n}": a for n, a in enumerate(w)})
    return {n: np.ascontiguousarray(a) for n, a in arrays.items()}, batch


def kernel(**inputs):
    import concourse.bacc as _bacc
    from concourse.bass_utils import run_bass_kernel_spmd as _run

    arrays, batch = lay_out({n: np.asarray(a) for n, a in inputs.items()})
    nc = _bacc.Bacc("TRN2", target_bir_lowering=False, num_devices=1, dynamic_dma_scratch_size=2048)
    dram, sent = {}, {}
    for name, a in arrays.items():
        sent[f"in_{name}_dram"] = a
        dram[name] = nc.dram_tensor(f"in_{name}_dram", a.shape, mybir.dt.from_np(a.dtype), kind="ExternalInput").ap()
    out = nc.dram_tensor("out_0_dram", (batch * S // P, P, D), F32, kind="ExternalOutput").ap()
    build(nc, dram["x"], dram["cond"], dram["mask_k"], dram["mask_q"], dram["vec"], dram["modw"],
          [dram[f"w{n}"] for n in range(len(PHASES))], out, PHASE_LIMIT)
    r = _run(nc, [sent], core_ids=[0])
    return r.results[0]["out_0_dram"].reshape(batch, S, D)


PHASE_LIMIT = len(PHASES)
```
